# Optimizing a Trainium2 kernel written in Bass

```python
import numpy as np
import jax
import jax.numpy as jnp

def _softmax(x, axis=-1):
    return jax.nn.softmax(x, axis=axis)

def _gelu(x):
    return jax.nn.gelu(x, approximate=True)

def _silu(x):
    return jax.nn.silu(x)

def _sigmoid(x):
    return jax.nn.sigmoid(x)

def _layernorm(x, axis=-1, eps=1e-05):
    m = jnp.mean(x, axis=axis, keepdims=True)
    v = jnp.var(x, axis=axis, keepdims=True)
    return (x - m) / jnp.sqrt(v + eps)

def _scatter_add(tgt, idx, src, axis=0):
    return tgt.at[idx].add(src)

def _segment_sum(src, seg, n):
    return jax.ops.segment_sum(src, seg, n)
kernel_name = 'mk_decoder_postln_d2_seqx_r8_9d4218'

def setup_inputs(seed: int=0):
    np.random.seed(seed)
    _w = jnp.asarray

    def _rec_inputs():
        import jax
        import jax.numpy as jnp
        _rk = jax.random.key(seed)
        x = -0.0003929 + 0.9999 * jax.random.normal(jax.random.fold_in(_rk, 1), (16, 56, 128), jnp.float32)
        _lenS = 56 - jax.random.randint(jax.random.fold_in(_rk, 7), (16,), 0, max(1, 56 // 4) + 1, jnp.int32)
        _lenS2 = 1500 - jax.random.randint(jax.random.fold_in(_rk, 8), (16,), 0, max(1, 1500 // 4) + 1, jnp.int32)
        _ctx_512P = jax.random.normal(jax.random.fold_in(_rk, 11), (16, 16, 64), jnp.float32)
        _ctx_512c = jax.random.dirichlet(jax.random.fold_in(_rk, 511), 0.3 * jnp.ones((16,), jnp.float32), (16, 1500))
        _ctx_512t = jnp.einsum('bsk,bkd->bsd', _ctx_512c, _ctx_512P)
        _ctx_512t = _ctx_512t * jax.lax.rsqrt(jnp.mean(jnp.square(_ctx_512t)) + 1e-12) * 0.953939
        ctx_512 = 4.13588e-05 + 0.999923 * (_ctx_512t + 0.3 * jax.random.normal(jax.random.fold_in(_rk, 611), (16, 1500, 64), jnp.float32))
        return (x, ctx_512)
    x, ctx_512 = _rec_inputs()

    def _L0_attn_setup():
        import jax, jax.numpy as jnp
        import numpy as np
        SCALE_BASE = 512.0
        GAMMA = 0.96875

        def xpos(x, downscale=False):
            B, L, d = x.shape
            half = d // 2
            scale_vec = (jnp.arange(0, d, 2, dtype=jnp.float32) + 0.4 * d) / (1.4 * d)
            pos = jnp.arange(L, dtype=jnp.float32)
            scale = scale_vec[None, :] ** (pos[:, None] / SCALE_BASE)
            if downscale:
                scale = 1.0 / scale
            inv_freq = 1.0 / 10000.0 ** (jnp.arange(half, dtype=jnp.float32) / half)
            sinusoid = pos[:, None] * inv_freq[None, :]
            sin_s = jnp.repeat(jnp.sin(sinusoid) * scale, 2, axis=-1)
            cos_s = jnp.repeat(jnp.cos(sinusoid) * scale, 2, axis=-1)
            x1, x2 = (x[..., ::2], x[..., 1::2])
            rot = jnp.stack((-x2, x1), axis=-1).reshape(x.shape)
            return x * cos_s + rot * sin_s

        def decay_mask(L, gamma):
            n = jnp.arange(L)[:, None]
            m = jnp.arange(L)[None, :]
            diff = n - m
            expo = jnp.where(diff >= 0, diff, 0).astype(jnp.float32)
            return jnp.where(diff >= 0, gamma ** expo, 0.0)
        key = jax.random.key(seed)
        kx, kq, kk, kv = jax.random.split(key, 4)
        B, L, H = (4, 256, 128)
        hs = 128
        X = jax.random.normal(kx, (B, L, H), dtype=jnp.float32)
        W_Q = jax.random.normal(kq, (H, hs), dtype=jnp.float32) / H
        W_K = jax.random.normal(kk, (H, hs), dtype=jnp.float32) / H
        W_V = jax.random.normal(kv, (H, hs), dtype=jnp.float32) / H
        return {'X': X, 'W_Q': W_Q, 'W_K': W_K, 'W_V': W_V}
    _L0_attn_all = _L0_attn_setup()
    _L0_attn_in = {k: v for k, v in _L0_attn_all.items() if k in ('W_Q', 'W_K', 'W_V')}
    del _L0_attn_all

    def _L0_xattn_setup():
        import jax, jax.numpy as jnp
        import numpy as np
        B, LQ, LK = (8, 256, 256)
        QD, KD, VD = (128, 64, 64)
        key = jax.random.key(seed)
        ks = jax.random.split(key, 9)
        s = 0.02
        return {'query': jax.random.normal(ks[0], (B, LQ, QD), jnp.float32), 'key': jax.random.normal(ks[1], (B, LK, KD), jnp.float32), 'value': jax.random.normal(ks[2], (B, LK, VD), jnp.float32), 'Wq': jax.random.normal(ks[3], (QD, QD), jnp.float32) * s, 'bq': jnp.zeros((QD,), jnp.float32), 'Wk': jax.random.normal(ks[4], (KD, QD), jnp.float32) * s, 'bk': jnp.zeros((QD,), jnp.float32), 'Wv': jax.random.normal(ks[5], (VD, QD), jnp.float32) * s, 'bv': jnp.zeros((QD,), jnp.float32)}
    _L0_xattn_all = _L0_xattn_setup()
    _L0_xattn_in = {k: v for k, v in _L0_xattn_all.items() if k in ('Wq', 'bq', 'Wk', 'bk', 'Wv', 'bv')}
    del _L0_xattn_all

    def _L0_ffn_setup():
        import jax, jax.numpy as jnp
        import numpy as np
        K = 2
        key = jax.random.key(seed)
        ks = jax.random.split(key, 7)
        B, S, H, F, E = (4, 256, 128, 512, 6)
        s = 0.02
        return {'x': jax.random.normal(ks[0], (B, S, H), dtype=jnp.float32), 'Wg': jax.random.normal(ks[1], (H, E), dtype=jnp.float32) * s, 'bg': jnp.zeros((E,), dtype=jnp.float32), 'W1': jax.random.normal(ks[2], (E, H, F), dtype=jnp.float32) * s, 'b1': jnp.zeros((E, F), dtype=jnp.float32), 'W2': jax.random.normal(ks[3], (E, F, H), dtype=jnp.float32) * s, 'b2': jnp.zeros((E, H), dtype=jnp.float32)}
    _L0_ffn_all = _L0_ffn_setup()
    _L0_ffn_in = {k: v for k, v in _L0_ffn_all.items() if k in ('Wg', 'bg', 'W1', 'b1', 'W2', 'b2')}
    del _L0_ffn_all

    def _L1_attn_setup():
        import jax, jax.numpy as jnp
        import numpy as np
        key = jax.random.key(seed)
        k1, k2, k3 = jax.random.split(key, 3)
        N, S, D = (8, 256, 128)
        x = jax.random.normal(k1, (N, S, D), dtype=jnp.float32)
        std = np.sqrt(2.0 / D).astype(np.float32)
        w_lhs = jax.random.normal(k2, (1, 1, D), dtype=jnp.float32) * std
        w_rhs = jax.random.normal(k3, (1, 1, D), dtype=jnp.float32) * std
        return {'x': x, 'w_lhs': w_lhs, 'w_rhs': w_rhs}
    _L1_attn_all = _L1_attn_setup()
    _L1_attn_in = {k: v for k, v in _L1_attn_all.items() if k in ('w_lhs', 'w_rhs')}
    del _L1_attn_all

    def _L1_xattn_setup():
        import jax, jax.numpy as jnp
        import numpy as np
        HEADS = 16
        D_MODEL = 128
        IMG_MODEL = 64
        D_K = D_MODEL // HEADS
        key = jax.random.key(seed)
        ks = jax.random.split(key, 12)
        B, LQ, LKV = (8, 256, 128)
        s_dm = 1.0 / np.sqrt(D_MODEL)
        s_im = 1.0 / np.sqrt(IMG_MODEL)
        return {'q': jax.random.normal(ks[0], (B, LQ, D_MODEL), jnp.float32), 'k': jax.random.normal(ks[1], (B, LKV, IMG_MODEL), jnp.float32), 'v': jax.random.normal(ks[2], (B, LKV, IMG_MODEL), jnp.float32), 'Wq': jax.random.normal(ks[3], (D_MODEL, D_MODEL), jnp.float32) * s_dm, 'bq': jnp.zeros((D_MODEL,), jnp.float32), 'Wk': jax.random.normal(ks[4], (IMG_MODEL, D_MODEL), jnp.float32) * s_im, 'bk': jnp.zeros((D_MODEL,), jnp.float32), 'Wv': jax.random.normal(ks[5], (IMG_MODEL, D_MODEL), jnp.float32) * s_im, 'bv': jnp.zeros((D_MODEL,), jnp.float32), 'Wo': jax.random.normal(ks[6], (D_MODEL, D_MODEL), jnp.float32) * s_dm, 'bo': jnp.zeros((D_MODEL,), jnp.float32)}
    _L1_xattn_all = _L1_xattn_setup()
    _L1_xattn_in = {k: v for k, v in _L1_xattn_all.items() if k in ('Wq', 'bq', 'Wk', 'bk', 'Wv', 'bv', 'Wo', 'bo')}
    del _L1_xattn_all

    def _L1_ffn_setup():
        import jax, jax.numpy as jnp
        import numpy as np
        HIDDEN = 128
        INTER = 512
        key = jax.random.key(seed)
        k1, k2, k3, k4, k5 = jax.random.split(key, 5)
        hidden_states = jax.random.normal(k1, (4, 256, HIDDEN), dtype=jnp.float32)
        W1 = jax.random.normal(k2, (HIDDEN, INTER), dtype=jnp.float32) * (1.0 / np.sqrt(HIDDEN))
        b1 = jax.random.normal(k3, (INTER,), dtype=jnp.float32) * 0.02
        W2 = jax.random.normal(k4, (INTER, HIDDEN), dtype=jnp.float32) * (1.0 / np.sqrt(INTER))
        b2 = jax.random.normal(k5, (HIDDEN,), dtype=jnp.float32) * 0.02
        return {'hidden_states': hidden_states, 'W1': W1, 'b1': b1, 'W2': W2, 'b2': b2}
    _L1_ffn_all = _L1_ffn_setup()
    _L1_ffn_in = {k: v for k, v in _L1_ffn_all.items() if k in ('W1', 'b1', 'W2', 'b2')}
    del _L1_ffn_all
    return {'x': x, 'ctx_512': ctx_512, 'L0_attn_W_Q': _L0_attn_in['W_Q'], 'L0_attn_W_K': _L0_attn_in['W_K'], 'L0_attn_W_V': _L0_attn_in['W_V'], 'L0_xattn_Wq': _L0_xattn_in['Wq'], 'L0_xattn_bq': _L0_xattn_in['bq'], 'L0_xattn_Wk': _L0_xattn_in['Wk'], 'L0_xattn_bk': _L0_xattn_in['bk'], 'L0_xattn_Wv': _L0_xattn_in['Wv'], 'L0_xattn_bv': _L0_xattn_in['bv'], 'L0_ffn_Wg': _L0_ffn_in['Wg'], 'L0_ffn_bg': _L0_ffn_in['bg'], 'L0_ffn_W1': _L0_ffn_in['W1'], 'L0_ffn_b1': _L0_ffn_in['b1'], 'L0_ffn_W2': _L0_ffn_in['W2'], 'L0_ffn_b2': _L0_ffn_in['b2'], 'L1_attn_w_lhs': _L1_attn_in['w_lhs'], 'L1_attn_w_rhs': _L1_attn_in['w_rhs'], 'L1_xattn_Wq': _L1_xattn_in['Wq'], 'L1_xattn_bq': _L1_xattn_in['bq'], 'L1_xattn_Wk': _L1_xattn_in['Wk'], 'L1_xattn_bk': _L1_xattn_in['bk'], 'L1_xattn_Wv': _L1_xattn_in['Wv'], 'L1_xattn_bv': _L1_xattn_in['bv'], 'L1_xattn_Wo': _L1_xattn_in['Wo'], 'L1_xattn_bo': _L1_xattn_in['bo'], 'L1_ffn_W1': _L1_ffn_in['W1'], 'L1_ffn_b1': _L1_ffn_in['b1'], 'L1_ffn_W2': _L1_ffn_in['W2'], 'L1_ffn_b2': _L1_ffn_in['b2']}

def reference(x, ctx_512, L0_attn_W_Q, L0_attn_W_K, L0_attn_W_V, L0_xattn_Wq, L0_xattn_bq, L0_xattn_Wk, L0_xattn_bk, L0_xattn_Wv, L0_xattn_bv, L0_ffn_Wg, L0_ffn_bg, L0_ffn_W1, L0_ffn_b1, L0_ffn_W2, L0_ffn_b2, L1_attn_w_lhs, L1_attn_w_rhs, L1_xattn_Wq, L1_xattn_bq, L1_xattn_Wk, L1_xattn_bk, L1_xattn_Wv, L1_xattn_bv, L1_xattn_Wo, L1_xattn_bo, L1_ffn_W1, L1_ffn_b1, L1_ffn_W2, L1_ffn_b2):
    import jax
    import jax.numpy as jnp

    def _L0_attn_ref(X, W_Q, W_K, W_V):
        import jax, jax.numpy as jnp
        import numpy as np
        SCALE_BASE = 512.0
        GAMMA = 0.96875

        def xpos(x, downscale=False):
            B, L, d = x.shape
            half = d // 2
            scale_vec = (jnp.arange(0, d, 2, dtype=jnp.float32) + 0.4 * d) / (1.4 * d)
            pos = jnp.arange(L, dtype=jnp.float32)
            scale = scale_vec[None, :] ** (pos[:, None] / SCALE_BASE)
            if downscale:
                scale = 1.0 / scale
            inv_freq = 1.0 / 10000.0 ** (jnp.arange(half, dtype=jnp.float32) / half)
            sinusoid = pos[:, None] * inv_freq[None, :]
            sin_s = jnp.repeat(jnp.sin(sinusoid) * scale, 2, axis=-1)
            cos_s = jnp.repeat(jnp.cos(sinusoid) * scale, 2, axis=-1)
            x1, x2 = (x[..., ::2], x[..., 1::2])
            rot = jnp.stack((-x2, x1), axis=-1).reshape(x.shape)
            return x * cos_s + rot * sin_s

        def decay_mask(L, gamma):
            n = jnp.arange(L)[:, None]
            m = jnp.arange(L)[None, :]
            diff = n - m
            expo = jnp.where(diff >= 0, diff, 0).astype(jnp.float32)
            return jnp.where(diff >= 0, gamma ** expo, 0.0)
        L = X.shape[1]
        Q = xpos(X @ W_Q)
        K = xpos(X @ W_K, downscale=True)
        V = X @ W_V
        D = decay_mask(L, GAMMA)
        ret = jnp.einsum('bnd,bmd->bnm', Q, K) * D[None]
        return ret @ V

    def _L0_xattn_ref(query, key, value, Wq, bq, Wk, bk, Wv, bv):
        import jax, jax.numpy as jnp
        import numpy as np
        B, LQ, LK = (8, 256, 256)
        QD, KD, VD = (128, 64, 64)
        q = jnp.einsum('bld,de->ble', query, Wq) + bq
        k = jnp.einsum('bld,de->ble', key, Wk) + bk
        v = jnp.einsum('bld,de->ble', value, Wv) + bv
        scores = jnp.einsum('bqe,bke->bqk', q, k)
        attn = jax.nn.softmax(scores, axis=-1)
        out = jnp.einsum('bqk,bke->bqe', attn, v)
        return out

    def _L0_ffn_ref(x, Wg, bg, W1, b1, W2, b2):
        import jax, jax.numpy as jnp
        import numpy as np
        K = 2
        B, S, H = x.shape
        xf = x.reshape(-1, H)
        gate = xf @ Wg + bg
        topk_scores, topk_idx = jax.lax.top_k(gate, K)
        topk_w = jax.nn.softmax(topk_scores, axis=-1)
        h = jnp.einsum('nh,ehf->nef', xf, W1) + b1
        h = jax.nn.gelu(h, approximate=False)
        eo = jnp.einsum('nef,efh->neh', h, W2) + b2
        sel = jnp.take_along_axis(eo, topk_idx[:, :, None], axis=1)
        out = jnp.einsum('nk,nkh->nh', topk_w, sel)
        return out.reshape(B, S, H)

    def _L1_attn_ref(x, w_lhs, w_rhs):
        import jax, jax.numpy as jnp
        import numpy as np
        lhs = x * w_lhs
        rhs = x * w_rhs
        scores = jnp.einsum('nsd,ntd->nst', lhs, rhs)
        attn = jax.nn.softmax(scores, axis=2)
        return jnp.einsum('nst,ntd->nsd', attn, x)

    def _L1_xattn_ref(q, k, v, Wq, bq, Wk, bk, Wv, bv, Wo, bo):
        import jax, jax.numpy as jnp
        import numpy as np
        HEADS = 16
        D_MODEL = 128
        IMG_MODEL = 64
        D_K = D_MODEL // HEADS
        B, LQ, _ = q.shape
        LKV = k.shape[1]
        qh = (q @ Wq + bq).reshape(B, LQ, HEADS, D_K).transpose(0, 2, 1, 3)
        kh = (k @ Wk + bk).reshape(B, LKV, HEADS, D_K).transpose(0, 2, 1, 3)
        vh = (v @ Wv + bv).reshape(B, LKV, HEADS, D_K).transpose(0, 2, 1, 3)
        scale = 1.0 / np.sqrt(D_K)
        scores = jnp.einsum('bhqd,bhkd->bhqk', qh, kh) * scale
        attn = jax.nn.softmax(scores, axis=-1)
        out = jnp.einsum('bhqk,bhkd->bhqd', attn, vh)
        concat = out.transpose(0, 2, 1, 3).reshape(B, LQ, D_MODEL)
        return concat @ Wo + bo

    def _L1_ffn_ref(hidden_states, W1, b1, W2, b2):
        import jax, jax.numpy as jnp
        import numpy as np
        HIDDEN = 128
        INTER = 512
        h = jax.nn.relu(jnp.einsum('bsh,hi->bsi', hidden_states, W1) + b1)
        return jnp.einsum('bsi,ih->bsh', h, W2) + b2
    x = _layernorm(x + _L0_attn_ref(x, L0_attn_W_Q, L0_attn_W_K, L0_attn_W_V), axis=-1)
    x = _layernorm(x + _L0_xattn_ref(x, ctx_512, ctx_512, L0_xattn_Wq, L0_xattn_bq, L0_xattn_Wk, L0_xattn_bk, L0_xattn_Wv, L0_xattn_bv), axis=-1)
    x = _layernorm(x + _L0_ffn_ref(x, L0_ffn_Wg, L0_ffn_bg, L0_ffn_W1, L0_ffn_b1, L0_ffn_W2, L0_ffn_b2), axis=-1)
    x = _layernorm(x + _L1_attn_ref(x, L1_attn_w_lhs, L1_attn_w_rhs), axis=-1)
    x = _layernorm(x + _L1_xattn_ref(x, ctx_512, ctx_512, L1_xattn_Wq, L1_xattn_bq, L1_xattn_Wk, L1_xattn_bk, L1_xattn_Wv, L1_xattn_bv, L1_xattn_Wo, L1_xattn_bo), axis=-1)
    x = _layernorm(x + _L1_ffn_ref(x, L1_ffn_W1, L1_ffn_b1, L1_ffn_W2, L1_ffn_b2), axis=-1)
    return x

_drawn_inputs = setup_inputs


def setup_inputs(seed=0):
    import zlib

    import numpy as np

    out = dict(_drawn_inputs(seed))
    spreads = {'L0_xattn_bq': (0.0, 0.674),
     'L0_xattn_bk': (0.0, 0.8),
     'L0_xattn_bv': (0.0, 0.1),
     'L0_ffn_bg': (0.0, 0.311),
     'L0_ffn_b1': (0.0, 0.426),
     'L0_ffn_b2': (0.0, 0.1),
     'L1_xattn_bq': (0.0, 0.406),
     'L1_xattn_bk': (0.0, 0.8),
     'L1_xattn_bv': (0.0, 0.1),
     'L1_xattn_bo': (0.0, 0.1)}
    factors = {'L0_xattn_Wq': 4.503,
     'L0_xattn_Wk': 3.434,
     'L1_attn_w_lhs': 2.754,
     'L1_ffn_b1': 5.055,
     'L1_ffn_b2': 3.42}
    for name, (base, spread) in spreads.items():
        noise = np.random.default_rng([zlib.crc32(name.encode()), seed]).standard_normal(out[name].shape)
        drawn = base * np.exp(spread * noise) if base else spread * noise
        out[name] = jnp.asarray(drawn.astype(out[name].dtype))
    for name, factor in factors.items():
        out[name] = (out[name] * factor).astype(out[name].dtype)
    return out
```

```python
from contextlib import ExitStack

import numpy as np

import concourse.bass as bass
from concourse import mybir
from concourse.alu_op_type import AluOpType as ALU

ACT = mybir.ActivationFunctionType
AX = mybir.AxisListType
F32 = mybir.dt.float32
F32R = mybir.dt.float32r
U32 = mybir.dt.uint32

B, L, D = 16, 56, 128
S, C = 1500, 64
SLOT = 64
PAIRS = B // 2
TOK = B * SLOT
KT, NT = 125, 12
CHUNK, NCH = 500, 3
TPC = CHUNK // KT
NE, F = 6, 512
FT = F // 128
H, DH = 16, 8
HH = H // 2
QC = HH * L
RT = 4
RR = QC // RT
EPS = 1e-5
NEG = -3.0e38

V_BQ0, V_BK0, V_BQ1, V_BK1, V_WL, V_WR, V_FB1, V_EB1 = 0, 1, 2, 3, 4, 5, 6, 10
NVEC = V_EB1 + NE * FT
K_COSQ, K_SINQ, K_COSK, K_SINK, K_MASK, K_HEAD, K_IOTA = 0, 64, 128, 192, 256, 384, 400
NCONST = K_IOTA + NE


def wait_count(eng, sem, value):
    if isinstance(value, int) and value <= 0:
        return
    eng.wait_ge(sem, value)


def peeled(eng, n, body):
    body(0)
    with eng.Fori(1, n - 1) as i:
        body(i)
    body(n - 1)


def decoder(nc: bass.Bass, t, consts, out):
    with ExitStack() as ctx:
        def sb(name, shape, dt=F32):
            return ctx.enter_context(nc.sbuf_tensor(name, shape, dt))

        def sem(name):
            return ctx.enter_context(nc.semaphore(name))

        ct_all = sb("ct_all", [128, B, S], F32R)
        cn = sb("cn", [KT, 4, NT * 129])
        ct_w = sb("ct_w", [128, 2, S], F32R)
        ct_1 = sb("ct_1", [C + 1, 2, S], F32R)
        q_hi = sb("q_hi", [128, 4, QC], F32R)
        q_lo = sb("q_lo", [C + 1, 4, QC], F32R)
        st_hi = sb("st_hi", [128, 2, 128], F32R)
        st_lo = sb("st_lo", [128, 2, 128], F32R)
        arena = sb("arena", [128, 4096])
        w1b = sb("w1b", [128, 2, F])
        w2b = sb("w2b", [128, 2, F])
        X = sb("X", [128, PAIRS, 128])
        Y = sb("Y", [128, PAIRS, 128])
        xT = sb("xT", [128, TOK])
        qT = sb("qT", [128, TOK])
        kc = sb("kc", [128, NCONST])
        ident = sb("ident", [128, 128])
        wq0 = sb("wq0", [128, 128])
        wq1 = sb("wq1", [128, 128])
        wkT0 = sb("wkT0", [128, 128])
        wkT1 = sb("wkT1", [128, 128])
        wv0 = sb("wv0", [C + 1, 128])
        wv1 = sb("wv1", [C + 1, H, DH + 1])
        wo = sb("wo", [128, 128])
        bo_b = sb("bo_b", [128, 128])
        fb2_b = sb("fb2_b", [128, 128])
        wg = sb("wg", [128, NE])
        bg = sb("bg", [1, NE])
        eb2 = sb("eb2", [NE, 128])
        ones = sb("ones", [128, 128])
        vecT = sb("vecT", [128, NVEC + FT])
        b1s = sb("b1s", [128, 2, FT])
        bkh = sb("bkh", [128, H])
        stats = sb("stats", [128, PAIRS, 6])
        mv = sb("mv", [128, PAIRS, 2])
        ve = sb("ve", [128, PAIRS])
        rstd = sb("rstd", [128, PAIRS])
        mhalf = sb("mhalf", [128, PAIRS])
        sm = sb("sm", [128, 8, PAIRS])
        gate = sb("gate", [128, PAIRS, 8])
        top = sb("top", [128, PAIRS, 8])
        topi = sb("topi", [128, PAIRS, 8], U32)
        topf = sb("topf", [128, PAIRS, 2])
        wexp = sb("wexp", [128, PAIRS, 8])
        wtmp = sb("wtmp", [128, PAIRS, NE])
        tmx = sb("tmx", [RR, RT, NCH])
        tm = sb("tm", [RR, RT])
        ps = ctx.enter_context(nc.psum_tensor("ps", [128, 8, 512], F32))
        qbk_dram = nc.dram_tensor("qbk_dram", (B, H, L), F32, kind="Internal").ap()

        ar4 = arena[:, :].rearrange("p (n c) -> p n c", n=4)
        rq, rk, rv, rm = (ar4[:, n, :] for n in range(4))
        e0 = arena[:, 0:S]
        e0T = arena[0:KT, S:S + NT * 128].rearrange("p (t n) -> p t n", n=128)
        qf0 = arena[:, S + NT * 128:S + NT * 128 + TOK]
        hT = ar4
        lT, rT, eb, ebT = (ar4[:, n, :] for n in range(4))
        u1 = arena[0:C + 1, 0:2 * QC].rearrange("p (s n) -> p s n", s=2)
        qbd = arena[:, 2 * QC:3 * QC]
        cat = arena[:, 3 * QC:3 * QC + 128]
        catT = arena[:, 3 * QC + 128:3 * QC + 128 + L]
        rec = arena[0:L, 3 * QC + 184:3 * QC + 184 + HH]
        qbkT = arena[0:H, 1536:1536 + TOK]
        u0 = w1b[0:C + 1, :, :].rearrange("p a b -> p (a b)")
        e1 = [cn[:, 2, n * QC:(n + 1) * QC] for n in range(3)]
        qrow = [cn[C:C + 1, 3, n * QC:(n + 1) * QC] for n in range(2)]
        mrow = cn[C:C + 1, 3, 2 * QC:3 * QC]
        wret = w1b[:, 1, :].rearrange("p (n c) -> p n c", n=4)
        wrkr = w2b[:, 1, 0:128]
        wT = qT
        wk_raw = [Y[0:C, n, :] for n in range(2)]
        vrows = Y[0:NVEC, 2, :]

        def cn_tile(s, k, lo, hi):
            return cn[:, s, k * 129 + lo:k * 129 + hi]

        def cn_cols(s, lo, hi):
            return cn[:, s, :].rearrange("p (t n) -> p t n", n=129)[:, :, lo:hi]

        def ctx_rows(b):
            return t["ctx_512"][b].rearrange("(p t) d -> p t d", t=NT)

        def banks(b, w=512):
            return ps[:, b:b + 2, :].rearrange("p b (t n) -> p (b t) n", n=128)

        x_in = sem("x_in")
        ret_in = sem("ret_in")
        vec_in = sem("vec_in")
        w0_in = sem("w0_in")
        w1_in = sem("w1_in")
        moe_in = sem("moe_in")
        ctx_in = [sem(f"ctx_in{s}") for s in range(4)]
        exp_in = [sem(f"exp_in{s}") for s in range(2)]
        ffn_in = sem("ffn_in")
        ct_in = [sem(f"ct_in{s}") for s in range(2)]
        qrow_in = [sem(f"qrow_in{s}") for s in range(2)]
        qbk_out = sem("qbk_out")
        out_done = sem("out_done")
        pool_set = sem("pool_set")
        x_pad = sem("x_pad")
        xt_ps = sem("xt_ps")
        xt_ready = sem("xt_ready")
        vec_ps = sem("vec_ps")
        vec_ready = sem("vec_ready")
        dve_step = sem("dve_step")
        ve_ready = sem("ve_ready")
        rstd_ready = sem("rstd_ready")
        x_norm = sem("x_norm")
        rot_ready = sem("rot_ready")
        ret_ps = sem("ret_ps")
        ret_read = sem("ret_read")
        rv_ready = sem("rv_ready")
        q_ps = sem("q_ps")
        q_ready = sem("q_ready")
        qf_ps = sem("qf_ps")
        qf_ready = sem("qf_ready")
        qbk_ps = sem("qbk_ps")
        qbk_ready = sem("qbk_ready")
        dup_ready = sem("dup_ready")
        t_ps = sem("t_ps")
        ct_hi = sem("ct_hi")
        ct_ready = sem("ct_ready")
        sthi_ready = sem("sthi_ready")
        stlo_ready = sem("stlo_ready")
        s0_ps = sem("s0_ps")
        m0_step = sem("m0_step")
        shift0 = sem("shift0")
        e0_ready = sem("e0_ready")
        e0t_ps = sem("e0t_ps")
        e0t_act = sem("e0t_act")
        e0t_dve = sem("e0t_dve")
        u0_ps = sem("u0_ps")
        u0_ready = sem("u0_ready")
        o0_ps = sem("o0_ps")
        gate_ps = sem("gate_ps")
        top_ready = sem("top_ready")
        e2_ready = sem("e2_ready")
        b1_ready = sem("b1_ready")
        wexp_ready = sem("wexp_ready")
        wt_ps = sem("wt_ps")
        wt_ready = sem("wt_ready")
        b2_ps = sem("b2_ps")
        y_init = sem("y_init")
        h_ps = sem("h_ps")
        h_ready = sem("h_ready")
        eo_ps = sem("eo_ps")
        eo_read = sem("eo_read")
        lr_ready = sem("lr_ready")
        sa_ps = sem("sa_ps")
        sa_sub = sem("sa_sub")
        eb_zero = sem("eb_zero")
        sa_exp = sem("sa_exp")
        ebt_ps = sem("ebt_ps")
        ebt_ready = sem("ebt_ready")
        sao_ps = sem("sao_ps")
        bkh_ready = sem("bkh_ready")
        q1_ps = sem("q1_ps")
        q1_ready = sem("q1_ready")
        qbkT_ps = sem("qbkT_ps")
        qbkT_ready = sem("qbkT_ready")
        qbd_ready = sem("qbd_ready")
        qfold = sem("qfold")
        qhi_ready = sem("qhi_ready")
        qlo_ready = sem("qlo_ready")
        mx_ps = sem("mx_ps")
        mx_read = sem("mx_read")
        tm_ready = sem("tm_ready")
        tm_row = sem("tm_row")
        m_ready = sem("m_ready")
        aux_ready = sem("aux_ready")
        st_ps = sem("st_ps")
        e1_ready = sem("e1_ready")
        pv_done = sem("pv_done")
        u1_ready = sem("u1_ready")
        oh_ps = sem("oh_ps")
        rec_ready = sem("rec_ready")
        cat_ready = sem("cat_ready")
        catT_ps = sem("catT_ps")
        catT_ready = sem("catT_ready")
        wo_ps = sem("wo_ps")
        y1_ready = sem("y1_ready")
        xb_ready = sem("xb_ready")
        f_ps = sem("f_ps")
        f_ready = sem("f_ready")
        fo_ps = sem("fo_ps")

        NB0 = PAIRS // 2
        NB1 = B // 2

        block = ctx.enter_context(nc.Block())

        @block.sync
        def _(sp):
            def load(dst, src, s):
                sp.dma_start(dst, src).then_inc(s, 16)

            sp.wait_ge(x_pad, 1)
            xs = t["x"].rearrange("(r two) l d -> two l r d", two=2)
            load(X[0:L, :, :], xs[0], x_in)
            load(X[SLOT:SLOT + L, :, :], xs[1], x_in)
            load(wret[:, 0, :], t["L0_attn_W_Q"], ret_in)
            load(wret[:, 1, :], t["L0_attn_W_K"], ret_in)
            load(wret[:, 2, :], t["L0_attn_W_V"], ret_in)
            load(kc[:, :], consts, ret_in)
            rows = [("L0_xattn_bq", V_BQ0), ("L0_xattn_bk", V_BK0), ("L1_xattn_bq", V_BQ1), ("L1_xattn_bk", V_BK1)]
            for name, r in rows:
                load(vrows[r:r + 1, :], t[name].rearrange("(o n) -> o n", o=1), vec_in)
            load(vrows[V_WL:V_WL + 1, :], t["L1_attn_w_lhs"].rearrange("a b n -> (a b) n"), vec_in)
            load(vrows[V_WR:V_WR + 1, :], t["L1_attn_w_rhs"].rearrange("a b n -> (a b) n"), vec_in)
            load(vrows[V_FB1:V_FB1 + FT, :], t["L1_ffn_b1"].rearrange("(f n) -> f n", n=128), vec_in)
            load(vrows[V_EB1:NVEC, :], t["L0_ffn_b1"].rearrange("e (f n) -> (e f) n", n=128), vec_in)
            load(wk_raw[0], t["L0_xattn_Wk"], vec_in)
            load(wk_raw[1], t["L1_xattn_Wk"], vec_in)
            for s in range(4):
                load(cn_cols(s, 64, 128), ctx_rows(s), ctx_in[s])
            load(wq0[:, :], t["L0_xattn_Wq"], w0_in)
            load(wv0[0:C, :], t["L0_xattn_Wv"], w0_in)
            load(wv0[C:C + 1, :], t["L0_xattn_bv"].rearrange("(o n) -> o n", o=1), w0_in)
            load(wg[:, :], t["L0_ffn_Wg"], moe_in)
            load(bg[:, :], t["L0_ffn_bg"].rearrange("(o n) -> o n", o=1), moe_in)
            load(eb2[:, :], t["L0_ffn_b2"], moe_in)
            load(wq1[:, :], t["L1_xattn_Wq"], w1_in)
            load(wo[:, :], t["L1_xattn_Wo"], w1_in)
            sp.wait_ge(x_pad, 4)
            load(wv1[0:C, :, 0:DH], t["L1_xattn_Wv"].rearrange("c (h d) -> c h d", d=DH), w1_in)
            load(wv1[C:C + 1, :, 0:DH], t["L1_xattn_bv"].rearrange("(o h d) -> o h d", o=1, d=DH), w1_in)
            load(bo_b[:, :], t["L1_xattn_bo"].rearrange("(o n) -> o n", o=1).to_broadcast([128, 128]), w1_in)
            load(fb2_b[:, :], t["L1_ffn_b2"].rearrange("(o n) -> o n", o=1).to_broadcast([128, 128]), w1_in)

            with sp.Fori(1, NB0) as i:
                for s in range(4):
                    sp.wait_ge(u0_ps, 2 * i - 1 + s // 2)
                    load(cn_cols(s, 64, 128), ctx_rows(4 * i + s), ctx_in[s])

            def experts(i):
                for s in range(2):
                    if isinstance(i, int):
                        sp.wait_ge(o0_ps, 2)
                    else:
                        sp.wait_ge(eo_ps, 4 * i - 2 + 2 * s)
                    load(w1b[:, s, :], t["L0_ffn_W1"][2 * i + s], exp_in[s])
                    load(w2b[:, s, :].rearrange("p (f n) -> p f n", n=128),
                         t["L0_ffn_W2"][2 * i + s].rearrange("(f p) n -> p f n", p=128), exp_in[s])
            experts(0)
            with sp.Fori(1, NE // 2) as i:
                experts(i)
            sp.wait_ge(eo_ps, 2 * NE - 2)
            load(w1b[:, 0, :], t["L1_ffn_W1"], ffn_in)
            load(w2b[:, 0, :].rearrange("p (f n) -> p f n", n=128),
                 t["L1_ffn_W2"].rearrange("(f p) n -> p f n", p=128), ffn_in)

            sp.wait_ge(qbkT_ready, 2)
            sp.dma_start(qbk_dram.rearrange("b h q -> h b q"),
                         qbkT.rearrange("h (b q) -> h b q", q=SLOT)[:, :, 0:L]).then_inc(qbk_out, 16)
            sp.wait_ge(qbk_out, 16)

            def context(i):
                for s in range(2):
                    wait_count(sp, pv_done, 48 * i + 24 * s - 24)
                    b = 2 * i + s
                    load(cn_cols(s, 64, 128), ctx_rows(b), ct_in[s])
                    load(ct_w[:, s, :].bitcast(F32), ct_all[:, b, :].bitcast(F32), ct_in[s])
                    load(ct_1[0:C, s, :].bitcast(F32), ct_all[0:C, b, :].bitcast(F32), ct_in[s])
                    for hf in range(2):
                        wait_count(sp, aux_ready, 4 * i + 2 * s + hf - 1)
                        load(qrow[hf].rearrange("o (h q) -> o h q", q=L), qbk_dram[bass.ts(b, 1), hf * HH:(hf + 1) * HH, :],
                             qrow_in[hf])
            context(0)
            with sp.Fori(1, NB1) as i:
                context(i)

            sp.wait_ge(x_norm, 6)
            os = out.rearrange("(r two) l d -> two l r d", two=2)
            load(os[0], X[0:L, :, :], out_done)
            load(os[1], X[SLOT:SLOT + L, :, :], out_done)
            sp.wait_ge(out_done, 32)

        @block.gpsimd
        def _(g):
            g.memset(ident[:, :], 0.0).then_inc(pool_set, 1)
            g.memset(ones[:, :], 1.0).then_inc(pool_set, 1)
            g.memset(mhalf[:, :], -0.5).then_inc(pool_set, 1)
            g.memset(cn[:, :, :].rearrange("p s (t n) -> p (s t) n", n=129)[:, :, 128:129], 1.0).then_inc(pool_set, 1)
            g.wait_ge(pool_set, 4)
            g.affine_select(out=ident[:, :], in_=ident[:, :], compare_op=ALU.not_equal, fill=1.0, base=0,
                            pattern=[[-1, 128]], channel_multiplier=1).then_inc(pool_set, 1)
            g.memset(st_hi[:, :, :].bitcast(F32), 0.0).then_inc(pool_set, 1)
            g.memset(st_lo[:, :, :].bitcast(F32), 0.0).then_inc(pool_set, 1)
            g.memset(gate[:, :, :], NEG).then_inc(pool_set, 1)
            g.memset(wexp[:, :, :], 0.0).then_inc(pool_set, 1)
            g.memset(vecT[:, NVEC:NVEC + FT], 0.0).then_inc(pool_set, 1)

            def power(k):
                g.wait_ge(ve_ready, k + 1)
                g.tensor_tensor(rstd[:, :], ve[:, :], mhalf[:, :], ALU.pow).then_inc(rstd_ready, 1)

            def double(i):
                one = ones[0:KT, 0:1].unsqueeze(1).to_broadcast([KT, NT, 64])
                for s in range(4):
                    g.wait_ge(ctx_in[s], 16 * i + 16)
                    g.tensor_tensor(cn_cols(s, 0, 64), cn_cols(s, 64, 128), one, ALU.mult).then_inc(dup_ready, 1)

            double(0)
            power(0)
            with g.Fori(1, NB0) as i:
                double(i)
            power(1)
            power(2)
            g.wait_ge(lr_ready, 2)
            g.memset(eb, 0.0).then_inc(eb_zero, 1)
            power(3)
            power(4)
            power(5)

        @block.tensor
        def _(pe):
            mm = nc.tensor.matmul

            def transpose_state(k):
                for n in range(PAIRS):
                    ins = pe.transpose(ps[:, n // 4, (n % 4) * 128:(n % 4 + 1) * 128], X[:, n, :], ident[:, :])
                    if n % 4 == 3:
                        ins.then_inc(xt_ps, 1)

            def wide(bank, w, x, m=128):
                for n in range(2):
                    ins = pe.matmul(ps[0:m, bank + n, :], w, x[:, n * 512:(n + 1) * 512], start=True, stop=True)
                return ins

            pe.wait_ge(pool_set, 5)
            pe.wait_ge(x_in, 32)
            transpose_state(0)
            pe.wait_ge(vec_in, 16 * 10)
            pe.transpose(ps[:, 2, 0:NVEC], vrows, ident[0:NVEC, 0:NVEC])
            pe.transpose(ps[:, 2, 64:128], wk_raw[0], ident[0:C, 0:C])
            pe.transpose(ps[:, 2, 128:192], wk_raw[1], ident[0:C, 0:C]).then_inc(vec_ps, 1)

            pe.wait_ge(xt_ready, 2)
            pe.wait_ge(ret_in, 16 * 4)
            wide(3, wret[:, 0, :], xT).then_inc(ret_ps, 1)
            pe.wait_ge(rot_ready, 2)
            wide(5, wret[:, 3, :], xT).then_inc(ret_ps, 1)
            for n, bank in ((0, 7), (1, 0)):
                ins = pe.matmul(ps[:, bank, :], wret[:, 1, :], xT[:, n * 512:(n + 1) * 512], start=True, stop=True)
            ins.then_inc(ret_ps, 1)
            pe.wait_ge(rot_ready, 4)
            pe.wait_ge(vec_ready, 3)
            wide(1, wrkr, xT).then_inc(ret_ps, 1)
            pe.wait_ge(ret_read, 1)
            for n in range(PAIRS):
                ins = pe.matmul(banks(3)[:, n, :], xT[:, n * 128:(n + 1) * 128], wret[:, 2, :], start=True, stop=True)
            ins.then_inc(ret_ps, 1)
            pe.wait_ge(ret_read, 4)
            for n in range(PAIRS):
                ins = pe.matmul(banks(5)[:, n, :], rk[:, n * 128:(n + 1) * 128], rq[:, n * 128:(n + 1) * 128],
                                start=True, stop=True)
            ins.then_inc(ret_ps, 1)
            pe.wait_ge(ret_read, 5)
            pe.wait_ge(rv_ready, 1)
            for n in range(PAIRS):
                ins = pe.matmul(banks(3)[:, n, :], rm[:, n * 128:(n + 1) * 128], rv[:, n * 128:(n + 1) * 128],
                                start=True, stop=True)
            ins.then_inc(ret_ps, 1)

            pe.wait_ge(x_norm, 1)
            transpose_state(1)
            pe.wait_ge(w0_in, 16 * 3)
            pe.wait_ge(xt_ready, 4)
            wide(2, wq0[:, :], xT).then_inc(q_ps, 1)
            pe.wait_ge(q_ready, 1)
            wide(4, wkT0[:, :], qT).then_inc(qf_ps, 1)
            for n in range(PAIRS):
                ins = pe.matmul(ps[:, 6, n:n + 1], qT[:, n * 128:(n + 1) * 128], vecT[:, V_BK0:V_BK0 + 1],
                                start=True, stop=True)
            ins.then_inc(qbk_ps, 1)

            def turn_context(p, h):
                for j in range(2):
                    pe.wait_ge(dup_ready, 2 * p + j + 1)
                    for c in range(NCH):
                        n = 6 * p + 3 * j + c
                        wait_count(pe, ct_ready, n - 1)
                        for k in range(TPC):
                            ins = pe.transpose(ps[:, (3 * j + c) % 2, k * KT:(k + 1) * KT],
                                               cn_tile(2 * h + j, c * TPC + k, 0, 128), ident[0:KT, 0:KT])
                        ins.then_inc(t_ps, 1)

            def attend0(i):
                for h in range(2):
                    p = 2 * i + h
                    last = isinstance(i, int) and p == PAIRS - 1
                    pe.wait_ge(stlo_ready, p + 1)
                    pe.wait_ge(ct_ready, 6 * p + 6)
                    wait_count(pe, e0_ready, p)
                    for c in range(NCH):
                        for n, (j, q) in enumerate(((0, st_hi), (0, st_lo), (1, st_hi), (1, st_lo))):
                            ins = pe.matmul(ps[:, 2 + c, 0:CHUNK], q[:, j, :],
                                            ct_all[:, 2 * p + j, c * CHUNK:(c + 1) * CHUNK],
                                            start=(n == 0), stop=(n == 3))
                    ins.then_inc(s0_ps, 1)
                    if not last:
                        turn_context(p + 1, 1 - h)
                    pe.wait_ge(e0_ready, p + 1)
                    for c in range(NCH):
                        m = 3 * p + c
                        bank = 5 + (3 * h + c) % 2
                        if c == 0:
                            wait_count(pe, e0t_dve, p)
                        elif c == 1:
                            wait_count(pe, e0t_act, 2 * p)
                        else:
                            pe.wait_ge(e0t_act, 2 * p + 1)
                        for k in range(TPC):
                            ins = pe.transpose(ps[0:KT, bank, k * 128:(k + 1) * 128],
                                               e0[:, (c * TPC + k) * KT:(c * TPC + k + 1) * KT], ident[:, :])
                        ins.then_inc(e0t_ps, 1)
                    pe.wait_ge(e0t_act, 2 * p + 2)
                    pe.wait_ge(e0t_dve, p + 1)
                    wait_count(pe, u0_ready, p)
                    for j in range(2):
                        for k in range(NT):
                            ins = pe.matmul(ps[0:C + 1, 7, j * 64:(j + 1) * 64], cn_tile(2 * h + j, k, 64, 129),
                                            e0T[:, k, j * 64:(j + 1) * 64], start=(k == 0), stop=(k == NT - 1))
                    ins.then_inc(u0_ps, 1)

            turn_context(0, 0)
            pe.wait_ge(qbk_ready, 1)
            peeled(pe, NB0, attend0)
            pe.wait_ge(u0_ready, PAIRS)
            for n in range(PAIRS):
                ins = pe.matmul(banks(0)[:, n, :], u0[:, n * 128:(n + 1) * 128], wv0[:, :], start=True, stop=True)
                if n % 4 == 3:
                    ins.then_inc(o0_ps, 1)

            pe.wait_ge(x_norm, 2)
            transpose_state(2)
            pe.wait_ge(moe_in, 16 * 3)
            pe.wait_ge(xt_ready, 6)
            for n in range(PAIRS):
                pe.matmul(ps[:, 4, n * 8:n * 8 + NE], xT[:, n * 128:(n + 1) * 128], wg[:, :], start=True, stop=False)
                ins = pe.matmul(ps[:, 4, n * 8:n * 8 + NE], ones[0:1, :], bg[:, :], start=False, stop=True)
            ins.then_inc(gate_ps, 1)

            def hidden(e, s):
                pe.wait_ge(exp_in[s], 16 * (e - s) + 32)
                for f in range(FT):
                    for n in range(2):
                        m = 8 * e + 2 * f + n
                        wait_count(pe, h_ready, m - 3)
                        pe.matmul(ps[:, (2 * f + n) % 4, :], w1b[:, s, f * 128:(f + 1) * 128],
                                  xT[:, n * 512:(n + 1) * 512], start=True, stop=True).then_inc(h_ps, 1)

            def expert_out(e, s):
                pe.wait_ge(h_ready, 8 * e + 8)
                wait_count(pe, eo_read, 2 * e - 2)
                for n in range(PAIRS):
                    for f in range(FT):
                        ins = pe.matmul(banks(4 + 2 * s)[:, n, :], hT[:, f, n * 128:(n + 1) * 128],
                                        w2b[:, s, f * 128:(f + 1) * 128], start=(f == 0), stop=(f == FT - 1))
                    if n % 4 == 3:
                        ins.then_inc(eo_ps, 1)

            def experts(i):
                for s in range(2):
                    if isinstance(i, int) and i + s == 0:
                        hidden(0, 0)
                        pe.wait_ge(wexp_ready, 1)
                        for n in range(PAIRS):
                            ins = pe.transpose(ps[0:8, 6 + n // 4, (n % 4) * 128:(n % 4 + 1) * 128], wexp[:, n, :],
                                               ident[:, :])
                        ins.then_inc(wt_ps, 1)
                        pe.wait_ge(wt_ready, 1)
                        for n in range(PAIRS):
                            ins = pe.matmul(banks(4)[:, n, :], wT[0:NE, n * 128:(n + 1) * 128], eb2[:, :],
                                            start=True, stop=True)
                        ins.then_inc(b2_ps, 1)
                        pe.wait_ge(y_init, 1)
                    else:
                        hidden(2 * i + s, s)
                    expert_out(2 * i + s, s)

            experts(0)
            with pe.Fori(1, NE // 2) as i:
                experts(i)

            pe.wait_ge(x_norm, 3)
            transpose_state(3)
            pe.wait_ge(lr_ready, 2)
            for n in range(PAIRS):
                for j in range(2):
                    o = n * 128 + j * 64
                    ins = pe.matmul(ps[j * 64:j * 64 + 64, 2, n * L:(n + 1) * L], lT[:, o:o + 64], rT[:, o:o + L],
                                    start=True, stop=True)
            ins.then_inc(sa_ps, 1)
            pe.wait_ge(sa_exp, 2)
            for n in range(PAIRS):
                ins = pe.transpose(banks(3)[:, n, :], eb[:, n * 128:(n + 1) * 128], ident[:, :])
            ins.then_inc(ebt_ps, 1)
            pe.wait_ge(ebt_ready, 1)
            for n in range(PAIRS):
                ins = pe.matmul(banks(5)[:, n, :], ebT[:, n * 128:(n + 1) * 128], X[:, n, :], start=True, stop=True)
            ins.then_inc(sao_ps, 1)

            pe.wait_ge(x_norm, 4)
            transpose_state(4)
            pe.wait_ge(w1_in, 16 * 6)
            pe.wait_ge(xt_ready, 10)
            wide(2, wq1[:, :], xT).then_inc(q1_ps, 1)
            pe.wait_ge(q1_ready, 1)
            pe.wait_ge(bkh_ready, 1)
            wide(4, bkh[:, :], qT, H).then_inc(qbkT_ps, 1)

            def fold(g, k):
                pe.wait_ge(qbd_ready, g + 1)
                pe.matmul(ps[:, 7, 0:QC], wkT1[:, :], qbd, start=True, stop=True).then_inc(qfold, 1)

            def scores_for_max(g, k, u):
                r, c = divmod(u, NCH)
                wait_count(pe, mx_read, 12 * g + u - 1)
                pe.matmul(ps[0:RR, 5 + u % 2, 0:CHUNK], q_hi[:, k, r * RR:(r + 1) * RR],
                          ct_w[:, (k // 2) % 2, c * CHUNK:(c + 1) * CHUNK], start=True, stop=True).then_inc(mx_ps, 1)

            def scores(g, k, u):
                n = 12 * g + u
                s = (k // 2) % 2
                wait_count(pe, e1_ready, n - 2)
                bank = ps[0:KT, u % 3, 0:QC]
                pe.matmul(bank, ct_w[:, s, u * KT:(u + 1) * KT], q_hi[:, k, :], start=True, stop=False)
                if u == 0:
                    pe.wait_ge(aux_ready, g + 1)
                pe.matmul(bank, ct_1[:, s, u * KT:(u + 1) * KT], q_lo[:, k, :], start=False, stop=True)\
                    .then_inc(st_ps, 1)

            def heads(g, k):
                if isinstance(g, int) and g == 2 * B - 2:
                    pe.wait_ge(aux_ready, 2 * B)
                elif isinstance(g, int) and g == 2 * B - 1:
                    pe.wait_ge(cat_ready, 2 * B - 1)
                else:
                    pe.wait_ge(qlo_ready, g + 3)
                pe.wait_ge(u1_ready, g + 1)
                for h in range(HH):
                    ins = pe.matmul(ps[0:L, 7, h * (DH + 1):(h + 1) * (DH + 1)], u1[:, k % 2, h * L:(h + 1) * L],
                                    wv1[:, (k % 2) * HH + h, :], start=True, stop=True)
                ins.then_inc(oh_ps, 1)

            def turn_heads(b):
                pe.wait_ge(cat_ready, 2 * b + 2)
                pe.transpose(ps[:, 7, 0:128], cat, ident[:, :]).then_inc(catT_ps, 1)

            def project(b, j):
                pe.wait_ge(catT_ready, b + 1)
                pe.matmul(ps[64 * j:64 * j + L, 7, 0:128], catT, wo[:, :], start=True, stop=True).then_inc(wo_ps, 1)

            def half(i, k, before, after, after2):
                g = 4 * i + k
                k1, k2, k0 = (k + 1) % 4, (k + 2) % 4, (k - 1) % 4
                done = 2 * i + k // 2 - 1
                for u in range(NT):
                    if u < NT - 2:
                        scores(g, k, u + 2)
                    elif after:
                        scores(g + 1, k1, u + 2 - NT)
                    pe.wait_ge(e1_ready, 12 * g + u + 1)
                    if u == 0:
                        wait_count(pe, u1_ready, g - 1)
                    pe.matmul(ps[0:C + 1, 3 + k % 2, 0:QC], cn_tile((k // 2) % 2, u, 64, 129), e1[u % 3],
                              start=(u == 0), stop=(u == NT - 1)).then_inc(pv_done, 1)
                    if u < 6 and after:
                        if u == 0:
                            pe.wait_ge(qhi_ready, g + 2)
                            if k % 2 == 1:
                                pe.wait_ge(ct_in[k1 // 2], 48 * (i + 1 + (k1 == 0)))
                        scores_for_max(g + 1, k1, 2 * u)
                        scores_for_max(g + 1, k1, 2 * u + 1)
                    if u == 1 and before:
                        heads(g - 1, k0)
                    if u == 3 and before and k % 2 == 0:
                        turn_heads(done)
                    if u == 5 and before and k % 2 == 0:
                        project(done, k0 // 2)
                    if u == 8 and after:
                        if before and k % 2 == 0:
                            pe.wait_ge(y1_ready, done + 1)
                        elif before:
                            pe.wait_ge(cat_ready, g)
                        maxima_row(g + 1)
                    if u == 10 and after2:
                        pe.wait_ge(aux_ready, g + 2)
                        fold(g + 2, k2)

            def maxima_row(g):
                pe.wait_ge(tm_ready, g + 1)
                for r in range(RT):
                    ins = pe.matmul(ps[C:C + 1, 7, r * RR:(r + 1) * RR], tm[:, r:r + 1], ident[0:RR, 0:RR],
                                    start=True, stop=True)
                ins.then_inc(tm_row, 1)

            fold(0, 0)
            pe.wait_ge(qlo_ready, 1)
            pe.wait_ge(ct_in[0], 48)
            fold(1, 1)
            pe.wait_ge(qhi_ready, 1)
            for u in range(NT):
                scores_for_max(0, 0, u)
            pe.wait_ge(qlo_ready, 2)
            maxima_row(0)
            scores(0, 0, 0)
            scores(0, 0, 1)

            def attend1(i):
                for k in range(4):
                    g = 4 * i + k
                    flat = isinstance(i, int)
                    half(i, k, before=not flat or g > 0, after=not flat or g < 2 * B - 1,
                         after2=not flat or g < 2 * B - 2)

            peeled(pe, NB1, attend1)
            heads(2 * B - 1, 3)
            turn_heads(B - 1)
            project(B - 1, 1)

            pe.wait_ge(x_norm, 5)
            transpose_state(5)
            pe.wait_ge(ffn_in, 32)
            pe.wait_ge(xt_ready, 12)
            for f in range(FT):
                for n in range(2):
                    m = 2 * f + n
                    wait_count(pe, f_ready, m - 3)
                    pe.matmul(ps[:, 2 + m % 4, :], w1b[:, 0, f * 128:(f + 1) * 128], xT[:, n * 512:(n + 1) * 512],
                              start=True, stop=True).then_inc(f_ps, 1)
            pe.wait_ge(f_ready, 8)
            for n in range(PAIRS):
                for f in range(FT):
                    ins = pe.matmul(banks(6)[:, n, :], hT[:, f, n * 128:(n + 1) * 128],
                                    w2b[:, 0, f * 128:(f + 1) * 128], start=(f == 0), stop=(f == FT - 1))
                if n % 4 == 3:
                    ins.then_inc(fo_ps, 1)

        @block.scalar
        def _(act):
            waited = act.alloc_register("waited")

            def wait_apart(s, value):
                wait_count(act, s, value)
                act.reg_mov(waited, 0)

            def state(k):
                for n in range(2):
                    act.wait_ge(xt_ps, 2 * k + n + 1)
                    act.activation(xT[:, n * 512:(n + 1) * 512], ps[:, n, :], ACT.Copy).then_inc(xt_ready, 1)

            state(0)
            act.wait_ge(vec_ps, 1)
            act.activation(vecT[:, 0:NVEC], ps[:, 2, 0:NVEC], ACT.Copy).then_inc(vec_ready, 1)
            for n, w in enumerate((wkT0, wkT1)):
                act.activation(w[:, :].rearrange("p (a c) -> p a c", a=2),
                               ps[:, 2, 64 + 64 * n:128 + 64 * n].unsqueeze(1).to_broadcast([128, 2, 64]),
                               ACT.Copy).then_inc(vec_ready, 1)
            act.wait_ge(ret_ps, 5)
            act.activation(rv.rearrange("p (b n) -> p b n", b=2), ps[:, 3:5, :], ACT.Copy).then_inc(rv_ready, 1)

            state(1)
            act.wait_ge(q_ps, 1)
            act.wait_ge(vec_ready, 1)
            act.activation(qT[:, :].rearrange("p (b n) -> p b n", b=2), ps[:, 2:4, :], ACT.Identity,
                           bias=vecT[:, V_BQ0:V_BQ0 + 1]).then_inc(q_ready, 1)
            act.wait_ge(qf_ps, 1)
            act.activation(qf0.rearrange("p (b n) -> p b n", b=2), ps[:, 4:6, :], ACT.Copy).then_inc(qf_ready, 1)

            def split_hi(p, j, c):
                wait_apart(t_ps, 6 * p + 3 * j + c + 1)
                act.activation(ct_all[:, 2 * p + j, c * CHUNK:(c + 1) * CHUNK], ps[:, (3 * j + c) % 2, 0:CHUNK],
                               ACT.Copy).then_inc(ct_hi, 1)

            def stage_hi(p):
                act.wait_ge(qf_ready, 1)
                act.wait_ge(pool_set, 10)
                wait_apart(s0_ps, p)
                act.activation(diag(st_hi), qf0[:, bass.ts(p, 128)].rearrange("p (j n) -> p j n", j=2),
                               ACT.Copy).then_inc(sthi_ready, 1)

            def diag(st):
                return st[:, :, :].rearrange("p j n -> p (j n)").rearrange("p (a n) -> p a n", n=64)[:, 0:4:3, :]

            def attend0(i):
                for h in range(2):
                    p = 2 * i + h
                    last = isinstance(i, int) and p == PAIRS - 1
                    if not last:
                        for j in range(2):
                            for c in range(NCH):
                                split_hi(p + 1, j, c)
                    act.wait_ge(shift0, p + 1)
                    wait_apart(e0t_ps, 3 * p)
                    act.activation(e0.rearrange("p (c n) -> p c n", c=NCH), ps[:, 2:5, 0:CHUNK], ACT.Exp,
                                   bias=sm[:, 1, 0:1], accum_out=sm[:, 2, bass.ts(p, 1)]).then_inc(e0_ready, 1)
                    if not last:
                        stage_hi(p + 1)
                    wait_count(act, u0_ps, p)
                    for c in (0, 2):
                        act.wait_ge(e0t_ps, 3 * p + c + 1)
                        act.activation(e0T[:, c * TPC:(c + 1) * TPC, :].rearrange("p t n -> p (t n)"),
                                       ps[0:KT, 5 + (3 * h + c) % 2, :], ACT.Copy).then_inc(e0t_act, 1)

            for j in range(2):
                for c in range(NCH):
                    split_hi(0, j, c)
            stage_hi(0)
            peeled(act, NB0, attend0)

            state(2)
            act.wait_ge(top_ready, 1)
            act.activation(sm[:, 3, :], sm[:, 3, :], ACT.Exp).then_inc(e2_ready, 1)

            def experts(i):
                for s in range(2):
                    e = 2 * i + s
                    wait_count(act, eo_ps, 2 * e)
                    act.wait_ge(b1_ready, e + 1)
                    for f in range(FT):
                        for n in range(2):
                            m = 8 * e + 2 * f + n
                            act.wait_ge(h_ps, m + 1)
                            act.activation(hT[:, f, n * 512:(n + 1) * 512], ps[:, (2 * f + n) % 4, :], ACT.Gelu,
                                           bias=b1s[:, s, f:f + 1]).then_inc(h_ready, 1)

            experts(0)
            with act.Fori(1, NE // 2) as i:
                experts(i)

            state(3)
            act.wait_ge(sa_sub, 2)
            act.wait_ge(eb_zero, 1)
            for j in range(2):
                r = slice(64 * j, 64 * j + 64)
                act.activation(eb[r, :].rearrange("p (t n) -> p t n", n=128)[:, :, 64 * j:64 * j + L],
                               lT[r, 0:PAIRS * L].rearrange("p (t n) -> p t n", n=L), ACT.Exp).then_inc(sa_exp, 1)
            act.wait_ge(ebt_ps, 1)
            act.activation(ebT.rearrange("p (b n) -> p b n", b=2), ps[:, 3:5, :], ACT.Copy).then_inc(ebt_ready, 1)

            state(4)
            act.wait_ge(q1_ps, 1)
            act.activation(qT[:, :].rearrange("p (b n) -> p b n", b=2), ps[:, 2:4, :], ACT.Identity,
                           bias=vecT[:, V_BQ1:V_BQ1 + 1]).then_inc(q1_ready, 1)
            act.wait_ge(qbkT_ps, 1)
            act.activation(qbkT.rearrange("p (b n) -> p b n", b=2), ps[0:H, 4:6, :], ACT.Copy).then_inc(qbkT_ready, 2)

            def high(g, k):
                act.wait_ge(qfold, g + 1)
                act.activation(q_hi[:, k, :], ps[:, 7, 0:QC], ACT.Copy).then_inc(qhi_ready, 1)

            def sums(g, k):
                act.wait_ge(pv_done, 12 * g + 12)
                wait_count(act, oh_ps, g - 1)
                act.activation(u1[:, k % 2, :], ps[0:C + 1, 3 + k % 2, 0:QC], ACT.Copy).then_inc(u1_ready, 1)

            def turned(b):
                act.wait_ge(catT_ps, b + 1)
                act.activation(catT, ps[:, 7, 0:L], ACT.Copy).then_inc(catT_ready, 1)

            def attend1(i):
                for k in range(4):
                    g = 4 * i + k
                    flat = isinstance(i, int)
                    for u in range(NT):
                        n = 12 * g + u
                        act.wait_ge(st_ps, n + 1)
                        wait_count(act, pv_done, n - 2)
                        act.activation(e1[u % 3], ps[0:KT, u % 3, 0:QC], ACT.Exp).then_inc(e1_ready, 1)
                        if u == 1 and (not flat or g > 0):
                            sums(g - 1, k - 1)
                        if u == 5 and k % 2 == 0 and (not flat or g > 0):
                            turned(2 * i + k // 2 - 1)
                    if not flat or g < 2 * B - 2:
                        high(g + 2, (k + 2) % 4)

            high(0, 0)
            high(1, 1)
            peeled(act, NB1, attend1)
            sums(2 * B - 1, 3)
            turned(B - 1)

            state(5)
            for f in range(FT):
                for n in range(2):
                    m = 2 * f + n
                    act.wait_ge(f_ps, m + 1)
                    act.activation(hT[:, f, n * 512:(n + 1) * 512], ps[:, 2 + m % 4, :], ACT.Relu,
                                   bias=vecT[:, V_FB1 + f:V_FB1 + f + 1]).then_inc(f_ready, 1)

        @block.vector
        def _(v):
            steps = [0]

            def step(ins):
                steps[0] += 1
                ins.then_inc(dve_step, 1)
                v.wait_ge(dve_step, steps[0])

            def norm(k):
                for n in range(PAIRS):
                    ins = v.bn_stats(stats[:, n, :], Y[:, n, :])
                step(ins)
                for n in range(PAIRS):
                    ins = v.bn_aggr(mv[:, n, :], stats[:, n, :])
                step(ins)
                v.tensor_scalar(ve[:, :], mv[:, :, 1], EPS, None, ALU.add).then_inc(ve_ready, 1)
                v.wait_ge(rstd_ready, k + 1)
                for n in range(PAIRS):
                    ins = v.tensor_scalar(X[:, n, :], Y[:, n, :], mv[:, n, 0:1], rstd[:, n:n + 1],
                                          ALU.subtract, ALU.mult)
                ins.then_inc(x_norm, 1)

            def heads8(a, w=128):
                return a.rearrange("p (t n) -> p t n", n=w)

            v.memset(X[:, :, :], 0.0).then_inc(x_pad, 1)
            v.memset(wv1[:, :, :], 0.0).then_inc(x_pad, 1)
            v.wait_ge(x_pad, 2)
            v.memset(wv1[C:C + 1, :, DH:DH + 1], 1.0).then_inc(x_pad, 1)
            v.memset(ct_1[C:C + 1, :, :].bitcast(F32), 1.0).then_inc(x_pad, 1)

            v.wait_ge(ret_in, 16 * 4)
            for src, dst in ((wret[:, 0, :], wret[:, 3, :]), (wret[:, 1, :], wrkr)):
                s2 = src.rearrange("p (i two) -> p i two", two=2)
                d2 = dst.rearrange("p (i two) -> p i two", two=2)
                v.tensor_scalar(d2[:, :, 0], s2[:, :, 1], -1.0, None, ALU.mult).then_inc(rot_ready, 1)
                v.tensor_copy(d2[:, :, 1], s2[:, :, 0]).then_inc(rot_ready, 1)

            def table(c):
                return kc[:, c:c + SLOT].unsqueeze(1).to_broadcast([128, B, SLOT])

            def rotary(dst, raw, rot, cos, sin, unit):
                v.wait_ge(ret_ps, unit + 1)
                for n, bank in enumerate(raw):
                    ins = v.tensor_tensor(dst[:, n * 512:(n + 1) * 512].rearrange("p (b q) -> p b q", q=SLOT),
                                          ps[:, bank, :].rearrange("p (b q) -> p b q", q=SLOT),
                                          table(cos)[:, 0:B // 2, :], ALU.mult)
                ins.then_inc(ret_read, 1)
                v.wait_ge(ret_ps, unit + 2)
                for n, bank in enumerate(rot):
                    ins = v.tensor_tensor(qT[:, n * 512:(n + 1) * 512].rearrange("p (b q) -> p b q", q=SLOT),
                                          ps[:, bank, :].rearrange("p (b q) -> p b q", q=SLOT),
                                          table(sin)[:, 0:B // 2, :], ALU.mult)
                step(ins)
                v.tensor_tensor(dst, dst, qT[:, :], ALU.add).then_inc(ret_read, 1)

            rotary(rq, (3, 4), (5, 6), K_COSQ, K_SINQ, 0)
            v.wait_ge(ret_read, 2)
            rotary(rk, (7, 0), (1, 2), K_COSK, K_SINK, 2)
            v.wait_ge(ret_ps, 6)
            v.tensor_tensor(heads8(rm), banks(5), kc[:, K_MASK:K_MASK + 128].unsqueeze(1).to_broadcast([128, PAIRS, 128]),
                            ALU.mult).then_inc(ret_read, 1)
            v.wait_ge(ret_ps, 7)
            step(v.tensor_tensor(Y[:, :, :], banks(3), X[:, :, :], ALU.add))
            norm(0)

            v.wait_ge(qbk_ps, 1)
            v.tensor_copy(sm[:, 0, :], ps[:, 6, 0:PAIRS]).then_inc(qbk_ready, 1)
            qbk0 = sm[:, 0, :]

            def split_lo(p, j, c):
                v.wait_ge(ct_hi, 6 * p + 3 * j + c + 1)
                lo = ct_all[64:128, 2 * p + j, c * CHUNK:(c + 1) * CHUNK]
                v.tensor_tensor(lo, ps[64:128, (3 * j + c) % 2, 0:CHUNK], lo.bitcast(F32), ALU.subtract)\
                    .then_inc(ct_ready, 1)

            def diag(st):
                return st[:, :, :].rearrange("p j n -> p (j n)").rearrange("p (a n) -> p a n", n=64)[:, 0:4:3, :]

            def stage_lo(p):
                v.wait_ge(sthi_ready, p + 1)
                v.tensor_tensor(diag(st_lo), qf0[:, bass.ts(p, 128)].rearrange("p (j n) -> p j n", j=2),
                                diag(st_hi).bitcast(F32), ALU.subtract).then_inc(stlo_ready, 1)

            def attend0(i):
                for h in range(2):
                    p = 2 * i + h
                    last = isinstance(i, int) and p == PAIRS - 1
                    v.wait_ge(s0_ps, p + 1)
                    wait_count(v, e0_ready, p)
                    v.tensor_reduce(sm[:, 4, 0:1], ps[:, 2:5, 0:CHUNK], AX.XY, ALU.max).then_inc(m0_step, 1)
                    v.wait_ge(m0_step, 2 * p + 1)
                    v.tensor_tensor(sm[:, 4, 1:2], sm[:, 4, 0:1], sm[:, 0, bass.ts(p, 1)], ALU.add).then_inc(m0_step, 1)
                    v.wait_ge(m0_step, 2 * p + 2)
                    v.tensor_tensor(sm[:, 1, 0:1], sm[:, 0, bass.ts(p, 1)], sm[:, 4, 1:2], ALU.subtract)\
                        .then_inc(shift0, 1)
                    if not last:
                        for j in range(2):
                            for c in range(NCH):
                                split_lo(p + 1, j, c)
                        stage_lo(p + 1)
                    wait_count(v, u0_ps, p)
                    v.wait_ge(e0t_ps, 3 * p + 2)
                    v.tensor_copy(e0T[:, TPC:2 * TPC, :].rearrange("p t n -> p (t n)"), ps[0:KT, 5 + (3 * h + 1) % 2, :])\
                        .then_inc(e0t_dve, 1)
                    v.wait_ge(u0_ps, p + 1)
                    v.tensor_copy(u0[:, bass.ts(p, 128)], ps[0:C + 1, 7, 0:128]).then_inc(u0_ready, 1)

            for j in range(2):
                for c in range(NCH):
                    split_lo(0, j, c)
            stage_lo(0)
            peeled(v, NB0, attend0)
            v.wait_ge(e0_ready, PAIRS)
            step(v.reciprocal(sm[:, 5, :], sm[:, 2, :]))
            for n in range(PAIRS):
                if n % 4 == 0:
                    v.wait_ge(o0_ps, n // 4 + 1)
                ins = v.scalar_tensor_tensor(out=Y[:, n, :], in0=banks(0)[:, n, :], scalar=sm[:, 5, n:n + 1],
                                             in1=X[:, n, :], op0=ALU.mult, op1=ALU.add)
            step(ins)
            norm(1)

            def first_bias(e, s):
                v.tensor_scalar(b1s[:, s, :], vecT[:, bass.ds(V_EB1 + FT * e, FT)], 1.0, None, ALU.mult)\
                    .then_inc(b1_ready, 1)

            v.wait_ge(vec_ready, 1)
            first_bias(0, 0)
            v.wait_ge(pool_set, 10)
            v.wait_ge(gate_ps, 1)
            step(v.tensor_copy(gate[:, :, 0:NE], ps[:, 4, 0:8 * PAIRS].rearrange("p (t n) -> p t n", n=8)[:, :, 0:NE]))
            for n in range(PAIRS):
                ins = v.max(top[:, n, :], gate[:, n, :])
            step(ins)
            v.tensor_tensor(sm[:, 3, :], top[:, :, 1], top[:, :, 0], ALU.subtract).then_inc(top_ready, 1)
            for n in range(PAIRS):
                ins = v.max_index(topi[:, n, :], top[:, n, :], gate[:, n, :])
            step(ins)
            step(v.tensor_copy(topf[:, :, :], topi[:, :, 0:2]))
            v.wait_ge(e2_ready, 1)
            step(v.tensor_scalar(sm[:, 6, :], sm[:, 3, :], 1.0, None, ALU.add))
            step(v.reciprocal(sm[:, 6, :], sm[:, 6, :]))
            step(v.tensor_tensor(sm[:, 7, :], sm[:, 3, :], sm[:, 6, :], ALU.mult))
            iota = kc[:, K_IOTA:K_IOTA + NE].unsqueeze(1).to_broadcast([128, PAIRS, NE])

            def spread(a):
                return a.unsqueeze(2).to_broadcast([128, PAIRS, NE])

            v.tensor_tensor(wexp[:, :, 0:NE], iota, spread(topf[:, :, 0]), ALU.is_equal)
            step(v.tensor_tensor(wtmp[:, :, :], iota, spread(topf[:, :, 1]), ALU.is_equal))
            v.tensor_tensor(wexp[:, :, 0:NE], wexp[:, :, 0:NE], spread(sm[:, 6, :]), ALU.mult)
            step(v.tensor_tensor(wtmp[:, :, :], wtmp[:, :, :], spread(sm[:, 7, :]), ALU.mult))
            v.tensor_tensor(wexp[:, :, 0:NE], wexp[:, :, 0:NE], wtmp[:, :, :], ALU.add).then_inc(wexp_ready, 1)
            v.wait_ge(wexp_ready, 1)
            v.wait_ge(wt_ps, 1)
            v.tensor_copy(wT[0:8, :].rearrange("p (b n) -> p b n", b=2), ps[0:8, 6:8, :]).then_inc(wt_ready, 1)
            v.wait_ge(b2_ps, 1)
            v.tensor_tensor(Y[:, :, :], banks(4), X[:, :, :], ALU.add).then_inc(y_init, 1)

            def experts(i):
                for s in range(2):
                    e = 2 * i + s
                    wait_count(v, eo_read, 2 * e)
                    first_bias(e + 1, 1 - s)
                    for n in range(PAIRS):
                        if n % 4 == 0:
                            v.wait_ge(eo_ps, 2 * e + n // 4 + 1)
                            if n == 0:
                                v.wait_ge(y_init, 1)
                            wait_count(v, eo_read, 2 * e - 1 + n // 4)
                        ins = v.scalar_tensor_tensor(out=Y[:, n, :], in0=banks(4 + 2 * s)[:, n, :],
                                                     scalar=wexp[:, n, bass.ts(e, 1)], in1=Y[:, n, :],
                                                     op0=ALU.mult, op1=ALU.add)
                        if n % 4 == 3:
                            ins.then_inc(eo_read, 1)

            experts(0)
            with v.Fori(1, NE // 2) as i:
                experts(i)
            v.wait_ge(eo_read, 2 * NE)
            norm(2)

            v.wait_ge(xt_ready, 8)
            v.tensor_scalar(lT, xT[:, :], vecT[:, V_WL:V_WL + 1], None, ALU.mult).then_inc(lr_ready, 1)
            v.tensor_scalar(rT, xT[:, :], vecT[:, V_WR:V_WR + 1], None, ALU.mult).then_inc(lr_ready, 1)
            v.wait_ge(sa_ps, 1)
            sa = ps[:, 2, 0:PAIRS * L].rearrange("p (t n) -> p t n", n=L)
            step(v.tensor_reduce(sm[:, 4, :], sa, AX.X, ALU.max))
            v.tensor_tensor(lT[:, 0:PAIRS * L].rearrange("p (t n) -> p t n", n=L), sa,
                            sm[:, 4, :].unsqueeze(2).to_broadcast([128, PAIRS, L]), ALU.subtract).then_inc(sa_sub, 2)
            v.wait_ge(sa_exp, 2)
            step(v.tensor_reduce(sm[:, 5, :], heads8(eb), AX.X, ALU.add))
            step(v.reciprocal(sm[:, 6, :], sm[:, 5, :]))
            v.wait_ge(sao_ps, 1)
            for n in range(PAIRS):
                ins = v.scalar_tensor_tensor(out=Y[:, n, :], in0=banks(5)[:, n, :], scalar=sm[:, 6, n:n + 1],
                                             in1=X[:, n, :], op0=ALU.mult, op1=ALU.add)
            step(ins)
            norm(3)

            v.tensor_scalar(bkh[:, :], kc[:, K_HEAD:K_HEAD + H], vecT[:, V_BK1:V_BK1 + 1], None, ALU.mult)\
                .then_inc(bkh_ready, 1)
            v.memset(cat, 0.0)
            v.wait_ge(x_norm, 4)
            v.tensor_tensor(Y[:, :, :], X[:, :, :], bo_b[:, :].unsqueeze(1).to_broadcast([128, PAIRS, 128]), ALU.add)\
                .then_inc(xb_ready, 1)
            v.wait_ge(q1_ready, 1)
            v.wait_ge(qbkT_ready, 2)

            def blocks(g, k, b):
                wait_count(v, qfold, g)
                hf = k % 2
                v.tensor_tensor(qbd.rearrange("p (h q) -> p h q", q=L),
                                qT[:, bass.ds(b * SLOT, L)].unsqueeze(1).to_broadcast([128, HH, L]),
                                kc[:, K_HEAD + hf * HH:K_HEAD + (hf + 1) * HH].unsqueeze(2).to_broadcast([128, HH, L]),
                                ALU.mult).then_inc(qbd_ready, 1)

            def low(g, k):
                v.wait_ge(qhi_ready, g + 1)
                v.tensor_tensor(q_lo[0:C, k, :], ps[0:C, 7, 0:QC], q_hi[0:C, k, :].bitcast(F32), ALU.subtract)\
                    .then_inc(qlo_ready, 1)

            def unit_max(g, u):
                r, c = divmod(u, NCH)
                v.wait_ge(mx_ps, 12 * g + u + 1)
                v.tensor_reduce(tmx[:, r, c:c + 1], ps[0:RR, 5 + u % 2, 0:CHUNK], AX.X, ALU.max).then_inc(mx_read, 1)

            def row_max(g):
                v.wait_ge(mx_read, 12 * g + 12)
                v.tensor_reduce(tm[:, :], tmx[:, :, :], AX.X, ALU.max).then_inc(tm_ready, 1)

            def shift(g, k, loads):
                v.wait_ge(qrow_in[k % 2], loads)
                v.wait_ge(tm_row, g + 1)
                v.tensor_tensor(mrow, ps[C:C + 1, 7, 0:QC], qrow[k % 2], ALU.add).then_inc(m_ready, 1)
                v.wait_ge(m_ready, g + 1)
                v.tensor_tensor(q_lo[C:C + 1, k, :], qrow[k % 2], mrow, ALU.subtract).then_inc(aux_ready, 1)

            def heads_out(g, k):
                v.wait_ge(oh_ps, g + 1)
                o = ps[0:L, 7, 0:HH * (DH + 1)].rearrange("p (h d) -> p h d", d=DH + 1)
                v.reciprocal(rec, o[:, :, DH]).then_inc(rec_ready, 1)
                v.wait_ge(rec_ready, g + 1)
                hf = k % 2
                v.tensor_tensor(cat[0:L, hf * 64:(hf + 1) * 64].rearrange("p (h d) -> p h d", d=DH), o[:, :, 0:DH],
                                rec.unsqueeze(2).to_broadcast([L, HH, DH]), ALU.mult).then_inc(cat_ready, 1)

            def output(b, n, j):
                v.wait_ge(wo_ps, b + 1)
                y = Y[64 * j:64 * j + L, bass.ts(n, 1), :].rearrange("p o n -> p (o n)")
                v.tensor_tensor(y, ps[64 * j:64 * j + L, 7, 0:128], y, ALU.add).then_inc(y1_ready, 1)

            def attend1(i):
                for k in range(4):
                    g = 4 * i + k
                    flat = isinstance(i, int)
                    before, after, after2 = (not flat or g > 0), (not flat or g < 2 * B - 1), (not flat or g < 2 * B - 2)
                    b2 = 2 * i + (k + 2) // 2
                    for u in range(6):
                        if after:
                            unit_max(g + 1, 2 * u)
                            unit_max(g + 1, 2 * u + 1)
                        if u == 1 and before:
                            heads_out(g - 1, k - 1)
                    if before and k % 2 == 0:
                        output(2 * i + k // 2 - 1, i - 1 + k // 2, (k // 2 + 1) % 2)
                    if after:
                        row_max(g + 1)
                    if after2:
                        blocks(g + 2, k, b2)
                    if after:
                        shift(g + 1, (k + 1) % 4, 16 * (2 * i + (k + 1) // 2 + 1))
                    if after2:
                        low(g + 2, (k + 2) % 4)

            blocks(0, 0, 0)
            low(0, 0)
            blocks(1, 1, 0)
            low(1, 1)
            for u in range(NT):
                unit_max(0, u)
            row_max(0)
            shift(0, 0, 16)
            v.wait_ge(xb_ready, 1)
            peeled(v, NB1, attend1)
            heads_out(2 * B - 1, 3)
            output(B - 1, PAIRS - 1, 1)
            v.wait_ge(y1_ready, B)
            norm(4)

            v.wait_ge(x_norm, 5)
            step(v.tensor_tensor(Y[:, :, :], X[:, :, :], fb2_b[:, :].unsqueeze(1).to_broadcast([128, PAIRS, 128]), ALU.add))
            for n in range(2):
                v.wait_ge(fo_ps, n + 1)
                ins = v.tensor_tensor(Y[:, 4 * n:4 * n + 4, :], banks(6)[:, 4 * n:4 * n + 4, :], Y[:, 4 * n:4 * n + 4, :],
                                      ALU.add)
            step(ins)
            norm(5)


def _constants():
    f = np.float32
    half = D // 2
    scale_vec = (np.arange(0, D, 2, dtype=f) + f(0.4 * D)) / f(1.4 * D)
    pos = np.arange(L, dtype=f)
    scale = scale_vec[None, :] ** (pos[:, None] / f(512.0))
    inv_freq = f(1.0) / f(10000.0) ** (np.arange(half, dtype=f) / f(half))
    sinusoid = pos[:, None] * inv_freq[None, :]
    k = np.zeros((128, NCONST), f)
    for col, fn, sc in ((K_COSQ, np.cos, scale), (K_SINQ, np.sin, scale),
                        (K_COSK, np.cos, f(1.0) / scale), (K_SINK, np.sin, f(1.0) / scale)):
        k[:, col:col + L] = np.repeat(fn(sinusoid) * sc, 2, axis=-1).T
    n = np.arange(L)
    diff = n[None, :] - n[:, None]
    decay = np.where(diff >= 0, f(0.96875) ** np.maximum(diff, 0).astype(f), f(0.0))
    for j in range(2):
        k[SLOT * j:SLOT * j + L, K_MASK + SLOT * j:K_MASK + SLOT * j + L] = decay
    k[np.arange(128), K_HEAD + np.arange(128) // DH] = f(1.0 / np.sqrt(DH))
    k[:, K_IOTA:K_IOTA + NE] = np.arange(NE)
    return k


_INS = ["x", "ctx_512", "L0_attn_W_Q", "L0_attn_W_K", "L0_attn_W_V", "L0_xattn_Wq", "L0_xattn_bq", "L0_xattn_Wk",
        "L0_xattn_bk", "L0_xattn_Wv", "L0_xattn_bv", "L0_ffn_Wg", "L0_ffn_bg", "L0_ffn_W1", "L0_ffn_b1", "L0_ffn_W2",
        "L0_ffn_b2", "L1_attn_w_lhs", "L1_attn_w_rhs", "L1_xattn_Wq", "L1_xattn_bq", "L1_xattn_Wk", "L1_xattn_bk",
        "L1_xattn_Wv", "L1_xattn_bv", "L1_xattn_Wo", "L1_xattn_bo", "L1_ffn_W1", "L1_ffn_b1", "L1_ffn_W2", "L1_ffn_b2"]


def kernel(**inputs):
    import concourse.bacc as _bacc
    from concourse.bass_utils import run_bass_kernel_spmd as _run

    nc = _bacc.Bacc("TRN2", target_bir_lowering=False, num_devices=1)
    arrays, aps = {}, {}
    for name in _INS:
        a = np.ascontiguousarray(inputs[name])
        arrays[f"in_{name}"] = a
        aps[name] = nc.dram_tensor(f"in_{name}", a.shape, mybir.dt.from_np(a.dtype), kind="ExternalInput").ap()
    arrays["in_constants"] = _constants()
    consts = nc.dram_tensor("in_constants", (128, NCONST), F32, kind="ExternalInput").ap()
    out = nc.dram_tensor("out_0", (B, L, D), F32, kind="ExternalOutput").ap()
    decoder(nc, aps, consts, out)
    r = _run(nc, [arrays], core_ids=[0])
    return r.results[0]["out_0"]
```

```python
from contextlib import ExitStack

import numpy as np

import concourse.bass as bass
from concourse import mybir
from concourse.alu_op_type import AluOpType as ALU

ACT = mybir.ActivationFunctionType
AX = mybir.AxisListType
F32 = mybir.dt.float32
F32R = mybir.dt.float32r
U32 = mybir.dt.uint32

B, L, D = 16, 56, 128
S, C = 1500, 64
SLOT = 64
PAIRS = B // 2
TOK = B * SLOT
KT, NT = 125, 12
CHUNK, NCH = 500, 3
TPC = CHUNK // KT
NCN = 6
NE, F = 6, 512
FT = F // 128
H, DH = 16, 8
HH = H // 2
QC = HH * L
HG, NG = 4, 4
GW, GC = HG * DH, HG * L
VROWS = 2 * GW + 1
RT = 4
RR = QC // RT
AHEAD = 5
LEAD = NCH + RT * NCH + AHEAD
EPS = 1e-5
NEG = -3.0e38

V_BQ0, V_BK0, V_BQ1, V_BK1, V_WL, V_WR, V_FB1, V_EB1 = 0, 1, 2, 3, 4, 5, 6, 10
NVEC = V_EB1 + NE * FT
K_COSQ, K_SINQ, K_COSK, K_SINK, K_MASK, K_HEAD, K_IOTA = 0, 64, 128, 192, 256, 384, 400
NCONST = K_IOTA + NE
K_SEL = NCONST
NALL = K_SEL + H * (DH + 1)


def wait_count(eng, sem, value):
    if isinstance(value, int) and value <= 0:
        return
    eng.wait_ge(sem, value)


def unit_base(i, k):
    return LEAD + 54 * i + (0, 12, 27, 39)[k]


def unit_at(k, u, value=False):
    values_before = min(u // 2, NCH) if k % 2 else 0
    return u + values_before + value


def unit_bank(k, m):
    return 5 + (unit_base(0, k) + m) % 2


def peeled(eng, n, body):
    body(0)
    with eng.Fori(1, n - 1) as i:
        body(i)
    body(n - 1)


def pairs_loop(eng, body):
    body(0, 0)
    with eng.Fori(0, (PAIRS - 2) // 3) as i:
        for h in range(3):
            body(3 * i + 1 + h, (1 + h) % 3)
    body(PAIRS - 1, (PAIRS - 1) % 3)


def decoder(nc: bass.Bass, t, consts, out):
    with ExitStack() as ctx:
        def sb(name, shape, dt=F32):
            return ctx.enter_context(nc.sbuf_tensor(name, shape, dt))

        def sem(name):
            return ctx.enter_context(nc.semaphore(name))

        ct_all = sb("ct_all", [128, B, S], F32R)
        X = sb("X", [128, PAIRS, 128])
        Y = sb("Y", [128, PAIRS, 128])
        qT = sb("qT", [128, TOK])
        kc = sb("kc", [128, NCONST])
        ident = sb("ident", [128, 128])
        wq1 = sb("wq1", [128, 128])
        wkT1 = sb("wkT1", [128, 128])
        wv_raw = sb("wv_raw", [128, 128])
        wv_hi = sb("wv_hi", [128, 128], F32R)
        wv_lo = sb("wv_lo", [C, 128], F32R)
        sel1 = sb("sel1", [C + 1, H, DH + 1])
        fw1 = sb("fw1", [128, F])
        fw2 = sb("fw2", [128, F])
        wo = sb("wo", [128, 128])
        bo_b = sb("bo_b", [128, 128])
        fb2_b = sb("fb2_b", [128, 128])
        bg_b = sb("bg_b", [128, NE])
        ones = sb("ones", [128, 128])
        vecT = sb("vecT", [128, NVEC + FT])
        b1s = sb("b1s", [128, 2, FT])
        bkh = sb("bkh", [128, H])
        stats = sb("stats", [128, PAIRS, 6])
        mv = sb("mv", [128, PAIRS, 2])
        ve = sb("ve", [128, PAIRS])
        rstd = sb("rstd", [128, PAIRS])
        mhalf = sb("mhalf", [128, PAIRS])
        sm = sb("sm", [128, 8, PAIRS])
        esum = sb("esum", [128, NCH, PAIRS])
        tmx = sb("tmx", [RR, 2, RT, NCH])
        tm = sb("tm", [RR, RT])
        ps = ctx.enter_context(nc.psum_tensor("ps", [128, 8, 512], F32))

        def lifetime(*tensors):
            with ExitStack() as scope:
                return [scope.enter_context(nc.sbuf_tensor(name, shape, dt)) for name, shape, dt in tensors]

        cn, arena, w1b, w2b, xT, st_hi, st_lo, wq0, wkT0, wv0, wg, eb2, gate, top, topi, topf, wexp, wtmp = lifetime(
            ("cn", [KT, NCN, NT * 129], F32),
            ("arena", [128, 4096], F32),
            ("w1b", [128, 2, F], F32),
            ("w2b", [128, 2, F], F32),
            ("xT", [128, TOK], F32),
            ("st_hi", [128, 2, 128], F32R),
            ("st_lo", [128, 2, 128], F32R),
            ("wq0", [128, 128], F32),
            ("wkT0", [128, 128], F32),
            ("wv0", [C + 1, 128], F32),
            ("wg", [128, NE], F32),
            ("eb2", [NE, 128], F32),
            ("gate", [128, PAIRS, 8], F32),
            ("top", [128, PAIRS, 8], F32),
            ("topi", [128, PAIRS, 8], U32),
            ("topf", [128, PAIRS, 2], F32),
            ("wexp", [128, PAIRS, 8], F32),
            ("wtmp", [128, PAIRS, NE], F32))
        vg, e1, e1_hi, e1_lo, qrow, u1, qbd, cat, catT, q_hi, q_lo, ct_w, ct_1 = lifetime(
            ("vg", [KT, 2, NT, NG, VROWS], F32R),
            ("e1", [KT, 3, QC], F32),
            ("e1_hi", [KT, 3, QC], F32R),
            ("e1_lo", [KT, 3, QC], F32R),
            ("qrow", [C + 1, 3, QC], F32),
            ("u1", [C + 1, 2, QC], F32),
            ("qbd", [128, QC], F32),
            ("cat", [128, 128], F32),
            ("catT", [128, L], F32),
            ("q_hi", [128, 4, QC], F32R),
            ("q_lo", [C + 1, 4, QC], F32R),
            ("ct_w", [128, 2, S], F32R),
            ("ct_1", [C + 1, 2, S], F32R))
        xT5, hT5 = lifetime(("xT5", [128, TOK], F32), ("hT5", [128, FT, TOK], F32))
        qbk_dram = nc.dram_tensor("qbk_dram", (B, H, L), F32, kind="Internal").ap()

        ar4 = arena[:, :].rearrange("p (n c) -> p n c", n=4)
        rq, rk, rv, rm = (ar4[:, n, :] for n in range(4))
        e0 = arena[:, 0:S]
        e0T = arena[0:KT, S:S + NT * 128].rearrange("p (t n) -> p t n", n=128)
        qf0 = arena[:, S + NT * 128:S + NT * 128 + TOK]
        hT = ar4
        lT, rT, eb, ebT = (ar4[:, n, :] for n in range(4))
        rec = qrow[0:L, 2, 0:HH]
        qbkT = arena[0:H, TOK:2 * TOK]
        u0 = w1b[0:C + 1, :, :].rearrange("p a b -> p (a b)")
        qbk_row = [qrow[C:C + 1, n, :] for n in range(2)]
        mrow = qrow[C:C + 1, 2, :]
        wret = w1b[:, 1, :].rearrange("p (n c) -> p n c", n=4)
        wrkr = w2b[:, 1, 0:128]
        wT = qT
        wk_raw = [Y[0:C, n, :] for n in range(2)]
        vrows = Y[0:NVEC, 2, :]

        def cn_tile(s, k, lo, hi):
            return cn[:, s, k * 129 + lo:k * 129 + hi]

        def cn_cols(s, lo, hi):
            return cn[:, s, :].rearrange("p (t n) -> p t n", n=129)[:, :, lo:hi]

        def ctx_rows(b):
            return t["ctx_512"][b].rearrange("(p t) d -> p t d", t=NT)

        def banks(b, w=512):
            return ps[:, b:b + 2, :].rearrange("p b (t n) -> p (b t) n", n=128)

        x_in = sem("x_in")
        ret_in = sem("ret_in")
        vec_in = sem("vec_in")
        w0_in = sem("w0_in")
        w1_in = sem("w1_in")
        moe_in = sem("moe_in")
        ctx_in = [sem(f"ctx_in{s}") for s in range(NCN)]
        exp_in = [sem(f"exp_in{s}") for s in range(2)]
        ffn_in = sem("ffn_in")
        ct_in = [sem(f"ct_in{s}") for s in range(2)]
        qrow_in = [sem(f"qrow_in{s}") for s in range(2)]
        qbk_out = sem("qbk_out")
        out_done = sem("out_done")
        pool_set = sem("pool_set")
        x_pad = sem("x_pad")
        xt_ps = sem("xt_ps")
        xt_ready = sem("xt_ready")
        vec_ps = sem("vec_ps")
        vec_ready = sem("vec_ready")
        dve_step = sem("dve_step")
        ve_ready = sem("ve_ready")
        rstd_ready = sem("rstd_ready")
        x_norm = sem("x_norm")
        rot_ready = sem("rot_ready")
        ret_ps = sem("ret_ps")
        ret_read = sem("ret_read")
        rv_ready = sem("rv_ready")
        q_ps = sem("q_ps")
        q_ready = sem("q_ready")
        qf_ps = sem("qf_ps")
        qf_ready = sem("qf_ready")
        qbk_ps = sem("qbk_ps")
        qbk_ready = sem("qbk_ready")
        dup_ready = sem("dup_ready")
        t_ps = sem("t_ps")
        ct_hi = sem("ct_hi")
        ct_ready = sem("ct_ready")
        sthi_ready = sem("sthi_ready")
        stlo_ready = sem("stlo_ready")
        s0_ps = sem("s0_ps")
        m0_step = sem("m0_step")
        shift0 = sem("shift0")
        e0_ready = sem("e0_ready")
        e0t_ps = sem("e0t_ps")
        e0t_act = sem("e0t_act")
        e0t_dve = sem("e0t_dve")
        u0_ps = sem("u0_ps")
        u0_ready = sem("u0_ready")
        o0_ps = sem("o0_ps")
        gate_ps = sem("gate_ps")
        top_ready = sem("top_ready")
        e2_ready = sem("e2_ready")
        b1_ready = sem("b1_ready")
        wexp_ready = sem("wexp_ready")
        wt_ps = sem("wt_ps")
        wt_ready = sem("wt_ready")
        b2_ps = sem("b2_ps")
        y_init = sem("y_init")
        h_ps = sem("h_ps")
        h_ready = sem("h_ready")
        eo_ps = sem("eo_ps")
        eo_read = sem("eo_read")
        lr_ready = sem("lr_ready")
        sa_ps = sem("sa_ps")
        sa_sub = sem("sa_sub")
        eb_zero = sem("eb_zero")
        sa_exp = sem("sa_exp")
        ebt_ps = sem("ebt_ps")
        ebt_ready = sem("ebt_ready")
        sao_ps = sem("sao_ps")
        bkh_ready = sem("bkh_ready")
        q1_ps = sem("q1_ps")
        q1_ready = sem("q1_ready")
        qbkT_ps = sem("qbkT_ps")
        qbkT_ready = sem("qbkT_ready")
        qbd_ready = sem("qbd_ready")
        qfold = sem("qfold")
        qhi_ready = sem("qhi_ready")
        qlo_ready = sem("qlo_ready")
        mx_ps = sem("mx_ps")
        mx_read = sem("mx_read")
        tm_ready = sem("tm_ready")
        tm_row = sem("tm_row")
        m_ready = sem("m_ready")
        aux_ready = sem("aux_ready")
        st_ps = sem("st_ps")
        e1_ready = sem("e1_ready")
        elo_ready = sem("elo_ready")
        wv_split = sem("wv_split")
        vhi_ready = sem("vhi_ready")
        pv_done = sem("pv_done")
        u1_ready = sem("u1_ready")
        oh_ps = sem("oh_ps")
        rec_ready = sem("rec_ready")
        cat_ready = sem("cat_ready")
        catT_ps = sem("catT_ps")
        catT_ready = sem("catT_ready")
        wo_ps = sem("wo_ps")
        y1_ready = sem("y1_ready")
        xb_ready = sem("xb_ready")
        f_ps = sem("f_ps")
        f_ready = sem("f_ready")
        fo_ps = sem("fo_ps")

        NB1 = B // 2

        block = ctx.enter_context(nc.Block())

        @block.sync
        def _(sp):
            def load(dst, src, s):
                sp.dma_start(dst, src).then_inc(s, 16)

            sp.wait_ge(x_pad, 1)
            xs = t["x"].rearrange("(r two) l d -> two l r d", two=2)
            load(X[0:L, :, :], xs[0], x_in)
            load(X[SLOT:SLOT + L, :, :], xs[1], x_in)
            load(wret[:, 0, :], t["L0_attn_W_Q"], ret_in)
            load(wret[:, 1, :], t["L0_attn_W_K"], ret_in)
            load(wret[:, 2, :], t["L0_attn_W_V"], ret_in)
            load(kc[:, :], consts[:, 0:NCONST], ret_in)
            for b in range(NCN):
                load(cn_cols(b, 64, 128), ctx_rows(b), ctx_in[b])
            rows = [("L0_xattn_bq", V_BQ0), ("L0_xattn_bk", V_BK0), ("L1_xattn_bq", V_BQ1), ("L1_xattn_bk", V_BK1)]
            for name, r in rows:
                load(vrows[r:r + 1, :], t[name].rearrange("(o n) -> o n", o=1), vec_in)
            load(vrows[V_WL:V_WL + 1, :], t["L1_attn_w_lhs"].rearrange("a b n -> (a b) n"), vec_in)
            load(vrows[V_WR:V_WR + 1, :], t["L1_attn_w_rhs"].rearrange("a b n -> (a b) n"), vec_in)
            load(vrows[V_FB1:V_FB1 + FT, :], t["L1_ffn_b1"].rearrange("(f n) -> f n", n=128), vec_in)
            load(vrows[V_EB1:NVEC, :], t["L0_ffn_b1"].rearrange("e (f n) -> (e f) n", n=128), vec_in)
            load(wk_raw[0], t["L0_xattn_Wk"], vec_in)
            load(wk_raw[1], t["L1_xattn_Wk"], vec_in)
            load(wq0[:, :], t["L0_xattn_Wq"], w0_in)
            load(wv0[0:C, :], t["L0_xattn_Wv"], w0_in)
            load(wv0[C:C + 1, :], t["L0_xattn_bv"].rearrange("(o n) -> o n", o=1), w0_in)
            load(wg[:, :], t["L0_ffn_Wg"], moe_in)
            load(bg_b[:, :], t["L0_ffn_bg"].rearrange("(o n) -> o n", o=1).to_broadcast([128, NE]), moe_in)
            load(eb2[:, :], t["L0_ffn_b2"], moe_in)
            load(wq1[:, :], t["L1_xattn_Wq"], w1_in)
            load(wo[:, :], t["L1_xattn_Wo"], w1_in)
            load(wv_raw[0:C, :], t["L1_xattn_Wv"], w1_in)
            load(wv_raw[C:2 * C, :], t["L1_xattn_Wv"], w1_in)
            load(sel1[0:C, :, :], consts[0:C, K_SEL:NALL].rearrange("c (h d) -> c h d", d=DH + 1), w1_in)
            load(sel1[C:C + 1, :, 0:DH], t["L1_xattn_bv"].rearrange("(o h d) -> o h d", o=1, d=DH), w1_in)
            load(fw1[:, :], t["L1_ffn_W1"], ffn_in)
            load(fw2[:, :].rearrange("p (f n) -> p f n", n=128), t["L1_ffn_W2"].rearrange("(f p) n -> p f n", p=128),
                 ffn_in)
            load(bo_b[:, :], t["L1_xattn_bo"].rearrange("(o n) -> o n", o=1).to_broadcast([128, 128]), w1_in)
            load(fb2_b[:, :], t["L1_ffn_b2"].rearrange("(o n) -> o n", o=1).to_broadcast([128, 128]), w1_in)

            for b in range(NCN, B):
                sp.wait_ge(u0_ps, (b - NCN) // 2 + 1)
                load(cn_cols(b % NCN, 64, 128), ctx_rows(b), ctx_in[b % NCN])

            def experts(i):
                for s in range(2):
                    if isinstance(i, int):
                        sp.wait_ge(o0_ps, 2)
                    else:
                        sp.wait_ge(eo_ps, 4 * i - 2 + 2 * s)
                    load(w1b[:, s, :], t["L0_ffn_W1"][2 * i + s], exp_in[s])
                    load(w2b[:, s, :].rearrange("p (f n) -> p f n", n=128),
                         t["L0_ffn_W2"][2 * i + s].rearrange("(f p) n -> p f n", p=128), exp_in[s])
            experts(0)
            with sp.Fori(1, NE // 2) as i:
                experts(i)

            sp.wait_ge(qbkT_ready, 2)
            sp.dma_start(qbk_dram.rearrange("b h q -> h b q"),
                         qbkT.rearrange("h (b q) -> h b q", q=SLOT)[:, :, 0:L]).then_inc(qbk_out, 16)
            sp.wait_ge(qbk_out, 16)

            def context(i):
                for s in range(2):
                    wait_count(sp, pv_done, 48 * i + 24 * s - 24)
                    b = 2 * i + s
                    load(ct_w[:, s, :].bitcast(F32), ct_all[:, b, :].bitcast(F32), ct_in[s])
                    load(ct_1[0:C, s, :].bitcast(F32), ct_all[0:C, b, :].bitcast(F32), ct_in[s])
                    for hf in range(2):
                        wait_count(sp, aux_ready, 4 * i + 2 * s + hf - 1)
                        load(qbk_row[hf].rearrange("o (h q) -> o h q", q=L), qbk_dram[bass.ts(b, 1), hf * HH:(hf + 1) * HH, :],
                             qrow_in[hf])
            context(0)
            with sp.Fori(1, NB1) as i:
                context(i)

            sp.wait_ge(x_norm, 12)
            os = out.rearrange("(r two) l d -> two l r d", two=2)
            load(os[0], X[0:L, :, :], out_done)
            load(os[1], X[SLOT:SLOT + L, :, :], out_done)
            sp.wait_ge(out_done, 32)

        @block.gpsimd
        def _(g):
            g.memset(ident[:, :], 0.0).then_inc(pool_set, 1)
            g.memset(ones[:, :], 1.0).then_inc(pool_set, 1)
            g.memset(mhalf[:, :], -0.5).then_inc(pool_set, 1)
            g.memset(cn[:, :, :].rearrange("p s (t n) -> p (s t) n", n=129)[:, :, 128:129], 1.0).then_inc(pool_set, 1)
            g.wait_ge(pool_set, 4)
            g.affine_select(out=ident[:, :], in_=ident[:, :], compare_op=ALU.not_equal, fill=1.0, base=0,
                            pattern=[[-1, 128]], channel_multiplier=1).then_inc(pool_set, 1)
            g.memset(st_hi[:, :, :].bitcast(F32), 0.0).then_inc(pool_set, 1)
            g.memset(st_lo[:, :, :].bitcast(F32), 0.0).then_inc(pool_set, 1)
            g.memset(gate[:, :, :], NEG).then_inc(pool_set, 1)
            g.memset(wexp[:, :, :], 0.0).then_inc(pool_set, 1)
            g.memset(vecT[:, NVEC:NVEC + FT], 0.0).then_inc(pool_set, 1)

            def power(k):
                for n in range(2):
                    g.wait_ge(ve_ready, 2 * k + n + 1)
                    g.tensor_tensor(rstd[:, 4 * n:4 * n + 4], ve[:, 4 * n:4 * n + 4], mhalf[:, 0:4], ALU.pow)\
                        .then_inc(rstd_ready, 1)

            def double(b):
                one = ones[0:KT, 0:1].unsqueeze(1).to_broadcast([KT, NT, 64])
                g.wait_ge(ctx_in[b % NCN], 16 * (b // NCN) + 16)
                g.tensor_tensor(cn_cols(b % NCN, 0, 64), cn_cols(b % NCN, 64, 128), one, ALU.mult).then_inc(dup_ready, 1)

            for b in range(NCN):
                if b == 2:
                    power(0)
                double(b)
            for b in range(NCN, B):
                double(b)
            power(1)
            power(2)
            g.wait_ge(lr_ready, 2)
            g.memset(eb, 0.0).then_inc(eb_zero, 1)
            power(3)

            def low_exp(i):
                for k in range(4):
                    for u in range(NT):
                        n = 48 * i + 12 * k + u
                        g.wait_ge(e1_ready, n + 1)
                        wait_count(g, pv_done, n - 2)
                        g.tensor_tensor(e1_lo[:, u % 3, :], e1[:, u % 3, :], e1_hi[:, u % 3, :].bitcast(F32),
                                        ALU.subtract).then_inc(elo_ready, 1)

            peeled(g, NB1, low_exp)
            power(4)
            power(5)

        @block.tensor
        def _(pe):
            mm = nc.tensor.matmul

            def transpose_state(k):
                for n in range(PAIRS):
                    if n % 4 == 0:
                        wait_count(pe, x_norm, 2 * k - 1 + n // 4 if k else 0)
                    ins = pe.transpose(ps[:, n // 4, (n % 4) * 128:(n % 4 + 1) * 128], X[:, n, :], ident[:, :])
                    if n % 4 == 3:
                        ins.then_inc(xt_ps, 1)

            def wide(bank, w, x, m=128, state=None):
                for n in range(2):
                    if state is not None:
                        pe.wait_ge(xt_ready, 2 * state + n + 1)
                    ins = pe.matmul(ps[0:m, bank + n, :], w, x[:, n * 512:(n + 1) * 512], start=True, stop=True)
                return ins

            pe.wait_ge(pool_set, 5)
            pe.wait_ge(x_in, 32)
            transpose_state(0)

            pe.wait_ge(xt_ready, 2)
            pe.wait_ge(ret_in, 16 * 4)
            wide(3, wret[:, 0, :], xT).then_inc(ret_ps, 1)
            pe.wait_ge(rot_ready, 2)
            wide(5, wret[:, 3, :], xT).then_inc(ret_ps, 1)
            for n, bank in ((0, 7), (1, 0)):
                ins = pe.matmul(ps[:, bank, :], wret[:, 1, :], xT[:, n * 512:(n + 1) * 512], start=True, stop=True)
            ins.then_inc(ret_ps, 1)
            pe.wait_ge(rot_ready, 4)
            pe.wait_ge(ret_read, 1)
            wide(1, wrkr, xT).then_inc(ret_ps, 1)
            for n in range(PAIRS):
                ins = pe.matmul(banks(3)[:, n, :], xT[:, n * 128:(n + 1) * 128], wret[:, 2, :], start=True, stop=True)
            ins.then_inc(ret_ps, 1)
            pe.wait_ge(vec_in, 16 * 10)
            pe.wait_ge(ret_read, 3)
            pe.transpose(ps[:, 7, 0:NVEC], vrows, ident[0:NVEC, 0:NVEC])
            pe.transpose(ps[:, 7, 64:128], wk_raw[0], ident[0:C, 0:C])
            pe.transpose(ps[:, 7, 128:192], wk_raw[1], ident[0:C, 0:C]).then_inc(vec_ps, 1)
            pe.wait_ge(ret_read, 4)
            for n in range(PAIRS):
                ins = pe.matmul(banks(5)[:, n, :], rk[:, n * 128:(n + 1) * 128], rq[:, n * 128:(n + 1) * 128],
                                start=True, stop=True)
            ins.then_inc(ret_ps, 1)
            pe.wait_ge(ret_read, 5)
            pe.wait_ge(rv_ready, 1)
            for n in range(PAIRS):
                ins = pe.matmul(banks(3)[:, n, :], rm[:, n * 128:(n + 1) * 128], rv[:, n * 128:(n + 1) * 128],
                                start=True, stop=True)
                if n % 4 == 3:
                    ins.then_inc(ret_ps, 1)

            transpose_state(1)
            pe.wait_ge(w0_in, 16 * 3)
            wide(2, wq0[:, :], xT, state=1).then_inc(q_ps, 1)
            pe.wait_ge(q_ready, 1)
            wide(4, wkT0[:, :], qT).then_inc(qf_ps, 1)
            for n in range(PAIRS):
                ins = pe.matmul(ps[:, 6, n:n + 1], qT[:, n * 128:(n + 1) * 128], vecT[:, V_BK0:V_BK0 + 1],
                                start=True, stop=True)
            ins.then_inc(qbk_ps, 1)

            def turn_context(p, h, m):
                j, c = divmod(m, NCH)
                if c == 0:
                    pe.wait_ge(dup_ready, 2 * p + j + 1)
                wait_count(pe, ct_ready, 6 * p + m - 1)
                for k in range(TPC):
                    ins = pe.transpose(ps[:, m % 2, k * KT:(k + 1) * KT],
                                       cn_tile(2 * h + j, c * TPC + k, 0, 128), ident[0:KT, 0:KT])
                ins.then_inc(t_ps, 1)

            def turn_exp(p, c):
                pe.wait_ge(e0_ready, 3 * p + c + 1)
                if c == 1:
                    wait_count(pe, e0t_act, p)
                else:
                    wait_count(pe, e0t_dve, 2 * p + c // 2)
                for k in range(TPC):
                    ins = pe.transpose(ps[0:KT, 5 + c % 2, k * 128:(k + 1) * 128],
                                       e0[:, (c * TPC + k) * KT:(c * TPC + k + 1) * KT], ident[:, :])
                ins.then_inc(e0t_ps, 1)

            def attend0(p, h):
                h1 = (h + 1) % 3
                last = isinstance(p, int) and p == PAIRS - 1
                pe.wait_ge(stlo_ready, p + 1)
                pe.wait_ge(ct_ready, 6 * p + 6)
                for c in range(NCH):
                    wait_count(pe, e0_ready, 3 * p - 2 + c)
                    for n, (j, q) in enumerate(((0, st_hi), (0, st_lo), (1, st_hi), (1, st_lo))):
                        ins = pe.matmul(ps[:, 2 + c, 0:CHUNK], q[:, j, :],
                                        ct_all[:, 2 * p + j, c * CHUNK:(c + 1) * CHUNK],
                                        start=(n == 0), stop=(n == 3))
                    ins.then_inc(s0_ps, 1)
                for m in range(2 * NCH):
                    if not last:
                        turn_context(p + 1, h1, m)
                    if 1 <= m < 1 + NCH:
                        turn_exp(p, m - 1)
                pe.wait_ge(e0t_act, p + 1)
                pe.wait_ge(e0t_dve, 2 * p + 2)
                wait_count(pe, u0_ready, p)
                for j in range(2):
                    for k in range(NT):
                        ins = pe.matmul(ps[0:C + 1, 7, j * 64:(j + 1) * 64], cn_tile(2 * h + j, k, 64, 129),
                                        e0T[:, k, j * 64:(j + 1) * 64], start=(k == 0), stop=(k == NT - 1))
                ins.then_inc(u0_ps, 1)

            for m in range(2 * NCH):
                turn_context(0, 0, m)
            pe.wait_ge(qbk_ready, 1)
            pairs_loop(pe, attend0)
            pe.wait_ge(u0_ready, PAIRS)
            for n in range(PAIRS):
                ins = pe.matmul(banks(0)[:, n, :], u0[:, n * 128:(n + 1) * 128], wv0[:, :], start=True, stop=True)
                if n % 4 == 3:
                    ins.then_inc(o0_ps, 1)

            transpose_state(2)
            pe.wait_ge(moe_in, 16 * 3)
            for n in range(PAIRS):
                if n % 4 == 0:
                    pe.wait_ge(xt_ready, 5 + n // 4)
                ins = pe.matmul(ps[:, 4, n * 8:n * 8 + NE], xT[:, n * 128:(n + 1) * 128], wg[:, :], start=True,
                                stop=True)
            ins.then_inc(gate_ps, 1)

            def hidden(e, s):
                pe.wait_ge(exp_in[s], 16 * (e - s) + 32)
                for f in range(FT):
                    for n in range(2):
                        m = 8 * e + 2 * f + n
                        wait_count(pe, h_ready, m - 3)
                        pe.matmul(ps[:, (2 * f + n) % 4, :], w1b[:, s, f * 128:(f + 1) * 128],
                                  xT[:, n * 512:(n + 1) * 512], start=True, stop=True).then_inc(h_ps, 1)
                    if isinstance(e, int) and e == 0:
                        second_biases(f)

            def second_biases(f):
                if f == 2:
                    pe.wait_ge(wexp_ready, 1)
                    for n in range(PAIRS):
                        ins = pe.transpose(ps[0:8, 6 + n // 4, (n % 4) * 128:(n % 4 + 1) * 128], wexp[:, n, :],
                                           ident[:, :])
                    ins.then_inc(wt_ps, 1)
                if f == FT - 1:
                    pe.wait_ge(wt_ready, 1)
                    for n in range(PAIRS):
                        ins = pe.matmul(banks(4)[:, n, :], wT[0:NE, n * 128:(n + 1) * 128], eb2[:, :],
                                        start=True, stop=True)
                    ins.then_inc(b2_ps, 1)

            def expert_out(e, s):
                pe.wait_ge(h_ready, 8 * e + 8)
                wait_count(pe, eo_read, 2 * e - 2)
                if isinstance(e, int) and e == 1:
                    pe.wait_ge(y_init, 1)
                for n in range(PAIRS):
                    for f in range(FT):
                        ins = pe.matmul(banks(6 - 2 * s)[:, n, :], hT[:, f, n * 128:(n + 1) * 128],
                                        w2b[:, s, f * 128:(f + 1) * 128], start=(f == 0), stop=(f == FT - 1))
                    if n % 4 == 3:
                        ins.then_inc(eo_ps, 1)

            def experts(i):
                for s in range(2):
                    hidden(2 * i + s, s)
                    expert_out(2 * i + s, s)

            experts(0)
            with pe.Fori(1, NE // 2) as i:
                experts(i)

            transpose_state(3)
            pe.wait_ge(lr_ready, 2)
            for n in range(PAIRS):
                for j in range(2):
                    o = n * 128 + j * 64
                    ins = pe.matmul(ps[j * 64:j * 64 + 64, 2, n * L:(n + 1) * L], lT[:, o:o + 64], rT[:, o:o + L],
                                    start=True, stop=True)
            ins.then_inc(sa_ps, 1)
            pe.wait_ge(sa_exp, 2)
            for n in range(PAIRS):
                ins = pe.transpose(banks(3)[:, n, :], eb[:, n * 128:(n + 1) * 128], ident[:, :])
            ins.then_inc(ebt_ps, 1)
            pe.wait_ge(ebt_ready, 1)
            for n in range(PAIRS):
                ins = pe.matmul(banks(5)[:, n, :], ebT[:, n * 128:(n + 1) * 128], X[:, n, :], start=True, stop=True)
                if n % 4 == 3:
                    ins.then_inc(sao_ps, 1)

            transpose_state(4)
            pe.wait_ge(w1_in, 16 * 8)
            wide(2, wq1[:, :], xT, state=4).then_inc(q1_ps, 1)
            pe.wait_ge(q1_ready, 1)
            pe.wait_ge(bkh_ready, 1)
            wide(4, bkh[:, :], qT, H).then_inc(qbkT_ps, 1)

            def fold(g, k):
                pe.wait_ge(qbd_ready, g + 1)
                pe.matmul(ps[:, 7, 0:QC], wkT1[:, :], qbd[:, :], start=True, stop=True).then_inc(qfold, 1)

            def scores_for_max(k, u, n, bank):
                r, c = divmod(u, NCH)
                wait_count(pe, mx_read, n - 1)
                pe.matmul(ps[0:RR, bank, 0:CHUNK], q_hi[:, k, r * RR:(r + 1) * RR],
                          ct_w[:, (k // 2) % 2, c * CHUNK:(c + 1) * CHUNK], start=True, stop=True).then_inc(mx_ps, 1)

            def values(s, c, n, bank):
                wait_count(pe, mx_read, n - 1)
                for j in range(TPC):
                    keys = slice((c * TPC + j) * KT, (c * TPC + j + 1) * KT)
                    o = ps[0:KT, bank, j * 128:(j + 1) * 128]
                    pe.matmul(o, ct_w[:, s, keys], wv_hi[:, :], start=True, stop=False)
                    ins = pe.matmul(o, ct_1[0:C, s, keys], wv_lo[:, :], start=False, stop=True)
                ins.then_inc(mx_ps, 1)

            def scores(g, k, u):
                n = 12 * g + u
                s = (k // 2) % 2
                wait_count(pe, e1_ready, n - 2)
                bank = ps[0:KT, u % 3, 0:QC]
                pe.matmul(bank, ct_w[:, s, u * KT:(u + 1) * KT], q_hi[:, k, :], start=True, stop=False)
                if u == 0:
                    pe.wait_ge(aux_ready, g + 1)
                pe.matmul(bank, ct_1[:, s, u * KT:(u + 1) * KT], q_lo[:, k, :], start=False, stop=True)\
                    .then_inc(st_ps, 1)

            def heads(g, k):
                if isinstance(g, int) and g == 2 * B - 1:
                    pe.wait_ge(cat_ready, 2 * B - 1)
                elif isinstance(g, int) and g >= 2 * B - 3:
                    pe.wait_ge(aux_ready, g + 2)
                else:
                    pe.wait_ge(qlo_ready, g + 4)
                pe.wait_ge(u1_ready, g + 1)
                for h in range(HH):
                    ins = pe.matmul(ps[0:L, 7, h * (DH + 1):(h + 1) * (DH + 1)], u1[:, k % 2, h * L:(h + 1) * L],
                                    sel1[:, (k % 2) * HH + h, :], start=True, stop=True)
                ins.then_inc(oh_ps, 1)

            def turn_heads(b):
                pe.wait_ge(cat_ready, 2 * b + 2)
                pe.transpose(ps[:, 7, 0:128], cat[:, :], ident[:, :]).then_inc(catT_ps, 1)

            def project(b, j):
                pe.wait_ge(catT_ready, b + 1)
                pe.matmul(ps[64 * j:64 * j + L, 7, 0:128], catT[:, :], wo[:, :], start=True, stop=True).then_inc(wo_ps, 1)

            def half(i, k, before, after, after2):
                g = 4 * i + k
                k1, k2, k0 = (k + 1) % 4, (k + 2) % 4, (k - 1) % 4
                done = 2 * i + k // 2 - 1
                for u in range(NT):
                    if u < NT - 2:
                        scores(g, k, u + 2)
                    elif after:
                        scores(g + 1, k1, u + 2 - NT)
                    m = unit_at(k, u)
                    if u < NT - AHEAD and after:
                        scores_for_max(k1, AHEAD + u, unit_base(i, k) + m, unit_bank(k, m))
                    elif u >= NT - AHEAD and after2:
                        if u == NT - AHEAD:
                            pe.wait_ge(qhi_ready, g + 3)
                            if k % 2 == 0:
                                pe.wait_ge(ct_in[k2 // 2], 32 * (i + 1 + (k2 == 0)))
                        scores_for_max(k2, u - (NT - AHEAD), unit_base(i, k) + m, unit_bank(k, m))
                    if u > 0:
                        weigh(g, k, u - 1)
                    elif before:
                        weigh(g - 1, k0, NT - 1)
                    if u == 0 and after2:
                        pe.wait_ge(aux_ready, g + 1)
                        fold(g + 2, k2)
                    if u in (1, 3, 5) and after and k % 2 == 1:
                        m = unit_at(k, u, value=True)
                        values(k1 // 2, u // 2, unit_base(i, k) + m, unit_bank(k, m))
                    if u == 3 and before:
                        heads(g - 1, k0)
                    if u == 5 and before and k % 2 == 0:
                        turn_heads(done)
                    if u == 6 and before and k % 2 == 0:
                        project(done, k0 // 2)
                    if u == 8 and after:
                        if before and k % 2 == 0:
                            pe.wait_ge(y1_ready, done + 1)
                        elif before:
                            pe.wait_ge(cat_ready, g)
                        else:
                            pe.wait_ge(qlo_ready, 3)
                        maxima_row(g + 1)

            def weigh(g, k, u):
                n = 12 * g + u
                if u == 0:
                    wait_count(pe, u1_ready, g - 1)
                for e, ready in ((e1_hi, e1_ready), (e1_lo, elo_ready)):
                    pe.wait_ge(ready, n + 1)
                    for a in range(2):
                        ins = pe.matmul(ps[0:VROWS, 3 + k % 2, a * GC:(a + 1) * GC],
                                        vg[:, (k // 2) % 2, u, 2 * (k % 2) + a, :], e[:, u % 3, a * GC:(a + 1) * GC],
                                        start=(u == 0 and e is e1_hi and a == 0),
                                        stop=(u == NT - 1 and e is e1_lo and a == 1))
                ins.then_inc(pv_done, 1)

            def maxima_row(g):
                pe.wait_ge(tm_ready, g + 1)
                for r in range(RT):
                    ins = pe.matmul(ps[C:C + 1, 7, r * RR:(r + 1) * RR], tm[:, r:r + 1], ident[0:RR, 0:RR],
                                    start=True, stop=True)
                ins.then_inc(tm_row, 1)

            fold(0, 0)
            pe.wait_ge(qlo_ready, 1)
            pe.wait_ge(ct_in[0], 32)
            pe.wait_ge(wv_split, 2)
            fold(1, 1)
            for c in range(NCH):
                values(0, c, c, 5 + c % 2)
            for u in range(NT):
                scores_for_max(0, u, NCH + u, 5 + (NCH + u) % 2)
            pe.wait_ge(qlo_ready, 2)
            maxima_row(0)
            for u in range(AHEAD):
                scores_for_max(1, u, NCH + NT + u, 5 + (NCH + NT + u) % 2)
            scores(0, 0, 0)
            scores(0, 0, 1)

            def attend1(i):
                for k in range(4):
                    g = 4 * i + k
                    flat = isinstance(i, int)
                    half(i, k, before=not flat or g > 0, after=not flat or g < 2 * B - 1,
                         after2=not flat or g < 2 * B - 2)

            peeled(pe, NB1, attend1)
            weigh(2 * B - 1, 3, NT - 1)
            heads(2 * B - 1, 3)
            turn_heads(B - 1)
            project(B - 1, 1)

            transpose_state(5)
            pe.wait_ge(ffn_in, 32)
            for f in range(FT):
                for n in range(2):
                    m = 2 * f + n
                    if f == 0:
                        pe.wait_ge(xt_ready, 11 + n)
                    wait_count(pe, f_ready, m - 3)
                    pe.matmul(ps[:, 2 + m % 4, :], fw1[:, f * 128:(f + 1) * 128], xT5[:, n * 512:(n + 1) * 512],
                              start=True, stop=True).then_inc(f_ps, 1)
            pe.wait_ge(f_ready, 8)
            for n in range(PAIRS):
                for f in range(FT):
                    ins = pe.matmul(banks(6)[:, n, :], hT5[:, f, n * 128:(n + 1) * 128],
                                    fw2[:, f * 128:(f + 1) * 128], start=(f == 0), stop=(f == FT - 1))
                if n % 4 == 3:
                    ins.then_inc(fo_ps, 1)

        @block.scalar
        def _(act):
            waited = act.alloc_register("waited")

            def wait_apart(s, value):
                wait_count(act, s, value)
                act.reg_mov(waited, 0)

            def state(k, xT=xT):
                for n in range(2):
                    act.wait_ge(xt_ps, 2 * k + n + 1)
                    act.activation(xT[:, n * 512:(n + 1) * 512], ps[:, n, :], ACT.Copy).then_inc(xt_ready, 1)

            state(0)
            act.wait_ge(ret_ps, 5)
            act.activation(rv.rearrange("p (b n) -> p b n", b=2), ps[:, 3:5, :], ACT.Copy).then_inc(rv_ready, 1)
            act.wait_ge(vec_ps, 1)
            act.activation(vecT[:, 0:NVEC], ps[:, 7, 0:NVEC], ACT.Copy).then_inc(vec_ready, 1)
            for n, w in enumerate((wkT0, wkT1)):
                act.activation(w[:, :].rearrange("p (a c) -> p a c", a=2),
                               ps[:, 7, 64 + 64 * n:128 + 64 * n].unsqueeze(1).to_broadcast([128, 2, 64]),
                               ACT.Copy).then_inc(vec_ready, 1)

            state(1)
            act.wait_ge(q_ps, 1)
            act.wait_ge(vec_ready, 1)
            act.activation(qT[:, :].rearrange("p (b n) -> p b n", b=2), ps[:, 2:4, :], ACT.Identity,
                           bias=vecT[:, V_BQ0:V_BQ0 + 1]).then_inc(q_ready, 1)
            act.wait_ge(qf_ps, 1)
            act.activation(qf0.rearrange("p (b n) -> p b n", b=2), ps[:, 4:6, :], ACT.Copy).then_inc(qf_ready, 1)

            def split_hi(p, m):
                j, c = divmod(m, NCH)
                wait_apart(t_ps, 6 * p + m + 1)
                act.activation(ct_all[:, 2 * p + j, c * CHUNK:(c + 1) * CHUNK], ps[:, m % 2, 0:CHUNK],
                               ACT.Copy).then_inc(ct_hi, 1)

            def stage_hi(p):
                wait_apart(s0_ps, 3 * p)
                act.activation(diag(st_hi), qf0[:, bass.ts(p, 128)].rearrange("p (j n) -> p j n", j=2),
                               ACT.Copy).then_inc(sthi_ready, 1)

            def exp0(p, c):
                act.wait_ge(shift0, p + 1)
                wait_apart(e0t_ps, 3 * p - 2 + c)
                act.activation(e0[:, c * CHUNK:(c + 1) * CHUNK], ps[:, 2 + c, 0:CHUNK], ACT.Exp,
                               bias=sm[:, 1, 0:1], accum_out=esum[:, c, bass.ts(p, 1)]).then_inc(e0_ready, 1)

            def diag(st):
                return st[:, :, :].rearrange("p j n -> p (j n)").rearrange("p (a n) -> p a n", n=64)[:, 0:4:3, :]

            def attend0(p, h):
                last = isinstance(p, int) and p == PAIRS - 1
                if not last:
                    split_hi(p + 1, 0)
                exp0(p, 0)
                if not last:
                    split_hi(p + 1, 1)
                exp0(p, 1)
                exp0(p, 2)
                if not last:
                    stage_hi(p + 1)
                    split_hi(p + 1, 2)
                wait_count(act, u0_ps, p)
                act.wait_ge(e0t_ps, 3 * p + 2)
                act.activation(e0T[:, TPC:2 * TPC, :].rearrange("p t n -> p (t n)"), ps[0:KT, 6, :], ACT.Copy)\
                    .then_inc(e0t_act, 1)
                if not last:
                    for m in range(3, 2 * NCH):
                        split_hi(p + 1, m)

            for m in range(2 * NCH):
                split_hi(0, m)
            act.wait_ge(qf_ready, 1)
            act.wait_ge(pool_set, 10)
            stage_hi(0)
            pairs_loop(act, attend0)

            state(2)
            act.wait_ge(top_ready, 1)
            act.activation(sm[:, 3, :], sm[:, 3, :], ACT.Exp).then_inc(e2_ready, 1)

            def experts(i):
                for s in range(2):
                    e = 2 * i + s
                    wait_count(act, eo_ps, 2 * e)
                    act.wait_ge(b1_ready, e + 1)
                    for f in range(FT):
                        for n in range(2):
                            m = 8 * e + 2 * f + n
                            act.wait_ge(h_ps, m + 1)
                            act.activation(hT[:, f, n * 512:(n + 1) * 512], ps[:, (2 * f + n) % 4, :], ACT.Gelu,
                                           bias=b1s[:, s, f:f + 1]).then_inc(h_ready, 1)

            experts(0)
            with act.Fori(1, NE // 2) as i:
                experts(i)

            state(3)
            act.wait_ge(sa_sub, 2)
            act.wait_ge(eb_zero, 1)
            for j in range(2):
                r = slice(64 * j, 64 * j + 64)
                act.activation(eb[r, :].rearrange("p (t n) -> p t n", n=128)[:, :, 64 * j:64 * j + L],
                               lT[r, 0:PAIRS * L].rearrange("p (t n) -> p t n", n=L), ACT.Exp).then_inc(sa_exp, 1)
            act.wait_ge(ebt_ps, 1)
            act.activation(ebT.rearrange("p (b n) -> p b n", b=2), ps[:, 3:5, :], ACT.Copy).then_inc(ebt_ready, 1)

            state(4)
            act.wait_ge(q1_ps, 1)
            act.activation(qT[:, :].rearrange("p (b n) -> p b n", b=2), ps[:, 2:4, :], ACT.Identity,
                           bias=vecT[:, V_BQ1:V_BQ1 + 1]).then_inc(q1_ready, 1)
            act.wait_ge(qbkT_ps, 1)
            act.activation(qbkT.rearrange("p (b n) -> p b n", b=2), ps[0:H, 4:6, :], ACT.Copy).then_inc(qbkT_ready, 2)

            def high(g, k):
                act.wait_ge(qfold, g + 1)
                act.activation(q_hi[:, k, :], ps[:, 7, 0:QC], ACT.Copy).then_inc(qhi_ready, 1)

            def sums(g, k):
                act.wait_ge(pv_done, 12 * g + 12)
                wait_count(act, oh_ps, g - 1)
                act.activation(u1[:, k % 2, :], ps[0:C + 1, 3 + k % 2, 0:QC], ACT.Copy).then_inc(u1_ready, 1)

            def value_hi(s, c, n, bank):
                act.wait_ge(mx_ps, n + 1)
                act.activation(vg[:, s, c * TPC:(c + 1) * TPC, :, 0:GW],
                               ps[0:KT, bank, :].rearrange("p (t g r) -> p t g r", t=TPC, g=NG), ACT.Copy)\
                    .then_inc(vhi_ready, 1)

            def turned(b):
                act.wait_ge(catT_ps, b + 1)
                act.activation(catT[:, :], ps[:, 7, 0:L], ACT.Copy).then_inc(catT_ready, 1)

            def attend1(i):
                for k in range(4):
                    g = 4 * i + k
                    flat = isinstance(i, int)
                    for u in range(NT):
                        n = 12 * g + u
                        act.wait_ge(st_ps, n + 1)
                        wait_count(act, elo_ready, n - 2)
                        act.activation(e1[:, u % 3, :], ps[0:KT, u % 3, 0:QC], ACT.Exp)
                        wait_count(act, pv_done, n - 2)
                        act.activation(e1_hi[:, u % 3, :], ps[0:KT, u % 3, 0:QC], ACT.Exp).then_inc(e1_ready, 1)
                        if u == 1 and (not flat or g > 0):
                            sums(g - 1, k - 1)
                        if u == 2 and (not flat or g < 2 * B - 2):
                            high(g + 2, (k + 2) % 4)
                        if u == 5 and k % 2 == 0 and (not flat or g > 0):
                            turned(2 * i + k // 2 - 1)
                        if u in (2, 4, 6) and k % 2 == 1 and (not flat or g < 2 * B - 1):
                            m = unit_at(k, u - 1, value=True)
                            value_hi(((k + 1) // 2) % 2, u // 2 - 1, unit_base(i, k) + m, unit_bank(k, m))

            high(0, 0)
            high(1, 1)
            for c in range(NCH):
                value_hi(0, c, c, 5 + c % 2)
            peeled(act, NB1, attend1)
            sums(2 * B - 1, 3)
            turned(B - 1)

            state(5, xT5)
            for f in range(FT):
                for n in range(2):
                    m = 2 * f + n
                    act.wait_ge(f_ps, m + 1)
                    act.activation(hT5[:, f, n * 512:(n + 1) * 512], ps[:, 2 + m % 4, :], ACT.Relu,
                                   bias=vecT[:, V_FB1 + f:V_FB1 + f + 1]).then_inc(f_ready, 1)

        @block.vector
        def _(v):
            steps = [0]

            def step(ins):
                steps[0] += 1
                ins.then_inc(dve_step, 1)
                v.wait_ge(dve_step, steps[0])

            def norm(k, make):
                for n in range(2):
                    ins = make(n)
                    if ins is not None:
                        step(ins)
                    for m in range(4 * n, 4 * n + 4):
                        ins = v.bn_stats(stats[:, m, :], Y[:, m, :])
                    step(ins)
                    for m in range(4 * n, 4 * n + 4):
                        ins = v.bn_aggr(mv[:, m, :], stats[:, m, :])
                    step(ins)
                    v.tensor_scalar(ve[:, 4 * n:4 * n + 4], mv[:, 4 * n:4 * n + 4, 1], EPS, None, ALU.add)\
                        .then_inc(ve_ready, 1)
                for n in range(2):
                    v.wait_ge(rstd_ready, 2 * k + n + 1)
                    for m in range(4 * n, 4 * n + 4):
                        ins = v.tensor_scalar(X[:, m, :], Y[:, m, :], mv[:, m, 0:1], rstd[:, m:m + 1],
                                              ALU.subtract, ALU.mult)
                    ins.then_inc(x_norm, 1)

            def heads8(a, w=128):
                return a.rearrange("p (t n) -> p t n", n=w)

            v.memset(X[:, :, :], 0.0).then_inc(x_pad, 1)
            v.memset(sel1[C:C + 1, :, DH:DH + 1], 1.0).then_inc(x_pad, 1)

            v.wait_ge(ret_in, 16 * 4)
            for src, dst in ((wret[:, 0, :], wret[:, 3, :]), (wret[:, 1, :], wrkr)):
                s2 = src.rearrange("p (i two) -> p i two", two=2)
                d2 = dst.rearrange("p (i two) -> p i two", two=2)
                v.tensor_scalar(d2[:, :, 0], s2[:, :, 1], -1.0, None, ALU.mult).then_inc(rot_ready, 1)
                v.tensor_copy(d2[:, :, 1], s2[:, :, 0]).then_inc(rot_ready, 1)

            def table(c):
                return kc[:, c:c + SLOT].unsqueeze(1).to_broadcast([128, B, SLOT])

            def rotary(dst, raw, rot, cos, sin, unit):
                v.wait_ge(ret_ps, unit + 1)
                for n, bank in enumerate(raw):
                    ins = v.tensor_tensor(dst[:, n * 512:(n + 1) * 512].rearrange("p (b q) -> p b q", q=SLOT),
                                          ps[:, bank, :].rearrange("p (b q) -> p b q", q=SLOT),
                                          table(cos)[:, 0:B // 2, :], ALU.mult)
                ins.then_inc(ret_read, 1)
                v.wait_ge(ret_ps, unit + 2)
                for n, bank in enumerate(rot):
                    ins = v.tensor_tensor(qT[:, n * 512:(n + 1) * 512].rearrange("p (b q) -> p b q", q=SLOT),
                                          ps[:, bank, :].rearrange("p (b q) -> p b q", q=SLOT),
                                          table(sin)[:, 0:B // 2, :], ALU.mult)
                step(ins)
                v.tensor_tensor(dst, dst, qT[:, :], ALU.add).then_inc(ret_read, 1)

            rotary(rq, (3, 4), (5, 6), K_COSQ, K_SINQ, 0)
            v.wait_ge(ret_read, 2)
            rotary(rk, (7, 0), (1, 2), K_COSK, K_SINK, 2)
            v.wait_ge(ret_ps, 6)
            v.tensor_tensor(heads8(rm), banks(5), kc[:, K_MASK:K_MASK + 128].unsqueeze(1).to_broadcast([128, PAIRS, 128]),
                            ALU.mult).then_inc(ret_read, 1)
            def add_retention(n):
                v.wait_ge(ret_ps, 7 + n)
                h = slice(4 * n, 4 * n + 4)
                return v.tensor_tensor(Y[:, h, :], banks(3)[:, h, :], X[:, h, :], ALU.add)

            norm(0, add_retention)

            v.wait_ge(qbk_ps, 1)
            v.tensor_copy(sm[:, 0, :], ps[:, 6, 0:PAIRS]).then_inc(qbk_ready, 1)
            qbk0 = sm[:, 0, :]

            def split_lo(p, m):
                j, c = divmod(m, NCH)
                v.wait_ge(ct_hi, 6 * p + m + 1)
                lo = ct_all[64:128, 2 * p + j, c * CHUNK:(c + 1) * CHUNK]
                v.tensor_tensor(lo, ps[64:128, m % 2, 0:CHUNK], lo.bitcast(F32), ALU.subtract).then_inc(ct_ready, 1)

            def diag(st):
                return st[:, :, :].rearrange("p j n -> p (j n)").rearrange("p (a n) -> p a n", n=64)[:, 0:4:3, :]

            def stage_lo(p):
                v.wait_ge(sthi_ready, p + 1)
                v.tensor_tensor(diag(st_lo), qf0[:, bass.ts(p, 128)].rearrange("p (j n) -> p j n", j=2),
                                diag(st_hi).bitcast(F32), ALU.subtract).then_inc(stlo_ready, 1)

            def sums_out(p):
                v.wait_ge(u0_ps, p + 1)
                v.tensor_copy(u0[:, bass.ts(p, 128)], ps[0:C + 1, 7, 0:128]).then_inc(u0_ready, 1)

            def exp_out(p, c):
                wait_count(v, u0_ps, p)
                v.wait_ge(e0t_ps, 3 * p + c + 1)
                v.tensor_copy(e0T[:, c * TPC:(c + 1) * TPC, :].rearrange("p t n -> p (t n)"), ps[0:KT, 5, :])\
                    .then_inc(e0t_dve, 1)

            def attend0(p, h):
                last = isinstance(p, int) and p == PAIRS - 1
                first = isinstance(p, int) and p == 0
                for c in range(NCH):
                    v.wait_ge(s0_ps, 3 * p + c + 1)
                    ins = v.tensor_reduce(sm[:, 4, c:c + 1], ps[:, 2 + c, 0:CHUNK], AX.X, ALU.max)
                    if c == 0 and not first:
                        sums_out(p - 1)
                ins.then_inc(m0_step, 1)
                v.wait_ge(m0_step, 3 * p + 1)
                v.tensor_reduce(sm[:, 4, 3:4], sm[:, 4, 0:NCH], AX.X, ALU.max).then_inc(m0_step, 1)
                v.wait_ge(m0_step, 3 * p + 2)
                v.tensor_tensor(sm[:, 4, 4:5], sm[:, 4, 3:4], sm[:, 0, bass.ts(p, 1)], ALU.add).then_inc(m0_step, 1)
                v.wait_ge(m0_step, 3 * p + 3)
                v.tensor_tensor(sm[:, 1, 0:1], sm[:, 0, bass.ts(p, 1)], sm[:, 4, 4:5], ALU.subtract).then_inc(shift0, 1)
                if not last:
                    split_lo(p + 1, 0)
                    split_lo(p + 1, 1)
                exp_out(p, 0)
                if not last:
                    split_lo(p + 1, 2)
                    split_lo(p + 1, 3)
                exp_out(p, 2)
                if not last:
                    stage_lo(p + 1)
                    split_lo(p + 1, 4)
                    split_lo(p + 1, 5)

            for m in range(2 * NCH):
                split_lo(0, m)
            stage_lo(0)
            pairs_loop(v, attend0)
            sums_out(PAIRS - 1)
            v.wait_ge(e0_ready, NCH * PAIRS)
            step(v.tensor_reduce(sm[:, 2, :], esum[:, :, :].rearrange("p c n -> p n c"), AX.X, ALU.add))
            step(v.reciprocal(sm[:, 5, :], sm[:, 2, :]))

            def add_cross0(n):
                v.wait_ge(o0_ps, n + 1)
                for m in range(4 * n, 4 * n + 4):
                    ins = v.scalar_tensor_tensor(out=Y[:, m, :], in0=banks(0)[:, m, :], scalar=sm[:, 5, m:m + 1],
                                                 in1=X[:, m, :], op0=ALU.mult, op1=ALU.add)
                return ins

            norm(1, add_cross0)

            def first_bias(e, s):
                v.tensor_scalar(b1s[:, s, :], vecT[:, bass.ds(V_EB1 + FT * e, FT)], 1.0, None, ALU.mult)\
                    .then_inc(b1_ready, 1)

            v.wait_ge(vec_ready, 1)
            first_bias(0, 0)
            v.wait_ge(pool_set, 10)
            v.wait_ge(gate_ps, 1)
            step(v.tensor_tensor(gate[:, :, 0:NE], ps[:, 4, 0:8 * PAIRS].rearrange("p (t n) -> p t n", n=8)[:, :, 0:NE],
                                 bg_b[:, :].unsqueeze(1).to_broadcast([128, PAIRS, NE]), ALU.add))
            for n in range(PAIRS):
                ins = v.max(top[:, n, :], gate[:, n, :])
            step(ins)
            v.tensor_tensor(sm[:, 3, :], top[:, :, 1], top[:, :, 0], ALU.subtract).then_inc(top_ready, 1)
            for n in range(PAIRS):
                ins = v.max_index(topi[:, n, :], top[:, n, :], gate[:, n, :])
            step(ins)
            step(v.tensor_copy(topf[:, :, :], topi[:, :, 0:2]))
            v.wait_ge(e2_ready, 1)
            step(v.tensor_scalar(sm[:, 6, :], sm[:, 3, :], 1.0, None, ALU.add))
            step(v.reciprocal(sm[:, 6, :], sm[:, 6, :]))
            step(v.tensor_tensor(sm[:, 7, :], sm[:, 3, :], sm[:, 6, :], ALU.mult))
            iota = kc[:, K_IOTA:K_IOTA + NE].unsqueeze(1).to_broadcast([128, PAIRS, NE])

            def spread(a):
                return a.unsqueeze(2).to_broadcast([128, PAIRS, NE])

            v.tensor_tensor(wexp[:, :, 0:NE], iota, spread(topf[:, :, 0]), ALU.is_equal)
            step(v.tensor_tensor(wtmp[:, :, :], iota, spread(topf[:, :, 1]), ALU.is_equal))
            v.tensor_tensor(wexp[:, :, 0:NE], wexp[:, :, 0:NE], spread(sm[:, 6, :]), ALU.mult)
            step(v.tensor_tensor(wtmp[:, :, :], wtmp[:, :, :], spread(sm[:, 7, :]), ALU.mult))
            v.tensor_tensor(wexp[:, :, 0:NE], wexp[:, :, 0:NE], wtmp[:, :, :], ALU.add).then_inc(wexp_ready, 1)
            v.wait_ge(wexp_ready, 1)
            v.wait_ge(wt_ps, 1)
            v.tensor_copy(wT[0:8, :].rearrange("p (b n) -> p b n", b=2), ps[0:8, 6:8, :]).then_inc(wt_ready, 1)
            v.wait_ge(b2_ps, 1)
            v.tensor_tensor(Y[:, :, :], banks(4), X[:, :, :], ALU.add).then_inc(y_init, 1)

            def add_expert(e, s, n):
                v.wait_ge(eo_ps, 2 * e + n + 1)
                wait_count(v, eo_read, 2 * e - 1 + n)
                for m in range(4 * n, 4 * n + 4):
                    ins = v.scalar_tensor_tensor(out=Y[:, m, :], in0=banks(6 - 2 * s)[:, m, :],
                                                 scalar=wexp[:, m, bass.ts(e, 1)], in1=Y[:, m, :],
                                                 op0=ALU.mult, op1=ALU.add)
                return ins.then_inc(eo_read, 1)

            def experts(i):
                for s in range(2):
                    e = 2 * i + s
                    wait_count(v, eo_read, 2 * e)
                    first_bias(e + 1, 1 - s)
                    if isinstance(i, int) and e == 0:
                        v.wait_ge(y_init, 1)
                    if isinstance(i, int) and e == NE - 1:
                        break
                    for n in range(2):
                        add_expert(e, s, n)

            def add_last_expert(n):
                add_expert(NE - 1, 1, n)
                v.wait_ge(eo_read, 2 * NE - 1 + n)

            experts(0)
            with v.Fori(1, NE // 2 - 1) as i:
                experts(i)
            experts(NE // 2 - 1)
            norm(2, add_last_expert)

            v.wait_ge(xt_ready, 8)
            v.tensor_scalar(lT, xT[:, :], vecT[:, V_WL:V_WL + 1], None, ALU.mult).then_inc(lr_ready, 1)
            v.tensor_scalar(rT, xT[:, :], vecT[:, V_WR:V_WR + 1], None, ALU.mult).then_inc(lr_ready, 1)
            v.wait_ge(sa_ps, 1)
            sa = ps[:, 2, 0:PAIRS * L].rearrange("p (t n) -> p t n", n=L)
            step(v.tensor_reduce(sm[:, 4, :], sa, AX.X, ALU.max))
            v.tensor_tensor(lT[:, 0:PAIRS * L].rearrange("p (t n) -> p t n", n=L), sa,
                            sm[:, 4, :].unsqueeze(2).to_broadcast([128, PAIRS, L]), ALU.subtract).then_inc(sa_sub, 2)
            v.wait_ge(sa_exp, 2)
            step(v.tensor_reduce(sm[:, 5, :], heads8(eb), AX.X, ALU.add))
            step(v.reciprocal(sm[:, 6, :], sm[:, 5, :]))

            def add_self(n):
                v.wait_ge(sao_ps, n + 1)
                for m in range(4 * n, 4 * n + 4):
                    ins = v.scalar_tensor_tensor(out=Y[:, m, :], in0=banks(5)[:, m, :], scalar=sm[:, 6, m:m + 1],
                                                 in1=X[:, m, :], op0=ALU.mult, op1=ALU.add)
                return ins

            norm(3, add_self)

            v.tensor_scalar(bkh[:, :], kc[:, K_HEAD:K_HEAD + H], vecT[:, V_BK1:V_BK1 + 1], None, ALU.mult)\
                .then_inc(bkh_ready, 1)
            v.wait_ge(w1_in, 16 * 8)
            v.tensor_copy(wv_hi[:, :], wv_raw[:, :]).then_inc(wv_split, 1)
            v.wait_ge(wv_split, 1)
            v.tensor_tensor(wv_lo[:, :], wv_raw[0:C, :], wv_hi[0:C, :].bitcast(F32), ALU.subtract)
            v.memset(ct_1[C:C + 1, :, :].bitcast(F32), 1.0)
            v.memset(vg[:, :, :, :, 2 * GW:VROWS].bitcast(F32), 1.0).then_inc(wv_split, 1)
            v.wait_ge(x_norm, 8)
            v.tensor_tensor(Y[:, :, :], X[:, :, :], bo_b[:, :].unsqueeze(1).to_broadcast([128, PAIRS, 128]), ALU.add)\
                .then_inc(xb_ready, 1)
            v.wait_ge(q1_ready, 1)
            v.wait_ge(qbkT_ready, 2)
            v.memset(cat[:, :], 0.0)

            def blocks(g, k, b):
                wait_count(v, qfold, g)
                hf = (k + 3) % 2
                v.tensor_tensor(qbd[:, :].rearrange("p (h q) -> p h q", q=L),
                                qT[:, bass.ds(b * SLOT, L)].unsqueeze(1).to_broadcast([128, HH, L]),
                                kc[:, K_HEAD + hf * HH:K_HEAD + (hf + 1) * HH].unsqueeze(2).to_broadcast([128, HH, L]),
                                ALU.mult).then_inc(qbd_ready, 1)

            def low(g, k):
                v.wait_ge(qhi_ready, g + 1)
                v.tensor_tensor(q_lo[0:C, k, :], ps[0:C, 7, 0:QC], q_hi[0:C, k, :].bitcast(F32), ALU.subtract)\
                    .then_inc(qlo_ready, 1)

            def value_lo(b, s, c, bank):
                v.wait_ge(vhi_ready, 3 * b + c + 1)
                tiles = vg[:, s, c * TPC:(c + 1) * TPC, :, :]
                v.tensor_tensor(tiles[:, :, :, GW:2 * GW], ps[0:KT, bank, :].rearrange("p (t g r) -> p t g r", t=TPC, g=NG),
                                tiles[:, :, :, 0:GW].bitcast(F32), ALU.subtract).then_inc(mx_read, 1)

            def unit_max(g2, u, n, bank):
                r, c = divmod(u, NCH)
                v.wait_ge(mx_ps, n + 1)
                v.tensor_reduce(tmx[:, g2, r, c:c + 1], ps[0:RR, bank, 0:CHUNK], AX.X, ALU.max).then_inc(mx_read, 1)

            def row_max(g2, n):
                v.wait_ge(mx_read, n + 1)
                v.tensor_reduce(tm[:, :], tmx[:, g2, :, :], AX.X, ALU.max).then_inc(tm_ready, 1)

            def shift(g, k, loads):
                v.wait_ge(qrow_in[k % 2], loads)
                v.wait_ge(tm_row, g + 1)
                v.tensor_tensor(mrow, ps[C:C + 1, 7, 0:QC], qbk_row[k % 2], ALU.add).then_inc(m_ready, 1)
                v.wait_ge(m_ready, g + 1)
                v.tensor_tensor(q_lo[C:C + 1, k, :], qbk_row[k % 2], mrow, ALU.subtract).then_inc(aux_ready, 1)

            def heads_out(g, k):
                v.wait_ge(oh_ps, g + 1)
                o = ps[0:L, 7, 0:HH * (DH + 1)].rearrange("p (h d) -> p h d", d=DH + 1)
                v.reciprocal(rec, o[:, :, DH]).then_inc(rec_ready, 1)
                v.wait_ge(rec_ready, g + 1)
                hf = k % 2
                v.tensor_tensor(cat[0:L, hf * 64:(hf + 1) * 64].rearrange("p (h d) -> p h d", d=DH), o[:, :, 0:DH],
                                rec.unsqueeze(2).to_broadcast([L, HH, DH]), ALU.mult).then_inc(cat_ready, 1)

            def output(b, n, j):
                v.wait_ge(wo_ps, b + 1)
                y = Y[64 * j:64 * j + L, bass.ts(n, 1), :].rearrange("p o n -> p (o n)")
                v.tensor_tensor(y, ps[64 * j:64 * j + L, 7, 0:128], y, ALU.add).then_inc(y1_ready, 1)

            def attend1(i):
                for k in range(4):
                    g = 4 * i + k
                    flat = isinstance(i, int)
                    before, after, after2 = (not flat or g > 0), (not flat or g < 2 * B - 1), (not flat or g < 2 * B - 2)
                    after3 = not flat or g < 2 * B - 3
                    for u in range(NT):
                        if u in (2, 4, 6) and after and k % 2 == 1:
                            c = u // 2 - 1
                            value_lo(2 * i + (k + 1) // 2, ((k + 1) // 2) % 2, c,
                                     unit_bank(k, unit_at(k, u - 1, value=True)))
                        m = unit_at(k, u)
                        if u < NT - AHEAD and after:
                            unit_max((k + 1) % 2, AHEAD + u, unit_base(i, k) + m, unit_bank(k, m))
                        elif u >= NT - AHEAD and after2:
                            unit_max(k % 2, u - (NT - AHEAD), unit_base(i, k) + m, unit_bank(k, m))
                        if u == 1 and after2:
                            low(g + 2, (k + 2) % 4)
                        if u == 3 and before:
                            heads_out(g - 1, k - 1)
                        if u == NT - AHEAD - 1 and after:
                            row_max((k + 1) % 2, unit_base(i, k) + m)
                        if u == 6 and before and k % 2 == 0:
                            output(2 * i + k // 2 - 1, i - 1 + k // 2, (k // 2 + 1) % 2)
                        if u == 7 and after:
                            shift(g + 1, (k + 1) % 4, 16 * (2 * i + (k + 1) // 2 + 1))
                        if u == 10 and after3:
                            blocks(g + 3, k, 2 * i + (k + 3) // 2)

            for n in range(2):
                blocks(n, n + 1, 0)
                low(n, n)
            blocks(2, 3, 1)
            for c in range(NCH):
                value_lo(0, 0, c, 5 + c % 2)
            for u in range(NT):
                unit_max(0, u, NCH + u, 5 + (NCH + u) % 2)
            row_max(0, NCH + NT - 1)
            shift(0, 0, 16)
            for u in range(AHEAD):
                unit_max(1, u, NCH + NT + u, 5 + (NCH + NT + u) % 2)
            v.wait_ge(xb_ready, 1)
            peeled(v, NB1, attend1)
            heads_out(2 * B - 1, 3)
            output(B - 1, PAIRS - 1, 1)
            v.wait_ge(y1_ready, B)
            norm(4, lambda n: None)

            v.wait_ge(x_norm, 10)
            step(v.tensor_tensor(Y[:, :, :], X[:, :, :], fb2_b[:, :].unsqueeze(1).to_broadcast([128, PAIRS, 128]), ALU.add))

            def add_forward(n):
                v.wait_ge(fo_ps, n + 1)
                h = slice(4 * n, 4 * n + 4)
                return v.tensor_tensor(Y[:, h, :], banks(6)[:, h, :], Y[:, h, :], ALU.add)

            norm(5, add_forward)


def _constants():
    f = np.float32
    half = D // 2
    scale_vec = (np.arange(0, D, 2, dtype=f) + f(0.4 * D)) / f(1.4 * D)
    pos = np.arange(L, dtype=f)
    scale = scale_vec[None, :] ** (pos[:, None] / f(512.0))
    inv_freq = f(1.0) / f(10000.0) ** (np.arange(half, dtype=f) / f(half))
    sinusoid = pos[:, None] * inv_freq[None, :]
    k = np.zeros((128, NALL), f)
    for col, fn, sc in ((K_COSQ, np.cos, scale), (K_SINQ, np.sin, scale),
                        (K_COSK, np.cos, f(1.0) / scale), (K_SINK, np.sin, f(1.0) / scale)):
        k[:, col:col + L] = np.repeat(fn(sinusoid) * sc, 2, axis=-1).T
    n = np.arange(L)
    diff = n[None, :] - n[:, None]
    decay = np.where(diff >= 0, f(0.96875) ** np.maximum(diff, 0).astype(f), f(0.0))
    for j in range(2):
        k[SLOT * j:SLOT * j + L, K_MASK + SLOT * j:K_MASK + SLOT * j + L] = decay
    k[np.arange(128), K_HEAD + np.arange(128) // DH] = f(1.0 / np.sqrt(DH))
    k[:, K_IOTA:K_IOTA + NE] = np.arange(NE)
    sel = k[0:C, K_SEL:NALL].reshape(C, H, DH + 1)
    r = np.arange(C) % GW
    for h in range(H):
        sel[r // DH == h % HG, h, r[r // DH == h % HG] % DH] = 1.0
    k[0:C, K_SEL:NALL] = sel.reshape(C, -1)
    return k


_INS = ["x", "ctx_512", "L0_attn_W_Q", "L0_attn_W_K", "L0_attn_W_V", "L0_xattn_Wq", "L0_xattn_bq", "L0_xattn_Wk",
        "L0_xattn_bk", "L0_xattn_Wv", "L0_xattn_bv", "L0_ffn_Wg", "L0_ffn_bg", "L0_ffn_W1", "L0_ffn_b1", "L0_ffn_W2",
        "L0_ffn_b2", "L1_attn_w_lhs", "L1_attn_w_rhs", "L1_xattn_Wq", "L1_xattn_bq", "L1_xattn_Wk", "L1_xattn_bk",
        "L1_xattn_Wv", "L1_xattn_bv", "L1_xattn_Wo", "L1_xattn_bo", "L1_ffn_W1", "L1_ffn_b1", "L1_ffn_W2", "L1_ffn_b2"]


def kernel(**inputs):
    import concourse.bacc as _bacc
    from concourse.bass_utils import run_bass_kernel_spmd as _run

    nc = _bacc.Bacc("TRN2", target_bir_lowering=False, num_devices=1)
    arrays, aps = {}, {}
    for name in _INS:
        a = np.ascontiguousarray(inputs[name])
        arrays[f"in_{name}"] = a
        aps[name] = nc.dram_tensor(f"in_{name}", a.shape, mybir.dt.from_np(a.dtype), kind="ExternalInput").ap()
    arrays["in_constants"] = _constants()
    consts = nc.dram_tensor("in_constants", (128, NALL), F32, kind="ExternalInput").ap()
    out = nc.dram_tensor("out_0", (B, L, D), F32, kind="ExternalOutput").ap()
    decoder(nc, aps, consts, out)
    r = _run(nc, [arrays], core_ids=[0])
    return r.results[0]["out_0"]
```

```python
from contextlib import ExitStack

import numpy as np

import concourse.bass as bass
from concourse import mybir
from concourse.alu_op_type import AluOpType as ALU

ACT = mybir.ActivationFunctionType
AX = mybir.AxisListType
F32 = mybir.dt.float32
F32R = mybir.dt.float32r
U32 = mybir.dt.uint32

B, L, D = 16, 56, 128
S, C = 1500, 64
SLOT = 64
PAIRS = B // 2
TOK = B * SLOT
KT, NT = 125, 12
CHUNK, NCH = 500, 3
TPC = CHUNK // KT
NCN = 6
NE, F = 6, 512
FT = F // 128
H, DH = 16, 8
HH = H // 2
QC = HH * L
HG, NG = 4, 4
GW, GC = HG * DH, HG * L
VROWS = 2 * GW + 1
VALS = NT * NG * VROWS
RT = 4
RR = QC // RT
DVE_LOWS = (9,)
AHEAD = 6
LEAD = NCH + RT * NCH + AHEAD
EPS = 1e-5
NEG = -3.0e38

V_BQ0, V_BK0, V_BQ1, V_BK1, V_WL, V_WR, V_FB1, V_EB1 = 0, 1, 2, 3, 4, 5, 6, 10
NVEC = V_EB1 + NE * FT
K_COSQ, K_SINQ, K_COSK, K_SINK, K_MASK, K_HEAD, K_IOTA = 0, 64, 128, 192, 256, 384, 400
NCONST = K_IOTA + NE
K_SEL = NCONST
NALL = K_SEL + H * (DH + 1)


def wait_count(eng, sem, value):
    if isinstance(value, int) and value <= 0:
        return
    eng.wait_ge(sem, value)


def unit_base(i, k):
    return LEAD + 54 * i + (0, 12, 27, 39)[k]


def unit_at(k, u, value=False):
    values_before = min(u // 2, NCH) if k % 2 else 0
    return u + values_before + value


def unit_bank(k, m):
    return 5 + (unit_base(0, k) + m) % 2


def lows_before(u):
    return sum(d < u for d in DVE_LOWS)


def context_bank(p, m):
    return (7, 6, 5, 2)[m] if isinstance(p, int) and p == 0 and m < 4 else m % 2


def peeled(eng, n, body):
    body(0)
    with eng.Fori(1, n - 1) as i:
        body(i)
    body(n - 1)


def pairs_loop(eng, body):
    body(0, 0)
    with eng.Fori(0, (PAIRS - 2) // 3) as i:
        for h in range(3):
            body(3 * i + 1 + h, (1 + h) % 3)
    body(PAIRS - 1, (PAIRS - 1) % 3)


def decoder(nc: bass.Bass, t, consts, out):
    with ExitStack() as ctx:
        def sb(name, shape, dt=F32):
            return ctx.enter_context(nc.sbuf_tensor(name, shape, dt))

        def sem(name):
            return ctx.enter_context(nc.semaphore(name))

        ct_all = sb("ct_all", [128, B, S], F32R)
        X = sb("X", [128, PAIRS, 128])
        Y = sb("Y", [128, PAIRS, 128])
        qT = sb("qT", [128, TOK])
        kc = sb("kc", [128, NCONST])
        ident = sb("ident", [128, 128])
        wq1 = sb("wq1", [128, 128])
        wkT1 = sb("wkT1", [128, 128])
        wv_raw = sb("wv_raw", [128, 128])
        wv_hi = sb("wv_hi", [128, 128], F32R)
        wv_lo = sb("wv_lo", [C, 128], F32R)
        sel1 = sb("sel1", [C + 1, H, DH + 1])
        fw1 = sb("fw1", [128, F])
        fw2 = sb("fw2", [128, F])
        wo = sb("wo", [128, 128])
        bo_b = sb("bo_b", [128, 128])
        fb2_b = sb("fb2_b", [128, 128])
        bg_b = sb("bg_b", [128, NE])
        ones = sb("ones", [128, 128])
        vecT = sb("vecT", [128, NVEC + FT])
        b1s = sb("b1s", [128, 2, FT])
        bkh = sb("bkh", [128, H])
        stats = sb("stats", [128, PAIRS, 6])
        mv = sb("mv", [128, PAIRS, 2])
        ve = sb("ve", [128, PAIRS])
        rstd = sb("rstd", [128, PAIRS])
        mhalf = sb("mhalf", [128, PAIRS])
        base_e = sb("base_e", [128, PAIRS])
        sm = sb("sm", [128, 8, PAIRS])
        esum = sb("esum", [128, NCH, PAIRS])
        tmx = sb("tmx", [RR, 2, RT, NCH])
        tm = sb("tm", [RR, RT])
        ps = ctx.enter_context(nc.psum_tensor("ps", [128, 8, 512], F32))

        def lifetime(*tensors):
            with ExitStack() as scope:
                return [scope.enter_context(nc.sbuf_tensor(name, shape, dt)) for name, shape, dt in tensors]

        cn, arena, w1b, w2b, xT, st_hi, st_lo, wq0, wkT0, wv0, wg, eb2, gate, top, topi, topf, wexp, wtmp = lifetime(
            ("cn", [KT, NCN, NT * 129], F32),
            ("arena", [128, 4096], F32),
            ("w1b", [128, 2, F], F32),
            ("w2b", [128, 2, F], F32),
            ("xT", [128, TOK], F32),
            ("st_hi", [128, 2, 128], F32R),
            ("st_lo", [128, 2, 128], F32R),
            ("wq0", [128, 128], F32),
            ("wkT0", [128, 128], F32),
            ("wv0", [C + 1, 128], F32),
            ("wg", [128, NE], F32),
            ("eb2", [NE, 128], F32),
            ("gate", [128, PAIRS, 8], F32),
            ("top", [128, PAIRS, 8], F32),
            ("topi", [128, PAIRS, 8], U32),
            ("topf", [128, PAIRS, 2], F32),
            ("wexp", [128, PAIRS, 8], F32),
            ("wtmp", [128, PAIRS, NE], F32))
        vg, ct_w, e1, e1_hi, e1_lo, qrow, qbd, u1, cat, catT, q_hi, q_lo, ct_1 = lifetime(
            ("vg", [KT, 2, NT, NG, VROWS], F32R),
            ("ct_w", [128, 2, S], F32R),
            ("e1", [KT, 3, QC], F32),
            ("e1_hi", [KT, 3, QC], F32R),
            ("e1_lo", [KT, 3, QC], F32R),
            ("qrow", [C + 1, 3, QC], F32),
            ("qbd", [128, QC], F32),
            ("u1", [C + 1, 2, QC], F32),
            ("cat", [128, 128], F32),
            ("catT", [128, L], F32),
            ("q_hi", [128, 4, QC], F32R),
            ("q_lo", [C + 1, 4, QC], F32R),
            ("ct_1", [C + 1, 2, S], F32R))
        _, xh, xl, wh0, wl0, _, wh1, wl1 = lifetime(
            ("values_0", [128, VALS], F32),
            ("xh", [128, TOK], F32R),
            ("xl", [128, TOK], F32R),
            ("wh0", [128, F], F32R),
            ("wl0", [128, F], F32R),
            ("context_0", [128, VALS + S - 2 * TOK - 2 * F], F32),
            ("wh1", [128, F], F32R),
            ("wl1", [128, F], F32R))
        w_hi, w_lo = (wh0, wh1), (wl0, wl1)
        xT5, hT5 = lifetime(("xT5", [128, TOK], F32), ("hT5", [128, FT, TOK], F32))
        qbk_dram = nc.dram_tensor("qbk_dram", (B, H, L), F32, kind="Internal").ap()

        ar4 = arena[:, :].rearrange("p (n c) -> p n c", n=4)
        rq, rk, rv, rm = (ar4[:, n, :] for n in range(4))
        e0 = arena[:, 0:S]
        e0T = arena[0:KT, S:S + NT * 128].rearrange("p (t n) -> p t n", n=128)
        qf0 = arena[:, S + NT * 128:S + NT * 128 + TOK]
        hT = ar4
        lT, rT, eb, ebT = (ar4[:, n, :] for n in range(4))
        rec = qrow[0:L, 2, 0:HH]
        qbkT = arena[0:H, TOK:2 * TOK]
        u0 = w1b[0:C + 1, :, :].rearrange("p a b -> p (a b)")
        qbk_row = [qrow[C:C + 1, n, :] for n in range(2)]
        mrow = qrow[C:C + 1, 2, :]
        wret = w1b[:, 1, :].rearrange("p (n c) -> p n c", n=4)
        wrkr = w2b[:, 1, 0:128]
        wT = qT
        wk_raw = [Y[0:C, n, :] for n in range(2)]
        vrows = Y[0:NVEC, 2, :]

        def cn_tile(s, k, lo, hi):
            return cn[:, s, k * 129 + lo:k * 129 + hi]

        def cn_cols(s, lo, hi):
            return cn[:, s, :].rearrange("p (t n) -> p t n", n=129)[:, :, lo:hi]

        def ctx_rows(b):
            return t["ctx_512"][b].rearrange("(p t) d -> p t d", t=NT)

        def banks(b):
            return ps[:, b:b + 2, :].rearrange("p b (t n) -> p (b t) n", n=128)

        x_in = sem("x_in")
        ret_in = sem("ret_in")
        vec_in = sem("vec_in")
        w0_in = sem("w0_in")
        w1_in = sem("w1_in")
        moe_in = sem("moe_in")
        ctx_in = [sem(f"ctx_in{s}") for s in range(NCN)]
        w1b_in = [sem(f"w1b_in{s}") for s in range(2)]
        w2b_in = [sem(f"w2b_in{s}") for s in range(2)]
        ffn_in = sem("ffn_in")
        ct_in = [sem(f"ct_in{s}") for s in range(2)]
        qrow_in = [sem(f"qrow_in{s}") for s in range(2)]
        qbk_out = sem("qbk_out")
        out_done = sem("out_done")
        pool_set = sem("pool_set")
        x_pad = sem("x_pad")
        xt_ps = sem("xt_ps")
        xt_ready = sem("xt_ready")
        vec_ps = sem("vec_ps")
        vec_ready = sem("vec_ready")
        dve_step = sem("dve_step")
        ve_ready = sem("ve_ready")
        rstd_ready = sem("rstd_ready")
        x_norm = sem("x_norm")
        rot_ready = sem("rot_ready")
        ret_ps = sem("ret_ps")
        ret_read = sem("ret_read")
        rv_ready = sem("rv_ready")
        q_ps = sem("q_ps")
        q_ready = sem("q_ready")
        qf_ps = sem("qf_ps")
        qf_ready = sem("qf_ready")
        qbk_ps = sem("qbk_ps")
        qbk_ready = sem("qbk_ready")
        dup_ready = sem("dup_ready")
        t_ps = sem("t_ps")
        ct_hi = sem("ct_hi")
        ct_ready = sem("ct_ready")
        sthi_ready = sem("sthi_ready")
        stlo_ready = sem("stlo_ready")
        s0_ps = sem("s0_ps")
        m0_step = sem("m0_step")
        shift0 = sem("shift0")
        e0_ready = sem("e0_ready")
        e0t_ps = sem("e0t_ps")
        e0t_act = sem("e0t_act")
        e0t_dve = sem("e0t_dve")
        u0_ps = sem("u0_ps")
        u0_ready = sem("u0_ready")
        o0_ps = sem("o0_ps")
        gate_ps = sem("gate_ps")
        top_ready = sem("top_ready")
        e2_ready = sem("e2_ready")
        b1_ready = sem("b1_ready")
        wexp_ready = sem("wexp_ready")
        wt_ps = sem("wt_ps")
        wt_ready = sem("wt_ready")
        b2_ps = sem("b2_ps")
        y_init = sem("y_init")
        w_hi_ready = sem("w_hi_ready")
        w_lo_ready = sem("w_lo_ready")
        xh_ready = sem("xh_ready")
        xl_ready = sem("xl_ready")
        h_ps = sem("h_ps")
        h_ready = sem("h_ready")
        eo_ps = sem("eo_ps")
        eo_read = sem("eo_read")
        lr_ready = sem("lr_ready")
        sa_ps = sem("sa_ps")
        sa_sub = sem("sa_sub")
        eb_zero = sem("eb_zero")
        sa_exp = sem("sa_exp")
        ebt_ps = sem("ebt_ps")
        ebt_ready = sem("ebt_ready")
        sao_ps = sem("sao_ps")
        bkh_ready = sem("bkh_ready")
        q1_ps = sem("q1_ps")
        q1_ready = sem("q1_ready")
        qbkT_ps = sem("qbkT_ps")
        qbkT_ready = sem("qbkT_ready")
        qbd_ready = sem("qbd_ready")
        qfold = sem("qfold")
        qhi_ready = sem("qhi_ready")
        qlo_ready = sem("qlo_ready")
        mx_ps = sem("mx_ps")
        mx_read = sem("mx_read")
        tm_ready = sem("tm_ready")
        tm_row = sem("tm_row")
        m_ready = sem("m_ready")
        aux_ready = sem("aux_ready")
        st_ps = sem("st_ps")
        e1_ready = sem("e1_ready")
        elo_pool = sem("elo_pool")
        elo_dve = sem("elo_dve")
        wv_split = sem("wv_split")
        vhi_ready = sem("vhi_ready")
        pv_done = sem("pv_done")
        u1_ready = sem("u1_ready")
        oh_ps = sem("oh_ps")
        rec_ready = sem("rec_ready")
        cat_ready = sem("cat_ready")
        catT_ps = sem("catT_ps")
        catT_ready = sem("catT_ready")
        wo_ps = sem("wo_ps")
        y1_ready = sem("y1_ready")
        xb_ready = sem("xb_ready")
        f_ps = sem("f_ps")
        f_ready = sem("f_ready")
        fo_ps = sem("fo_ps")

        NB1 = B // 2

        def wait_low(eng, g, u):
            if u < 0:
                g, u = g - 1, u + NT
            n = len(DVE_LOWS)
            if u in DVE_LOWS:
                wait_count(eng, elo_dve, n * g + lows_before(u) + 1)
            else:
                wait_count(eng, elo_pool, (NT - n) * g + u - lows_before(u) + 1)

        def low_exp(eng, g, u):
            n = NT * g + u
            eng.wait_ge(e1_ready, n + 1)
            wait_count(eng, pv_done, n - 2)
            return eng.tensor_tensor(e1_lo[:, u % 3, :], e1[:, u % 3, :], e1_hi[:, u % 3, :].bitcast(F32),
                                     ALU.subtract)

        block = ctx.enter_context(nc.Block())

        @block.sync
        def _(sp):
            def load(dst, src, s):
                sp.dma_start(dst, src).then_inc(s, 16)

            sp.wait_ge(x_pad, 1)
            xs = t["x"].rearrange("(r two) l d -> two l r d", two=2)
            load(X[0:L, :, :], xs[0], x_in)
            load(X[SLOT:SLOT + L, :, :], xs[1], x_in)
            load(wret[:, 0, :], t["L0_attn_W_Q"], ret_in)
            load(wret[:, 1, :], t["L0_attn_W_K"], ret_in)
            load(wret[:, 2, :], t["L0_attn_W_V"], ret_in)
            load(kc[:, :], consts[:, 0:NCONST], ret_in)
            for b in range(NCN):
                load(cn_cols(b, 64, 128), ctx_rows(b), ctx_in[b])
            rows = [("L0_xattn_bq", V_BQ0), ("L0_xattn_bk", V_BK0), ("L1_xattn_bq", V_BQ1), ("L1_xattn_bk", V_BK1)]
            for name, r in rows:
                load(vrows[r:r + 1, :], t[name].rearrange("(o n) -> o n", o=1), vec_in)
            load(vrows[V_WL:V_WL + 1, :], t["L1_attn_w_lhs"].rearrange("a b n -> (a b) n"), vec_in)
            load(vrows[V_WR:V_WR + 1, :], t["L1_attn_w_rhs"].rearrange("a b n -> (a b) n"), vec_in)
            load(vrows[V_FB1:V_FB1 + FT, :], t["L1_ffn_b1"].rearrange("(f n) -> f n", n=128), vec_in)
            load(vrows[V_EB1:NVEC, :], t["L0_ffn_b1"].rearrange("e (f n) -> (e f) n", n=128), vec_in)
            load(wk_raw[0], t["L0_xattn_Wk"], vec_in)
            load(wk_raw[1], t["L1_xattn_Wk"], vec_in)
            load(wq0[:, :], t["L0_xattn_Wq"], w0_in)
            load(wv0[0:C, :], t["L0_xattn_Wv"], w0_in)
            load(wv0[C:C + 1, :], t["L0_xattn_bv"].rearrange("(o n) -> o n", o=1), w0_in)
            load(wg[:, :], t["L0_ffn_Wg"], moe_in)
            load(bg_b[:, :], t["L0_ffn_bg"].rearrange("(o n) -> o n", o=1).to_broadcast([128, NE]), moe_in)
            load(eb2[:, :], t["L0_ffn_b2"], moe_in)
            load(wq1[:, :], t["L1_xattn_Wq"], w1_in)
            load(wo[:, :], t["L1_xattn_Wo"], w1_in)
            load(wv_raw[0:C, :], t["L1_xattn_Wv"], w1_in)
            load(wv_raw[C:2 * C, :], t["L1_xattn_Wv"], w1_in)
            load(sel1[0:C, :, :], consts[0:C, K_SEL:NALL].rearrange("c (h d) -> c h d", d=DH + 1), w1_in)
            load(sel1[C:C + 1, :, 0:DH], t["L1_xattn_bv"].rearrange("(o h d) -> o h d", o=1, d=DH), w1_in)
            load(fw1[:, :], t["L1_ffn_W1"], ffn_in)
            load(fw2[:, :].rearrange("p (f n) -> p f n", n=128), t["L1_ffn_W2"].rearrange("(f p) n -> p f n", p=128),
                 ffn_in)
            load(bo_b[:, :], t["L1_xattn_bo"].rearrange("(o n) -> o n", o=1).to_broadcast([128, 128]), w1_in)
            load(fb2_b[:, :], t["L1_ffn_b2"].rearrange("(o n) -> o n", o=1).to_broadcast([128, 128]), w1_in)

            for b in range(NCN, B):
                sp.wait_ge(u0_ps, (b - NCN) // 2 + 1)
                load(cn_cols(b % NCN, 64, 128), ctx_rows(b), ctx_in[b % NCN])

            def context(i, s):
                wait_count(sp, pv_done, 48 * i + 24 * s - 24)
                b = 2 * i + s
                load(ct_w[:, s, :].bitcast(F32), ct_all[:, b, :].bitcast(F32), ct_in[s])
                load(ct_1[0:C, s, :].bitcast(F32), ct_all[0:C, b, :].bitcast(F32), ct_in[s])

            def bias_rows(i, s):
                for hf in range(2):
                    wait_count(sp, aux_ready, 4 * i + 2 * s + hf - 1)
                    load(qbk_row[hf].rearrange("o (h q) -> o h q", q=L),
                         qbk_dram[bass.ts(2 * i + s, 1), hf * HH:(hf + 1) * HH, :], qrow_in[hf])

            def experts(i):
                for s in range(2):
                    if isinstance(i, int):
                        sp.wait_ge(o0_ps, 2)
                    else:
                        sp.wait_ge(w_lo_ready, 2 * i - 1 + s)
                    load(w1b[:, s, :], t["L0_ffn_W1"][2 * i + s], w1b_in[s])
                for s in range(2):
                    if not isinstance(i, int):
                        sp.wait_ge(eo_ps, 4 * i - 2 + 2 * s)
                    load(w2b[:, s, :].rearrange("p (f n) -> p f n", n=128),
                         t["L0_ffn_W2"][2 * i + s].rearrange("(f p) n -> p f n", p=128), w2b_in[s])
            experts(0)
            sp.wait_ge(ct_ready, 6 * PAIRS)
            context(0, 0)
            with sp.Fori(1, NE // 2) as i:
                experts(i)

            sp.wait_ge(eo_ps, 2 * NE)
            context(0, 1)

            sp.wait_ge(qbkT_ready, 2)
            sp.dma_start(qbk_dram.rearrange("b h q -> h b q"),
                         qbkT.rearrange("h (b q) -> h b q", q=SLOT)[:, :, 0:L]).then_inc(qbk_out, 16)
            sp.wait_ge(qbk_out, 16)
            for s in range(2):
                bias_rows(0, s)
            with sp.Fori(1, NB1) as i:
                for s in range(2):
                    context(i, s)
                    bias_rows(i, s)


            sp.wait_ge(x_norm, 12)
            os = out.rearrange("(r two) l d -> two l r d", two=2)
            load(os[0], X[0:L, :, :], out_done)
            load(os[1], X[SLOT:SLOT + L, :, :], out_done)
            sp.wait_ge(out_done, 32)

        @block.gpsimd
        def _(g):
            g.memset(ident[:, :], 0.0).then_inc(pool_set, 1)
            g.memset(ones[:, :], 1.0).then_inc(pool_set, 1)
            g.memset(mhalf[:, :], -0.5).then_inc(pool_set, 1)
            g.memset(base_e[:, :], float(np.e)).then_inc(pool_set, 1)
            g.memset(cn[:, :, :].rearrange("p s (t n) -> p (s t) n", n=129)[:, :, 128:129], 1.0).then_inc(pool_set, 1)
            g.wait_ge(pool_set, 5)
            g.affine_select(out=ident[:, :], in_=ident[:, :], compare_op=ALU.not_equal, fill=1.0, base=0,
                            pattern=[[-1, 128]], channel_multiplier=1).then_inc(pool_set, 1)
            g.memset(st_hi[:, :, :].bitcast(F32), 0.0).then_inc(pool_set, 1)
            g.memset(st_lo[:, :, :].bitcast(F32), 0.0).then_inc(pool_set, 1)
            g.memset(gate[:, :, :], NEG).then_inc(pool_set, 1)
            g.memset(wexp[:, :, :], 0.0).then_inc(pool_set, 1)
            g.memset(vecT[:, NVEC:NVEC + FT], 0.0).then_inc(pool_set, 1)

            def power(k):
                for n in range(2):
                    g.wait_ge(ve_ready, 2 * k + n + 1)
                    g.tensor_tensor(rstd[:, 4 * n:4 * n + 4], ve[:, 4 * n:4 * n + 4], mhalf[:, 0:4], ALU.pow)\
                        .then_inc(rstd_ready, 1)

            def double(b):
                one = ones[0:KT, 0:1].unsqueeze(1).to_broadcast([KT, NT, 64])
                g.wait_ge(ctx_in[b % NCN], 16 * (b // NCN) + 16)
                g.tensor_tensor(cn_cols(b % NCN, 0, 64), cn_cols(b % NCN, 64, 128), one, ALU.mult)\
                    .then_inc(dup_ready, 1)

            for b in range(NCN):
                if b == 2:
                    power(0)
                double(b)
            for b in range(NCN, B):
                double(b)
            power(1)

            def split_weights(i, s):
                e = 2 * i + s
                g.wait_ge(w1b_in[s], 16 * i + 16)
                wait_count(g, h_ps, 8 * e - 8)
                g.tensor_tensor(w_hi[s][:, :], w1b[:, s, :], ones[:, 0:1].to_broadcast([128, F]), ALU.mult)\
                    .then_inc(w_hi_ready, 1)
                g.wait_ge(w_hi_ready, e + 1)
                g.tensor_tensor(w_lo[s][:, :], w1b[:, s, :], w_hi[s][:, :].bitcast(F32), ALU.subtract)\
                    .then_inc(w_lo_ready, 1)

            split_weights(0, 0)
            g.wait_ge(top_ready, 1)
            g.tensor_tensor(sm[:, 3, :], base_e[:, :], sm[:, 3, :], ALU.pow).then_inc(e2_ready, 1)
            split_weights(0, 1)
            with g.Fori(1, NE // 2) as i:
                for s in range(2):
                    split_weights(i, s)
            power(2)
            g.wait_ge(lr_ready, 2)
            g.memset(eb, 0.0).then_inc(eb_zero, 1)
            power(3)

            def low_exps(i):
                for k in range(4):
                    for u in range(NT):
                        if u not in DVE_LOWS:
                            low_exp(g, 4 * i + k, u).then_inc(elo_pool, 1)

            peeled(g, NB1, low_exps)
            power(4)
            power(5)

        @block.tensor
        def _(pe):
            def transpose_state(k):
                for n in range(PAIRS):
                    if n % 4 == 0:
                        wait_count(pe, x_norm, 2 * k - 1 + n // 4 if k else 0)
                    ins = pe.transpose(ps[:, n // 4, (n % 4) * 128:(n % 4 + 1) * 128], X[:, n, :], ident[:, :])
                    if n % 4 == 3:
                        ins.then_inc(xt_ps, 1)

            def wide(bank, w, x):
                for n in range(2):
                    ins = pe.matmul(ps[:, bank + n, :], w, x[:, n * 512:(n + 1) * 512], start=True, stop=True)
                return ins

            def keep_warm(bank, n):
                for _ in range(n):
                    pe.matmul(ps[:, bank, 0:128], ones[:, :], ones[:, :], start=True, stop=True)

            pe.wait_ge(pool_set, 6)
            keep_warm(7, 8)
            pe.wait_ge(x_in, 32)
            transpose_state(0)
            keep_warm(7, 2)

            pe.wait_ge(xt_ready, 2)
            pe.wait_ge(ret_in, 16 * 4)
            wide(3, wret[:, 0, :], xT).then_inc(ret_ps, 1)
            pe.wait_ge(rot_ready, 2)
            wide(5, wret[:, 3, :], xT).then_inc(ret_ps, 1)
            for n, bank in ((0, 7), (1, 0)):
                ins = pe.matmul(ps[:, bank, :], wret[:, 1, :], xT[:, n * 512:(n + 1) * 512], start=True, stop=True)
            ins.then_inc(ret_ps, 1)
            pe.wait_ge(rot_ready, 4)
            pe.wait_ge(ret_read, 1)
            wide(1, wrkr, xT).then_inc(ret_ps, 1)
            for n in range(PAIRS):
                ins = pe.matmul(banks(3)[:, n, :], xT[:, n * 128:(n + 1) * 128], wret[:, 2, :], start=True, stop=True)
            ins.then_inc(ret_ps, 1)
            pe.wait_ge(vec_in, 16 * 10)
            pe.wait_ge(ret_read, 3)
            pe.transpose(ps[:, 7, 0:NVEC], vrows, ident[0:NVEC, 0:NVEC])
            pe.transpose(ps[:, 7, 64:128], wk_raw[0], ident[0:C, 0:C])
            pe.transpose(ps[:, 7, 128:192], wk_raw[1], ident[0:C, 0:C]).then_inc(vec_ps, 1)
            pe.wait_ge(ret_read, 4)
            for n in range(PAIRS):
                ins = pe.matmul(banks(5)[:, n, :], rk[:, n * 128:(n + 1) * 128], rq[:, n * 128:(n + 1) * 128],
                                start=True, stop=True)
            ins.then_inc(ret_ps, 1)
            pe.wait_ge(ret_read, 5)
            pe.wait_ge(rv_ready, 1)
            for n in range(PAIRS):
                ins = pe.matmul(banks(3)[:, n, :], rm[:, n * 128:(n + 1) * 128], rv[:, n * 128:(n + 1) * 128],
                                start=True, stop=True)
                if n % 4 == 3:
                    ins.then_inc(ret_ps, 1)

            def turn_context(p, h, m):
                j, c = divmod(m, NCH)
                if c == 0:
                    pe.wait_ge(dup_ready, 2 * p + j + 1)
                if not (isinstance(p, int) and p == 0):
                    pe.wait_ge(ct_ready, 6 * p + m - 1)
                for k in range(TPC):
                    ins = pe.transpose(ps[:, context_bank(p, m), k * KT:(k + 1) * KT],
                                       cn_tile(2 * h + j, c * TPC + k, 0, 128), ident[0:KT, 0:KT])
                ins.then_inc(t_ps, 1)

            pe.wait_ge(vec_ready, 3)
            for m in range(4):
                turn_context(0, 0, m)
            keep_warm(0, 10)
            transpose_state(1)
            pe.wait_ge(w0_in, 16 * 3)
            for n in range(2):
                pe.wait_ge(xt_ready, 3 + n)
                pe.matmul(ps[:, 3 + n, :], wq0[:, :], xT[:, n * 512:(n + 1) * 512], start=True, stop=True)\
                    .then_inc(q_ps, 1)
            for m in range(4, 6):
                turn_context(0, 0, m)
            pe.wait_ge(ct_ready, 4)
            for n in range(2):
                pe.wait_ge(q_ready, n + 1)
                pe.matmul(ps[:, 5 + n, :], wkT0[:, :], qT[:, n * 512:(n + 1) * 512], start=True, stop=True)\
                    .then_inc(qf_ps, 1)
            for n in range(PAIRS):
                ins = pe.matmul(ps[:, 7, n:n + 1], qT[:, n * 128:(n + 1) * 128], vecT[:, V_BK0:V_BK0 + 1],
                                start=True, stop=True)
            ins.then_inc(qbk_ps, 1)

            def turn_exp(p, c):
                pe.wait_ge(e0_ready, 3 * p + c + 1)
                if c == 1:
                    wait_count(pe, e0t_act, p)
                else:
                    wait_count(pe, e0t_dve, 2 * p + c // 2)
                for k in range(TPC):
                    ins = pe.transpose(ps[0:KT, 5 + c % 2, k * 128:(k + 1) * 128],
                                       e0[:, (c * TPC + k) * KT:(c * TPC + k + 1) * KT], ident[:, :])
                ins.then_inc(e0t_ps, 1)

            def weigh0(p, h, j):
                if j == 0:
                    pe.wait_ge(e0t_act, p + 1)
                    pe.wait_ge(e0t_dve, 2 * p + 2)
                    wait_count(pe, u0_ready, p)
                for k in range(NT):
                    ins = pe.matmul(ps[0:C + 1, 7, j * 64:(j + 1) * 64], cn_tile(2 * h + j, k, 64, 129),
                                    e0T[:, k, j * 64:(j + 1) * 64], start=(k == 0), stop=(k == NT - 1))
                if j == 1:
                    ins.then_inc(u0_ps, 1)

            def attend0(p, h):
                h1, h0 = (h + 1) % 3, (h - 1) % 3
                first, last = isinstance(p, int) and p == 0, isinstance(p, int) and p == PAIRS - 1
                pe.wait_ge(stlo_ready, p + 1)
                for c in range(NCH):
                    pe.wait_ge(ct_ready, 6 * p + NCH + c + 1)
                    wait_count(pe, e0_ready, 3 * p - 2 + c)
                    for n, (j, q) in enumerate(((0, st_hi), (0, st_lo), (1, st_hi), (1, st_lo))):
                        ins = pe.matmul(ps[:, 2 + c, 0:CHUNK], q[:, j, :],
                                        ct_all[:, 2 * p + j, c * CHUNK:(c + 1) * CHUNK],
                                        start=(n == 0), stop=(n == 3))
                    ins.then_inc(s0_ps, 1)
                for what, m in (("context", 0), ("sums", 0), ("context", 1), ("sums", 1), ("context", 2),
                                ("context", 3), ("exp", 0), ("context", 4), ("exp", 1), ("context", 5), ("exp", 2)):
                    if what == "context" and not last:
                        turn_context(p + 1, h1, m)
                    if what == "sums" and not first:
                        weigh0(p - 1, h0, m)
                    if what == "exp":
                        turn_exp(p, m)

            pe.wait_ge(qf_ready, 2)
            pe.wait_ge(qbk_ready, 1)
            pairs_loop(pe, attend0)
            for j in range(2):
                weigh0(PAIRS - 1, (PAIRS - 1) % 3, j)
            pe.wait_ge(u0_ready, PAIRS)
            for n in range(PAIRS):
                ins = pe.matmul(banks(0)[:, n, :], u0[:, n * 128:(n + 1) * 128], wv0[:, :], start=True, stop=True)
                if n % 4 == 3:
                    ins.then_inc(o0_ps, 1)

            keep_warm(7, 16)
            transpose_state(2)
            pe.wait_ge(moe_in, 16 * 3)
            def gates():
                for n in range(PAIRS):
                    if n % 4 == 0:
                        pe.wait_ge(xt_ready, 5 + n // 4)
                    ins = pe.matmul(ps[:, 4, n * 8:n * 8 + NE], xT[:, n * 128:(n + 1) * 128], wg[:, :], start=True,
                                    stop=True)
                ins.then_inc(gate_ps, 1)

            def hidden(e, s, ms):
                for m in ms:
                    f, n = divmod(m, 2)
                    if m == 0:
                        pe.wait_ge(w_lo_ready, e + 1)
                    if isinstance(e, int) and e == 0 and f == 0:
                        pe.wait_ge(xl_ready, n + 1)
                    wait_count(pe, h_ready, 8 * e + m - 3)
                    cols, toks = slice(f * 128, (f + 1) * 128), slice(n * 512, (n + 1) * 512)
                    pe.matmul(ps[:, m % 4, :], w_hi[s][:, cols], xh[:, toks], start=True, stop=False)
                    pe.matmul(ps[:, m % 4, :], w_lo[s][:, cols], xh[:, toks], start=False, stop=False)
                    pe.matmul(ps[:, m % 4, :], w_hi[s][:, cols], xl[:, toks], start=False, stop=True)\
                        .then_inc(h_ps, 1)
                    if isinstance(e, int) and e == 0 and n == 1:
                        second_biases(f)

            def second_biases(f):
                if f == 2:
                    pe.wait_ge(wexp_ready, 1)
                    for n in range(PAIRS):
                        ins = pe.transpose(ps[0:8, 6 + n // 4, (n % 4) * 128:(n % 4 + 1) * 128], wexp[:, n, :],
                                           ident[:, :])
                    ins.then_inc(wt_ps, 1)
                if f == FT - 1:
                    pe.wait_ge(wt_ready, 1)
                    for n in range(PAIRS):
                        ins = pe.matmul(banks(4)[:, n, :], wT[0:NE, n * 128:(n + 1) * 128], eb2[:, :],
                                        start=True, stop=True)
                    ins.then_inc(b2_ps, 1)

            def expert_out(e, s):
                pe.wait_ge(h_ready, 8 * e + 8)
                wait_count(pe, eo_read, 2 * e - 2)
                if isinstance(e, int) and e == 1:
                    pe.wait_ge(y_init, 1)
                pe.wait_ge(w2b_in[s], 8 * (e - s) + 16)
                for n in range(PAIRS):
                    for f in range(FT):
                        ins = pe.matmul(banks(6 - 2 * s)[:, n, :], hT[:, f, n * 128:(n + 1) * 128],
                                        w2b[:, s, f * 128:(f + 1) * 128], start=(f == 0), stop=(f == FT - 1))
                    if n % 4 == 3:
                        ins.then_inc(eo_ps, 1)

            def experts(i):
                for s in range(2):
                    e = 2 * i + s
                    hidden(e, s, range(2, 2 * FT))
                    if not (isinstance(e, int) and e == NE - 1):
                        hidden(e + 1, 1 - s, range(2))
                    expert_out(2 * i + s, s)

            gates()
            hidden(0, 0, range(2))
            experts(0)
            with pe.Fori(1, NE // 2 - 1) as i:
                experts(i)
            experts(NE // 2 - 1)

            def values(s, c, n, bank):
                wait_count(pe, mx_read, n - 1)
                for j in range(TPC):
                    keys = slice((c * TPC + j) * KT, (c * TPC + j + 1) * KT)
                    o = ps[0:KT, bank, j * 128:(j + 1) * 128]
                    pe.matmul(o, ct_w[:, s, keys], wv_hi[:, :], start=True, stop=False)
                    ins = pe.matmul(o, ct_1[0:C, s, keys], wv_lo[:, :], start=False, stop=True)
                ins.then_inc(mx_ps, 1)

            keep_warm(2, 16)
            transpose_state(3)
            pe.wait_ge(lr_ready, 2)
            for n in range(PAIRS):
                for j in range(2):
                    o = n * 128 + j * 64
                    ins = pe.matmul(ps[j * 64:j * 64 + 64, 2, n * L:(n + 1) * L], lT[:, o:o + 64], rT[:, o:o + L],
                                    start=True, stop=True)
            ins.then_inc(sa_ps, 1)
            pe.wait_ge(ct_in[0], 32)
            pe.wait_ge(wv_split, 2)
            for c in range(NCH):
                values(0, c, c, 5 + c)
            pe.wait_ge(sa_exp, 2)
            for n in range(PAIRS):
                ins = pe.transpose(banks(3)[:, n, :], eb[:, n * 128:(n + 1) * 128], ident[:, :])
            ins.then_inc(ebt_ps, 1)
            pe.wait_ge(ebt_ready, 1)
            pe.wait_ge(mx_read, NCH)
            for n in range(PAIRS):
                ins = pe.matmul(banks(5)[:, n, :], ebT[:, n * 128:(n + 1) * 128], X[:, n, :], start=True, stop=True)
                if n % 4 == 3:
                    ins.then_inc(sao_ps, 1)

            keep_warm(2, 16)
            transpose_state(4)
            pe.wait_ge(w1_in, 16 * 8)
            for n in range(2):
                pe.wait_ge(xt_ready, 9 + n)
                pe.matmul(ps[:, 2 + n, :], wq1[:, :], xT[:, n * 512:(n + 1) * 512], start=True, stop=True)\
                    .then_inc(q1_ps, 1)

            def bias_products(n):
                pe.wait_ge(q1_ready, 2)
                pe.wait_ge(bkh_ready, 1)
                pe.matmul(ps[0:H, 3 + n, :], bkh[:, :], qT[:, n * 512:(n + 1) * 512], start=True, stop=True)\
                    .then_inc(qbkT_ps, 1)

            def fold(g, k):
                pe.wait_ge(qbd_ready, g + 1)
                pe.matmul(ps[:, 7, 0:QC], wkT1[:, :], qbd[:, :], start=True, stop=True).then_inc(qfold, 1)

            def scores_for_max(k, u, n, bank):
                r, c = divmod(u, NCH)
                wait_count(pe, mx_read, n - 1)
                pe.matmul(ps[0:RR, bank, 0:CHUNK], q_hi[:, k, r * RR:(r + 1) * RR],
                          ct_w[:, (k // 2) % 2, c * CHUNK:(c + 1) * CHUNK], start=True, stop=True).then_inc(mx_ps, 1)

            def scores(g, k, u):
                n = 12 * g + u
                s = (k // 2) % 2
                wait_count(pe, e1_ready, n - 2)
                bank = ps[0:KT, u % 3, 0:QC]
                pe.matmul(bank, ct_w[:, s, u * KT:(u + 1) * KT], q_hi[:, k, :], start=True, stop=False)
                if u == 0:
                    pe.wait_ge(aux_ready, g + 1)
                pe.matmul(bank, ct_1[:, s, u * KT:(u + 1) * KT], q_lo[:, k, :], start=False, stop=True)\
                    .then_inc(st_ps, 1)

            def heads(g, k):
                if isinstance(g, int) and g == 2 * B - 1:
                    pe.wait_ge(cat_ready, 2 * B - 1)
                elif isinstance(g, int) and g == 2 * B - 2:
                    pe.wait_ge(y1_ready, B - 1)
                elif isinstance(g, int) and g == 2 * B - 3:
                    pe.wait_ge(cat_ready, 2 * B - 3)
                else:
                    pe.wait_ge(qlo_ready, g + 4)
                pe.wait_ge(u1_ready, g + 1)
                for h in range(HH):
                    ins = pe.matmul(ps[0:L, 7, h * (DH + 1):(h + 1) * (DH + 1)], u1[:, k % 2, h * L:(h + 1) * L],
                                    sel1[:, (k % 2) * HH + h, :], start=True, stop=True)
                ins.then_inc(oh_ps, 1)

            def turn_heads(b):
                pe.wait_ge(cat_ready, 2 * b + 2)
                pe.transpose(ps[:, 7, 0:128], cat[:, :], ident[:, :]).then_inc(catT_ps, 1)

            def project(b, j):
                pe.wait_ge(catT_ready, b + 1)
                pe.matmul(ps[64 * j:64 * j + L, 7, 0:128], catT[:, :], wo[:, :], start=True, stop=True)\
                    .then_inc(wo_ps, 1)

            def half(i, k, before, after, after2):
                g = 4 * i + k
                k1, k2, k0 = (k + 1) % 4, (k + 2) % 4, (k - 1) % 4
                done = 2 * i + k // 2 - 1
                for u in range(NT):
                    if u < NT - 2:
                        scores(g, k, u + 2)
                    elif after:
                        scores(g + 1, k1, u + 2 - NT)
                    m = unit_at(k, u)
                    if u < NT - AHEAD and after:
                        scores_for_max(k1, AHEAD + u, unit_base(i, k) + m, unit_bank(k, m))
                    elif u >= NT - AHEAD and after2:
                        if u == NT - AHEAD:
                            pe.wait_ge(qhi_ready, g + 3)
                            if k % 2 == 0:
                                pe.wait_ge(ct_in[k2 // 2], 32 * (i + 1 + (k2 == 0)))
                        scores_for_max(k2, u - (NT - AHEAD), unit_base(i, k) + m, unit_bank(k, m))
                    if u > 0:
                        weigh(g, k, u - 1)
                    elif before:
                        weigh(g - 1, k0, NT - 1)
                    if u == 0 and after2:
                        if k % 2 == 1:
                            wait_count(pe, y1_ready, 2 * i + k // 2)
                        else:
                            wait_count(pe, cat_ready, g - 1)
                        if isinstance(g, int) and g == 1:
                            pe.wait_ge(qlo_ready, 3)
                        fold(g + 2, k2)
                    if u in (1, 3, 5) and after and k % 2 == 1:
                        m = unit_at(k, u, value=True)
                        values(k1 // 2, u // 2, unit_base(i, k) + m, unit_bank(k, m))
                    if u == 3 and before:
                        heads(g - 1, k0)
                    if u == 5 and before and k % 2 == 0:
                        turn_heads(done)
                    if u == 8 and before and k % 2 == 0:
                        project(done, k0 // 2)
                    if u == 7 and after:
                        maxima_row(g + 1, k1)

            def weigh(g, k, u):
                n = 12 * g + u
                if u == 0:
                    wait_count(pe, u1_ready, g - 1)
                for e in (e1_hi, e1_lo):
                    if e is e1_hi:
                        pe.wait_ge(e1_ready, n + 1)
                    else:
                        wait_low(pe, g, u)
                    for a in range(2):
                        ins = pe.matmul(ps[0:VROWS, 3 + k % 2, a * GC:(a + 1) * GC],
                                        vg[:, (k // 2) % 2, u, 2 * (k % 2) + a, :], e[:, u % 3, a * GC:(a + 1) * GC],
                                        start=(u == 0 and e is e1_hi and a == 0),
                                        stop=(u == NT - 1 and e is e1_lo and a == 1))
                ins.then_inc(pv_done, 1)

            def maxima_row(g, k):
                pe.wait_ge(tm_ready, g + 1)
                wait_count(pe, u1_ready, g - 1)
                for r in range(RT):
                    ins = pe.matmul(ps[C:C + 1, 3 + k % 2, r * RR:(r + 1) * RR], tm[:, r:r + 1], ident[0:RR, 0:RR],
                                    start=True, stop=True)
                ins.then_inc(tm_row, 1)

            def first_max(us):
                for u in us:
                    scores_for_max(0, u, NCH + u, 5 + (NCH + u) % 2)

            fold(0, 0)
            pe.wait_ge(qhi_ready, 1)
            first_max(range(0, 2))
            bias_products(0)
            first_max(range(2, 4))
            bias_products(1)
            pe.wait_ge(qlo_ready, 1)
            fold(1, 1)
            first_max(range(4, NT))
            pe.wait_ge(qlo_ready, 2)
            pe.wait_ge(qbkT_ready, 2)
            maxima_row(0, 0)
            for u in range(AHEAD):
                scores_for_max(1, u, NCH + NT + u, 5 + (NCH + NT + u) % 2)
                if u == 1:
                    scores(0, 0, 0)
                    scores(0, 0, 1)

            def attend1(i):
                for k in range(4):
                    g = 4 * i + k
                    flat = isinstance(i, int)
                    half(i, k, before=not flat or g > 0, after=not flat or g < 2 * B - 1,
                         after2=not flat or g < 2 * B - 2)

            peeled(pe, NB1, attend1)
            weigh(2 * B - 1, 3, NT - 1)
            heads(2 * B - 1, 3)
            turn_heads(B - 1)
            project(B - 1, 1)

            keep_warm(1, 16)
            transpose_state(5)
            pe.wait_ge(ffn_in, 32)
            for f in range(FT):
                for n in range(2):
                    m = 2 * f + n
                    if f == 0:
                        pe.wait_ge(xt_ready, 11 + n)
                    wait_count(pe, f_ready, m - 3)
                    pe.matmul(ps[:, 2 + m % 4, :], fw1[:, f * 128:(f + 1) * 128], xT5[:, n * 512:(n + 1) * 512],
                              start=True, stop=True).then_inc(f_ps, 1)
            pe.wait_ge(f_ready, 8)
            for n in range(PAIRS):
                for f in range(FT):
                    ins = pe.matmul(banks(6)[:, n, :], hT5[:, f, n * 128:(n + 1) * 128],
                                    fw2[:, f * 128:(f + 1) * 128], start=(f == 0), stop=(f == FT - 1))
                if n % 4 == 3:
                    ins.then_inc(fo_ps, 1)

        @block.scalar
        def _(act):
            waited = act.alloc_register("waited")

            def wait_apart(s, value):
                wait_count(act, s, value)
                act.reg_mov(waited, 0)

            def state(k, xT=xT):
                for n in range(2):
                    act.wait_ge(xt_ps, 2 * k + n + 1)
                    act.activation(xT[:, n * 512:(n + 1) * 512], ps[:, n, :], ACT.Copy).then_inc(xt_ready, 1)

            state(0)
            act.wait_ge(ret_ps, 5)
            act.activation(rv.rearrange("p (b n) -> p b n", b=2), ps[:, 3:5, :], ACT.Copy).then_inc(rv_ready, 1)
            act.wait_ge(vec_ps, 1)
            act.activation(vecT[:, 0:NVEC], ps[:, 7, 0:NVEC], ACT.Copy).then_inc(vec_ready, 1)
            for n, w in enumerate((wkT0, wkT1)):
                act.activation(w[:, :].rearrange("p (a c) -> p a c", a=2),
                               ps[:, 7, 64 + 64 * n:128 + 64 * n].unsqueeze(1).to_broadcast([128, 2, 64]),
                               ACT.Copy).then_inc(vec_ready, 1)

            def split_hi(p, m):
                j, c = divmod(m, NCH)
                wait_apart(t_ps, 6 * p + m + 1)
                act.activation(ct_all[:, 2 * p + j, c * CHUNK:(c + 1) * CHUNK], ps[:, context_bank(p, m), 0:CHUNK],
                               ACT.Copy).then_inc(ct_hi, 1)

            for m in range(4):
                split_hi(0, m)
            state(1)
            for n in range(2):
                act.wait_ge(q_ps, n + 1)
                act.activation(qT[:, n * 512:(n + 1) * 512], ps[:, 3 + n, :], ACT.Identity,
                               bias=vecT[:, V_BQ0:V_BQ0 + 1]).then_inc(q_ready, 1)
            for m in range(4, 6):
                split_hi(0, m)
            for n in range(2):
                act.wait_ge(qf_ps, n + 1)
                act.activation(qf0[:, n * 512:(n + 1) * 512], ps[:, 5 + n, :], ACT.Copy).then_inc(qf_ready, 1)

            def stage_hi(p):
                wait_apart(s0_ps, 3 * p)
                act.activation(diag(st_hi), qf0[:, bass.ts(p, 128)].rearrange("p (j n) -> p j n", j=2),
                               ACT.Copy).then_inc(sthi_ready, 1)

            def exp0(p, c):
                act.wait_ge(shift0, p + 1)
                wait_apart(e0t_ps, 3 * p - 2 + c)
                act.activation(e0[:, c * CHUNK:(c + 1) * CHUNK], ps[:, 2 + c, 0:CHUNK], ACT.Exp,
                               bias=sm[:, 1, 0:1], accum_out=esum[:, c, bass.ts(p, 1)]).then_inc(e0_ready, 1)

            def diag(st):
                return st[:, :, :].rearrange("p j n -> p (j n)").rearrange("p (a n) -> p a n", n=64)[:, 0:4:3, :]

            def attend0(p, h):
                last = isinstance(p, int) and p == PAIRS - 1
                if not last:
                    split_hi(p + 1, 0)
                exp0(p, 0)
                if not last:
                    split_hi(p + 1, 1)
                exp0(p, 1)
                exp0(p, 2)
                if not last:
                    split_hi(p + 1, 2)
                    stage_hi(p + 1)
                    for m in range(3, 2 * NCH):
                        split_hi(p + 1, m)
                wait_count(act, u0_ps, p)
                act.wait_ge(e0t_ps, 3 * p + 2)
                act.activation(e0T[:, TPC:2 * TPC, :].rearrange("p t n -> p (t n)"), ps[0:KT, 6, :], ACT.Copy)\
                    .then_inc(e0t_act, 1)

            act.wait_ge(qf_ready, 2)
            act.wait_ge(pool_set, 11)
            stage_hi(0)
            pairs_loop(act, attend0)

            for n in range(2):
                act.wait_ge(xt_ps, 5 + n)
                act.activation(xT[:, n * 512:(n + 1) * 512], ps[:, n, :], ACT.Copy).then_inc(xt_ready, 1)
                act.activation(xh[:, n * 512:(n + 1) * 512], ps[:, n, :], ACT.Copy).then_inc(xh_ready, 1)

            def experts(i):
                for s in range(2):
                    e = 2 * i + s
                    wait_count(act, eo_ps, 2 * e)
                    act.wait_ge(b1_ready, e + 1)
                    for f in range(FT):
                        for n in range(2):
                            m = 8 * e + 2 * f + n
                            act.wait_ge(h_ps, m + 1)
                            act.activation(hT[:, f, n * 512:(n + 1) * 512], ps[:, (2 * f + n) % 4, :], ACT.Gelu,
                                           bias=b1s[:, s, f:f + 1]).then_inc(h_ready, 1)

            experts(0)
            with act.Fori(1, NE // 2) as i:
                experts(i)

            def value_hi(s, c, n, bank):
                act.wait_ge(mx_ps, n + 1)
                act.activation(vg[:, s, c * TPC:(c + 1) * TPC, :, 0:GW],
                               ps[0:KT, bank, :].rearrange("p (t g r) -> p t g r", t=TPC, g=NG), ACT.Copy)\
                    .then_inc(vhi_ready, 1)

            state(3)
            act.wait_ge(sa_sub, 2)
            act.wait_ge(eb_zero, 1)
            for j in range(2):
                r = slice(64 * j, 64 * j + 64)
                act.activation(eb[r, :].rearrange("p (t n) -> p t n", n=128)[:, :, 64 * j:64 * j + L],
                               lT[r, 0:PAIRS * L].rearrange("p (t n) -> p t n", n=L), ACT.Exp).then_inc(sa_exp, 1)
            for c in range(NCH):
                value_hi(0, c, c, 5 + c)
            act.wait_ge(ebt_ps, 1)
            act.activation(ebT.rearrange("p (b n) -> p b n", b=2), ps[:, 3:5, :], ACT.Copy).then_inc(ebt_ready, 1)

            state(4)
            for n in range(2):
                act.wait_ge(q1_ps, n + 1)
                act.activation(qT[:, n * 512:(n + 1) * 512], ps[:, 2 + n, :], ACT.Identity,
                               bias=vecT[:, V_BQ1:V_BQ1 + 1]).then_inc(q1_ready, 1)

            def high(g, k):
                act.wait_ge(qfold, g + 1)
                act.activation(q_hi[:, k, :], ps[:, 7, 0:QC], ACT.Copy).then_inc(qhi_ready, 1)

            def sums(g, k):
                act.wait_ge(pv_done, 12 * g + 12)
                wait_count(act, oh_ps, g - 1)
                act.activation(u1[:, k % 2, :], ps[0:C + 1, 3 + k % 2, 0:QC], ACT.Copy).then_inc(u1_ready, 1)

            def turned(b):
                act.wait_ge(catT_ps, b + 1)
                act.activation(catT[:, :], ps[:, 7, 0:L], ACT.Copy).then_inc(catT_ready, 1)

            def attend1(i):
                for k in range(4):
                    g = 4 * i + k
                    flat = isinstance(i, int)
                    for u in range(NT):
                        n = 12 * g + u
                        act.wait_ge(st_ps, n + 1)
                        if not flat or n > 2:
                            wait_low(act, g, u - 3)
                        act.activation(e1[:, u % 3, :], ps[0:KT, u % 3, 0:QC], ACT.Exp)
                        wait_count(act, pv_done, n - 2)
                        act.activation(e1_hi[:, u % 3, :], ps[0:KT, u % 3, 0:QC], ACT.Exp).then_inc(e1_ready, 1)
                        if u == 1 and (not flat or g > 0):
                            sums(g - 1, k - 1)
                        if u == 2 and (not flat or g < 2 * B - 2):
                            high(g + 2, (k + 2) % 4)
                        if u == 5 and k % 2 == 0 and (not flat or g > 0):
                            turned(2 * i + k // 2 - 1)
                        if u in (2, 4, 6) and k % 2 == 1 and (not flat or g < 2 * B - 1):
                            m = unit_at(k, u - 1, value=True)
                            value_hi(((k + 1) // 2) % 2, u // 2 - 1, unit_base(i, k) + m, unit_bank(k, m))

            high(0, 0)
            for n in range(2):
                act.wait_ge(qbkT_ps, n + 1)
                act.activation(qbkT[:, n * 512:(n + 1) * 512], ps[0:H, 3 + n, :], ACT.Copy).then_inc(qbkT_ready, 1)
            high(1, 1)
            peeled(act, NB1, attend1)
            sums(2 * B - 1, 3)
            turned(B - 1)

            state(5, xT5)
            for f in range(FT):
                for n in range(2):
                    m = 2 * f + n
                    act.wait_ge(f_ps, m + 1)
                    act.activation(hT5[:, f, n * 512:(n + 1) * 512], ps[:, 2 + m % 4, :], ACT.Relu,
                                   bias=vecT[:, V_FB1 + f:V_FB1 + f + 1]).then_inc(f_ready, 1)

        @block.vector
        def _(v):
            steps = [0]

            def step(ins):
                steps[0] += 1
                ins.then_inc(dve_step, 1)
                v.wait_ge(dve_step, steps[0])

            def norm(k, make):
                for n in range(2):
                    ins = make(n)
                    if ins is not None:
                        step(ins)
                    for m in range(4 * n, 4 * n + 4):
                        ins = v.bn_stats(stats[:, m, :], Y[:, m, :])
                    step(ins)
                    for m in range(4 * n, 4 * n + 4):
                        ins = v.bn_aggr(mv[:, m, :], stats[:, m, :])
                    step(ins)
                    v.tensor_scalar(ve[:, 4 * n:4 * n + 4], mv[:, 4 * n:4 * n + 4, 1], EPS, None, ALU.add)\
                        .then_inc(ve_ready, 1)
                for n in range(2):
                    v.wait_ge(rstd_ready, 2 * k + n + 1)
                    for m in range(4 * n, 4 * n + 4):
                        ins = v.tensor_scalar(X[:, m, :], Y[:, m, :], mv[:, m, 0:1], rstd[:, m:m + 1],
                                              ALU.subtract, ALU.mult)
                    ins.then_inc(x_norm, 1)

            def tiles8(a):
                return a.rearrange("p (t n) -> p t n", n=128)

            v.memset(X[:, :, :], 0.0).then_inc(x_pad, 1)
            v.memset(sel1[C:C + 1, :, DH:DH + 1], 1.0).then_inc(x_pad, 1)

            v.wait_ge(ret_in, 16 * 4)
            for src, dst in ((wret[:, 0, :], wret[:, 3, :]), (wret[:, 1, :], wrkr)):
                s2 = src.rearrange("p (i two) -> p i two", two=2)
                d2 = dst.rearrange("p (i two) -> p i two", two=2)
                v.tensor_scalar(d2[:, :, 0], s2[:, :, 1], -1.0, None, ALU.mult).then_inc(rot_ready, 1)
                v.tensor_copy(d2[:, :, 1], s2[:, :, 0]).then_inc(rot_ready, 1)

            def table(c):
                return kc[:, c:c + SLOT].unsqueeze(1).to_broadcast([128, B, SLOT])

            def rotary(dst, raw, rot, cos, sin, unit):
                v.wait_ge(ret_ps, unit + 1)
                for n, bank in enumerate(raw):
                    ins = v.tensor_tensor(dst[:, n * 512:(n + 1) * 512].rearrange("p (b q) -> p b q", q=SLOT),
                                          ps[:, bank, :].rearrange("p (b q) -> p b q", q=SLOT),
                                          table(cos)[:, 0:B // 2, :], ALU.mult)
                ins.then_inc(ret_read, 1)
                v.wait_ge(ret_ps, unit + 2)
                for n, bank in enumerate(rot):
                    ins = v.tensor_tensor(qT[:, n * 512:(n + 1) * 512].rearrange("p (b q) -> p b q", q=SLOT),
                                          ps[:, bank, :].rearrange("p (b q) -> p b q", q=SLOT),
                                          table(sin)[:, 0:B // 2, :], ALU.mult)
                step(ins)
                v.tensor_tensor(dst, dst, qT[:, :], ALU.add).then_inc(ret_read, 1)

            rotary(rq, (3, 4), (5, 6), K_COSQ, K_SINQ, 0)
            v.wait_ge(ret_read, 2)
            rotary(rk, (7, 0), (1, 2), K_COSK, K_SINK, 2)
            v.wait_ge(ret_ps, 6)
            v.tensor_tensor(tiles8(rm), banks(5), kc[:, K_MASK:K_MASK + 128].unsqueeze(1).to_broadcast([128, PAIRS, 128]),
                            ALU.mult).then_inc(ret_read, 1)
            def add_retention(n):
                v.wait_ge(ret_ps, 7 + n)
                h = slice(4 * n, 4 * n + 4)
                return v.tensor_tensor(Y[:, h, :], banks(3)[:, h, :], X[:, h, :], ALU.add)

            norm(0, add_retention)

            def split_lo(p, m):
                j, c = divmod(m, NCH)
                v.wait_ge(ct_hi, 6 * p + m + 1)
                lo = ct_all[64:128, 2 * p + j, c * CHUNK:(c + 1) * CHUNK]
                v.tensor_tensor(lo, ps[64:128, context_bank(p, m), 0:CHUNK], lo.bitcast(F32), ALU.subtract)\
                    .then_inc(ct_ready, 1)

            def diag(st):
                return st[:, :, :].rearrange("p j n -> p (j n)").rearrange("p (a n) -> p a n", n=64)[:, 0:4:3, :]

            def stage_lo(p):
                v.wait_ge(sthi_ready, p + 1)
                v.tensor_tensor(diag(st_lo), qf0[:, bass.ts(p, 128)].rearrange("p (j n) -> p j n", j=2),
                                diag(st_hi).bitcast(F32), ALU.subtract).then_inc(stlo_ready, 1)

            def sums_out(p):
                v.wait_ge(u0_ps, p + 1)
                v.tensor_copy(u0[:, bass.ts(p, 128)], ps[0:C + 1, 7, 0:128]).then_inc(u0_ready, 1)

            def exp_out(p, c):
                wait_count(v, u0_ps, p)
                v.wait_ge(e0t_ps, 3 * p + c + 1)
                v.tensor_copy(e0T[:, c * TPC:(c + 1) * TPC, :].rearrange("p t n -> p (t n)"), ps[0:KT, 5, :])\
                    .then_inc(e0t_dve, 1)

            def attend0(p, h):
                last = isinstance(p, int) and p == PAIRS - 1
                first = isinstance(p, int) and p == 0
                for c in range(NCH):
                    v.wait_ge(s0_ps, 3 * p + c + 1)
                    ins = v.tensor_reduce(sm[:, 4, c:c + 1], ps[:, 2 + c, 0:CHUNK], AX.X, ALU.max)
                ins.then_inc(m0_step, 1)
                v.wait_ge(m0_step, 3 * p + 1)
                v.tensor_reduce(sm[:, 4, 3:4], sm[:, 4, 0:NCH], AX.X, ALU.max).then_inc(m0_step, 1)
                v.wait_ge(m0_step, 3 * p + 2)
                v.tensor_tensor(sm[:, 4, 4:5], sm[:, 4, 3:4], sm[:, 0, bass.ts(p, 1)], ALU.add).then_inc(m0_step, 1)
                v.wait_ge(m0_step, 3 * p + 3)
                v.tensor_tensor(sm[:, 1, 0:1], sm[:, 0, bass.ts(p, 1)], sm[:, 4, 4:5], ALU.subtract).then_inc(shift0, 1)
                if not last:
                    split_lo(p + 1, 0)
                    split_lo(p + 1, 1)
                if not first:
                    sums_out(p - 1)
                if not last:
                    split_lo(p + 1, 2)
                    split_lo(p + 1, 3)
                    stage_lo(p + 1)
                exp_out(p, 0)
                if not last:
                    split_lo(p + 1, 4)
                exp_out(p, 2)
                if not last:
                    split_lo(p + 1, 5)

            for m in range(2 * NCH):
                split_lo(0, m)
            v.wait_ge(qbk_ps, 1)
            v.tensor_copy(sm[:, 0, :], ps[:, 7, 0:PAIRS]).then_inc(qbk_ready, 1)
            stage_lo(0)
            pairs_loop(v, attend0)
            sums_out(PAIRS - 1)
            v.wait_ge(e0_ready, NCH * PAIRS)
            step(v.tensor_reduce(sm[:, 2, :], esum[:, :, :].rearrange("p c n -> p n c"), AX.X, ALU.add))
            step(v.reciprocal(sm[:, 5, :], sm[:, 2, :]))

            def add_cross0(n):
                v.wait_ge(o0_ps, n + 1)
                for m in range(4 * n, 4 * n + 4):
                    ins = v.scalar_tensor_tensor(out=Y[:, m, :], in0=banks(0)[:, m, :], scalar=sm[:, 5, m:m + 1],
                                                 in1=X[:, m, :], op0=ALU.mult, op1=ALU.add)
                return ins

            norm(1, add_cross0)

            def first_bias(e, s):
                v.tensor_scalar(b1s[:, s, :], vecT[:, bass.ds(V_EB1 + FT * e, FT)], 1.0, None, ALU.mult)\
                    .then_inc(b1_ready, 1)

            v.wait_ge(vec_ready, 1)
            first_bias(0, 0)
            for n in range(2):
                half = slice(n * 512, (n + 1) * 512)
                v.wait_ge(xh_ready, n + 1)
                v.tensor_tensor(xl[:, half], xT[:, half], xh[:, half].bitcast(F32), ALU.subtract).then_inc(xl_ready, 1)
            v.wait_ge(pool_set, 11)
            v.wait_ge(gate_ps, 1)
            step(v.tensor_tensor(gate[:, :, 0:NE], ps[:, 4, 0:8 * PAIRS].rearrange("p (t n) -> p t n", n=8)[:, :, 0:NE],
                                 bg_b[:, :].unsqueeze(1).to_broadcast([128, PAIRS, NE]), ALU.add))
            for n in range(PAIRS):
                ins = v.max(top[:, n, :], gate[:, n, :])
            step(ins)
            v.tensor_tensor(sm[:, 3, :], top[:, :, 1], top[:, :, 0], ALU.subtract).then_inc(top_ready, 1)
            for n in range(PAIRS):
                ins = v.max_index(topi[:, n, :], top[:, n, :], gate[:, n, :])
            step(ins)
            step(v.tensor_copy(topf[:, :, :], topi[:, :, 0:2]))
            v.wait_ge(e2_ready, 1)
            step(v.tensor_scalar(sm[:, 6, :], sm[:, 3, :], 1.0, None, ALU.add))
            step(v.reciprocal(sm[:, 6, :], sm[:, 6, :]))
            step(v.tensor_tensor(sm[:, 7, :], sm[:, 3, :], sm[:, 6, :], ALU.mult))
            iota = kc[:, K_IOTA:K_IOTA + NE].unsqueeze(1).to_broadcast([128, PAIRS, NE])

            def spread(a):
                return a.unsqueeze(2).to_broadcast([128, PAIRS, NE])

            v.tensor_tensor(wexp[:, :, 0:NE], iota, spread(topf[:, :, 0]), ALU.is_equal)
            step(v.tensor_tensor(wtmp[:, :, :], iota, spread(topf[:, :, 1]), ALU.is_equal))
            v.tensor_tensor(wexp[:, :, 0:NE], wexp[:, :, 0:NE], spread(sm[:, 6, :]), ALU.mult)
            step(v.tensor_tensor(wtmp[:, :, :], wtmp[:, :, :], spread(sm[:, 7, :]), ALU.mult))
            v.tensor_tensor(wexp[:, :, 0:NE], wexp[:, :, 0:NE], wtmp[:, :, :], ALU.add).then_inc(wexp_ready, 1)
            v.wait_ge(wexp_ready, 1)
            v.wait_ge(wt_ps, 1)
            v.tensor_copy(wT[0:8, :].rearrange("p (b n) -> p b n", b=2), ps[0:8, 6:8, :]).then_inc(wt_ready, 1)
            v.wait_ge(b2_ps, 1)
            v.tensor_tensor(Y[:, :, :], banks(4), X[:, :, :], ALU.add).then_inc(y_init, 1)

            def prepare_cross1():
                v.tensor_scalar(bkh[:, :], kc[:, K_HEAD:K_HEAD + H], vecT[:, V_BK1:V_BK1 + 1], None, ALU.mult)\
                    .then_inc(bkh_ready, 1)
                v.wait_ge(w1_in, 16 * 8)
                v.tensor_copy(wv_hi[:, :], wv_raw[:, :]).then_inc(wv_split, 1)
                v.wait_ge(wv_split, 1)
                v.tensor_tensor(wv_lo[:, :], wv_raw[0:C, :], wv_hi[0:C, :].bitcast(F32), ALU.subtract)
                v.memset(ct_1[C:C + 1, :, :].bitcast(F32), 1.0)
                v.memset(vg[:, 0, :, :, 2 * GW:VROWS].bitcast(F32), 1.0).then_inc(wv_split, 1)

            def add_expert(e, s, n):
                v.wait_ge(eo_ps, 2 * e + n + 1)
                wait_count(v, eo_read, 2 * e - 1 + n)
                for m in range(4 * n, 4 * n + 4):
                    ins = v.scalar_tensor_tensor(out=Y[:, m, :], in0=banks(6 - 2 * s)[:, m, :],
                                                 scalar=wexp[:, m, bass.ts(e, 1)], in1=Y[:, m, :],
                                                 op0=ALU.mult, op1=ALU.add)
                return ins.then_inc(eo_read, 1)

            def experts(i):
                for s in range(2):
                    e = 2 * i + s
                    wait_count(v, eo_read, 2 * e)
                    first_bias(e + 1, 1 - s)
                    if isinstance(i, int) and e == 0:
                        v.wait_ge(y_init, 1)
                    if isinstance(i, int) and e == NE - 1:
                        break
                    for n in range(2):
                        add_expert(e, s, n)
                    if isinstance(i, int) and e == 0:
                        prepare_cross1()

            def add_last_expert(n):
                add_expert(NE - 1, 1, n)
                v.wait_ge(eo_read, 2 * NE - 1 + n)

            experts(0)
            with v.Fori(1, NE // 2 - 1) as i:
                experts(i)
            experts(NE // 2 - 1)
            norm(2, add_last_expert)
            v.memset(vg[:, 1, :, :, 2 * GW:VROWS].bitcast(F32), 1.0).then_inc(wv_split, 1)

            def value_lo(b, s, c, bank):
                v.wait_ge(vhi_ready, 3 * b + c + 1)
                tiles = vg[:, s, c * TPC:(c + 1) * TPC, :, :]
                v.tensor_tensor(tiles[:, :, :, GW:2 * GW], ps[0:KT, bank, :].rearrange("p (t g r) -> p t g r", t=TPC, g=NG),
                                tiles[:, :, :, 0:GW].bitcast(F32), ALU.subtract).then_inc(mx_read, 1)

            v.wait_ge(xt_ready, 8)
            v.tensor_scalar(lT, xT[:, :], vecT[:, V_WL:V_WL + 1], None, ALU.mult).then_inc(lr_ready, 1)
            v.tensor_scalar(rT, xT[:, :], vecT[:, V_WR:V_WR + 1], None, ALU.mult).then_inc(lr_ready, 1)
            v.wait_ge(sa_ps, 1)
            sa = ps[:, 2, 0:PAIRS * L].rearrange("p (t n) -> p t n", n=L)
            step(v.tensor_reduce(sm[:, 4, :], sa, AX.X, ALU.max))
            v.tensor_tensor(lT[:, 0:PAIRS * L].rearrange("p (t n) -> p t n", n=L), sa,
                            sm[:, 4, :].unsqueeze(2).to_broadcast([128, PAIRS, L]), ALU.subtract).then_inc(sa_sub, 2)
            v.wait_ge(sa_exp, 2)
            step(v.tensor_reduce(sm[:, 5, :], tiles8(eb), AX.X, ALU.add))
            step(v.reciprocal(sm[:, 6, :], sm[:, 5, :]))
            for c in range(NCH):
                value_lo(0, 0, c, 5 + c)

            def add_self(n):
                v.wait_ge(sao_ps, n + 1)
                for m in range(4 * n, 4 * n + 4):
                    ins = v.scalar_tensor_tensor(out=Y[:, m, :], in0=banks(5)[:, m, :], scalar=sm[:, 6, m:m + 1],
                                                 in1=X[:, m, :], op0=ALU.mult, op1=ALU.add)
                return ins

            norm(3, add_self)

            v.wait_ge(x_norm, 8)
            v.tensor_tensor(Y[:, :, :], X[:, :, :], bo_b[:, :].unsqueeze(1).to_broadcast([128, PAIRS, 128]), ALU.add)\
                .then_inc(xb_ready, 1)
            v.wait_ge(q1_ready, 1)

            def blocks(g, k, b):
                wait_count(v, qfold, g)
                hf = (k + 3) % 2
                v.tensor_tensor(qbd[:, :].rearrange("p (h q) -> p h q", q=L),
                                qT[:, bass.ds(b * SLOT, L)].unsqueeze(1).to_broadcast([128, HH, L]),
                                kc[:, K_HEAD + hf * HH:K_HEAD + (hf + 1) * HH].unsqueeze(2).to_broadcast([128, HH, L]),
                                ALU.mult).then_inc(qbd_ready, 1)

            def low(g, k):
                v.wait_ge(qhi_ready, g + 1)
                v.tensor_tensor(q_lo[0:C, k, :], ps[0:C, 7, 0:QC], q_hi[0:C, k, :].bitcast(F32), ALU.subtract)\
                    .then_inc(qlo_ready, 1)

            def unit_max(g2, u, n, bank):
                r, c = divmod(u, NCH)
                v.wait_ge(mx_ps, n + 1)
                v.tensor_reduce(tmx[:, g2, r, c:c + 1], ps[0:RR, bank, 0:CHUNK], AX.X, ALU.max).then_inc(mx_read, 1)

            def row_max(g2, n):
                v.wait_ge(mx_read, n + 1)
                v.tensor_reduce(tm[:, :], tmx[:, g2, :, :], AX.X, ALU.max).then_inc(tm_ready, 1)

            def shift(g, k, loads):
                v.wait_ge(qrow_in[k % 2], loads)
                v.wait_ge(tm_row, g + 1)
                v.tensor_tensor(mrow, ps[C:C + 1, 3 + k % 2, 0:QC], qbk_row[k % 2], ALU.add).then_inc(m_ready, 1)
                v.wait_ge(m_ready, g + 1)
                v.tensor_tensor(q_lo[C:C + 1, k, :], qbk_row[k % 2], mrow, ALU.subtract).then_inc(aux_ready, 1)

            def heads_out(g, k):
                v.wait_ge(oh_ps, g + 1)
                o = ps[0:L, 7, 0:HH * (DH + 1)].rearrange("p (h d) -> p h d", d=DH + 1)
                v.reciprocal(rec, o[:, :, DH]).then_inc(rec_ready, 1)
                v.wait_ge(rec_ready, g + 1)
                hf = k % 2
                v.tensor_tensor(cat[0:L, hf * 64:(hf + 1) * 64].rearrange("p (h d) -> p h d", d=DH), o[:, :, 0:DH],
                                rec.unsqueeze(2).to_broadcast([L, HH, DH]), ALU.mult).then_inc(cat_ready, 1)

            def output(b, n, j):
                v.wait_ge(wo_ps, b + 1)
                y = Y[64 * j:64 * j + L, bass.ts(n, 1), :].rearrange("p o n -> p (o n)")
                v.tensor_tensor(y, ps[64 * j:64 * j + L, 7, 0:128], y, ALU.add).then_inc(y1_ready, 1)

            def attend1(i):
                for k in range(4):
                    g = 4 * i + k
                    flat = isinstance(i, int)
                    before, after, after2 = (not flat or g > 0), (not flat or g < 2 * B - 1), (not flat or g < 2 * B - 2)
                    after3 = not flat or g < 2 * B - 3
                    for u in range(NT):
                        if u in (2, 4, 6) and after and k % 2 == 1:
                            c = u // 2 - 1
                            value_lo(2 * i + (k + 1) // 2, ((k + 1) // 2) % 2, c,
                                     unit_bank(k, unit_at(k, u - 1, value=True)))
                        if u in DVE_LOWS:
                            low_exp(v, g, u).then_inc(elo_dve, 1)
                        m = unit_at(k, u)
                        if u < NT - AHEAD and after:
                            unit_max((k + 1) % 2, AHEAD + u, unit_base(i, k) + m, unit_bank(k, m))
                        elif u >= NT - AHEAD and after2:
                            unit_max(k % 2, u - (NT - AHEAD), unit_base(i, k) + m, unit_bank(k, m))
                        if u == 1 and after2:
                            low(g + 2, (k + 2) % 4)
                        if u == 3 and before:
                            heads_out(g - 1, k - 1)
                        if u == NT - AHEAD - 1 and after:
                            row_max((k + 1) % 2, unit_base(i, k) + m)
                        if u == 7 and after:
                            shift(g + 1, (k + 1) % 4, 16 * (2 * i + (k + 1) // 2 + 1))
                        if u == 9 and before and k % 2 == 0:
                            output(2 * i + k // 2 - 1, i - 1 + k // 2, (k // 2 + 1) % 2)
                        if u == 10 and after3:
                            blocks(g + 3, k, 2 * i + (k + 3) // 2)

            blocks(0, 1, 0)
            low(0, 0)
            blocks(1, 2, 0)
            v.wait_ge(q1_ready, 2)
            v.memset(cat[:, :], 0.0)
            for u in range(NT):
                if u == 4:
                    low(1, 1)
                    blocks(2, 3, 1)
                unit_max(0, u, NCH + u, 5 + (NCH + u) % 2)
            row_max(0, NCH + NT - 1)
            shift(0, 0, 16)
            for u in range(AHEAD):
                unit_max(1, u, NCH + NT + u, 5 + (NCH + NT + u) % 2)
            v.wait_ge(xb_ready, 1)
            peeled(v, NB1, attend1)
            heads_out(2 * B - 1, 3)
            output(B - 1, PAIRS - 1, 1)
            v.wait_ge(y1_ready, B)
            norm(4, lambda n: None)

            v.wait_ge(x_norm, 10)
            step(v.tensor_tensor(Y[:, :, :], X[:, :, :], fb2_b[:, :].unsqueeze(1).to_broadcast([128, PAIRS, 128]), ALU.add))

            def add_forward(n):
                v.wait_ge(fo_ps, n + 1)
                h = slice(4 * n, 4 * n + 4)
                return v.tensor_tensor(Y[:, h, :], banks(6)[:, h, :], Y[:, h, :], ALU.add)

            norm(5, add_forward)


def _constants():
    f = np.float32
    half = D // 2
    scale_vec = (np.arange(0, D, 2, dtype=f) + f(0.4 * D)) / f(1.4 * D)
    pos = np.arange(L, dtype=f)
    scale = scale_vec[None, :] ** (pos[:, None] / f(512.0))
    inv_freq = f(1.0) / f(10000.0) ** (np.arange(half, dtype=f) / f(half))
    sinusoid = pos[:, None] * inv_freq[None, :]
    k = np.zeros((128, NALL), f)
    for col, fn, sc in ((K_COSQ, np.cos, scale), (K_SINQ, np.sin, scale),
                        (K_COSK, np.cos, f(1.0) / scale), (K_SINK, np.sin, f(1.0) / scale)):
        k[:, col:col + L] = np.repeat(fn(sinusoid) * sc, 2, axis=-1).T
    n = np.arange(L)
    diff = n[None, :] - n[:, None]
    decay = np.where(diff >= 0, f(0.96875) ** np.maximum(diff, 0).astype(f), f(0.0))
    for j in range(2):
        k[SLOT * j:SLOT * j + L, K_MASK + SLOT * j:K_MASK + SLOT * j + L] = decay
    k[np.arange(128), K_HEAD + np.arange(128) // DH] = f(1.0 / np.sqrt(DH))
    k[:, K_IOTA:K_IOTA + NE] = np.arange(NE)
    sel = k[0:C, K_SEL:NALL].reshape(C, H, DH + 1)
    r = np.arange(C) % GW
    for h in range(H):
        sel[r // DH == h % HG, h, r[r // DH == h % HG] % DH] = 1.0
    k[0:C, K_SEL:NALL] = sel.reshape(C, -1)
    return k


_INS = ["x", "ctx_512", "L0_attn_W_Q", "L0_attn_W_K", "L0_attn_W_V", "L0_xattn_Wq", "L0_xattn_bq", "L0_xattn_Wk",
        "L0_xattn_bk", "L0_xattn_Wv", "L0_xattn_bv", "L0_ffn_Wg", "L0_ffn_bg", "L0_ffn_W1", "L0_ffn_b1", "L0_ffn_W2",
        "L0_ffn_b2", "L1_attn_w_lhs", "L1_attn_w_rhs", "L1_xattn_Wq", "L1_xattn_bq", "L1_xattn_Wk", "L1_xattn_bk",
        "L1_xattn_Wv", "L1_xattn_bv", "L1_xattn_Wo", "L1_xattn_bo", "L1_ffn_W1", "L1_ffn_b1", "L1_ffn_W2", "L1_ffn_b2"]


def kernel(**inputs):
    import concourse.bacc as _bacc
    from concourse.bass_utils import run_bass_kernel_spmd as _run

    nc = _bacc.Bacc("TRN2", target_bir_lowering=False, num_devices=1)
    arrays, aps = {}, {}
    for name in _INS:
        a = np.ascontiguousarray(inputs[name])
        arrays[f"in_{name}"] = a
        aps[name] = nc.dram_tensor(f"in_{name}", a.shape, mybir.dt.from_np(a.dtype), kind="ExternalInput").ap()
    arrays["in_constants"] = _constants()
    consts = nc.dram_tensor("in_constants", (128, NALL), F32, kind="ExternalInput").ap()
    out = nc.dram_tensor("out_0", (B, L, D), F32, kind="ExternalOutput").ap()
    decoder(nc, aps, consts, out)
    r = _run(nc, [arrays], core_ids=[0])
    return r.results[0]["out_0"]
```
